# Optimizing a Trainium2 kernel written in Bass

```python
import numpy as np
import jax
import jax.numpy as jnp

def _softmax(x, axis=-1):
    return jax.nn.softmax(x, axis=axis)

def _gelu(x):
    return jax.nn.gelu(x, approximate=True)

def _silu(x):
    return jax.nn.silu(x)

def _sigmoid(x):
    return jax.nn.sigmoid(x)

def _layernorm(x, axis=-1, eps=1e-05):
    m = jnp.mean(x, axis=axis, keepdims=True)
    v = jnp.var(x, axis=axis, keepdims=True)
    return (x - m) / jnp.sqrt(v + eps)

def _scatter_add(tgt, idx, src, axis=0):
    return tgt.at[idx].add(src)

def _segment_sum(src, seg, n):
    return jax.ops.segment_sum(src, seg, n)
kernel_name = 'mk_metaformer_d1_conv_nchw384_r2_8828d5'

def setup_inputs(seed: int=0):
    np.random.seed(seed)
    _w = jnp.asarray

    def _rec_inputs():
        import jax
        import jax.numpy as jnp
        _gk = jax.random.key(seed)
        x = -0.0002221 + 1 * jax.random.normal(jax.random.fold_in(_gk, 1), (1, 192, 128, 128), jnp.float32)
        return x
    x = _rec_inputs()

    def _L0_conv_setup():
        import jax, jax.numpy as jnp
        import numpy as np
        from jax import lax
        EPS_LN = 1e-05
        EPS_NORM = 1e-12
        NUM_HEADS = 8
        key = jax.random.key(seed)
        ks = jax.random.split(key, 5)
        b, c, h, w = (1, 192, 128, 128)
        return {'x': jax.random.normal(ks[0], (b, c, h, w), dtype=jnp.float32), 'spatial_interaction': jax.random.uniform(ks[1], (b, 1, h, w), dtype=jnp.float32), 'ln_w': jnp.ones((c,), dtype=jnp.float32), 'ln_b': jnp.zeros((c,), dtype=jnp.float32), 'w_qkv': jax.random.normal(ks[2], (3 * c, c), dtype=jnp.float32) * (1.0 / np.sqrt(c)), 'w_dw': jax.random.normal(ks[3], (3 * c, 1, 3, 3), dtype=jnp.float32) * (1.0 / 3.0), 'w_proj': jax.random.normal(ks[4], (c, c), dtype=jnp.float32) * (1.0 / np.sqrt(c)), 'temperature': jnp.ones((NUM_HEADS, 1, 1), dtype=jnp.float32)}
    _L0_conv_all = _L0_conv_setup()
    _L0_conv_in = {k: v for k, v in _L0_conv_all.items() if k in ('spatial_interaction', 'ln_w', 'ln_b', 'w_qkv', 'w_dw', 'w_proj', 'temperature')}
    del _L0_conv_all

    def _L0_ffn_setup():
        import jax, jax.numpy as jnp
        import numpy as np
        NUM_EXPERTS = 4
        TOP_K = 2
        DIM = 192
        HID = 4 * DIM
        key = jax.random.key(seed)
        ks = jax.random.split(key, 5)
        B, S = (16, 1024)
        scale_in = 1.0 / np.sqrt(DIM)
        scale_hid = 1.0 / np.sqrt(HID)
        return {'x': jax.random.normal(ks[0], (B, S, DIM), dtype=jnp.float32), 'gate_w': jax.random.normal(ks[1], (DIM, NUM_EXPERTS), dtype=jnp.float32) * scale_in, 'gate_b': jnp.zeros((NUM_EXPERTS,), dtype=jnp.float32), 'w1': jax.random.normal(ks[2], (NUM_EXPERTS, DIM, HID), dtype=jnp.float32) * scale_in, 'b1': jnp.zeros((NUM_EXPERTS, HID), dtype=jnp.float32), 'w2': jax.random.normal(ks[3], (NUM_EXPERTS, HID, DIM), dtype=jnp.float32) * scale_hid, 'b2': jnp.zeros((NUM_EXPERTS, DIM), dtype=jnp.float32)}
    _L0_ffn_all = _L0_ffn_setup()
    _L0_ffn_in = {k: v for k, v in _L0_ffn_all.items() if k in ('gate_w', 'gate_b', 'w1', 'b1', 'w2', 'b2')}
    del _L0_ffn_all
    return {'x': x, 'L0_conv_spatial_interaction': _L0_conv_in['spatial_interaction'], 'L0_conv_ln_w': _L0_conv_in['ln_w'], 'L0_conv_ln_b': _L0_conv_in['ln_b'], 'L0_conv_w_qkv': _L0_conv_in['w_qkv'], 'L0_conv_w_dw': _L0_conv_in['w_dw'], 'L0_conv_w_proj': _L0_conv_in['w_proj'], 'L0_conv_temperature': _L0_conv_in['temperature'], 'L0_ffn_gate_w': _L0_ffn_in['gate_w'], 'L0_ffn_gate_b': _L0_ffn_in['gate_b'], 'L0_ffn_w1': _L0_ffn_in['w1'], 'L0_ffn_b1': _L0_ffn_in['b1'], 'L0_ffn_w2': _L0_ffn_in['w2'], 'L0_ffn_b2': _L0_ffn_in['b2']}

def reference(x, L0_conv_spatial_interaction, L0_conv_ln_w, L0_conv_ln_b, L0_conv_w_qkv, L0_conv_w_dw, L0_conv_w_proj, L0_conv_temperature, L0_ffn_gate_w, L0_ffn_gate_b, L0_ffn_w1, L0_ffn_b1, L0_ffn_w2, L0_ffn_b2):
    import jax
    import jax.numpy as jnp

    def _L0_conv_ref(x, spatial_interaction, ln_w, ln_b, w_qkv, w_dw, w_proj, temperature):
        import jax, jax.numpy as jnp
        import numpy as np
        from jax import lax
        EPS_LN = 1e-05
        EPS_NORM = 1e-12
        NUM_HEADS = 8
        b, c, h, w = x.shape
        heads = NUM_HEADS
        mu = jnp.mean(x, axis=1, keepdims=True)
        var = jnp.mean((x - mu) ** 2, axis=1, keepdims=True)
        xn = (x - mu) / jnp.sqrt(var + EPS_LN) * ln_w[None, :, None, None] + ln_b[None, :, None, None]
        qkv = jnp.einsum('bchw,oc->bohw', xn, w_qkv)
        qkv = lax.conv_general_dilated(qkv, w_dw, window_strides=(1, 1), padding='SAME', dimension_numbers=('NCHW', 'OIHW', 'NCHW'), feature_group_count=3 * c)
        q, k, v = jnp.split(qkv, 3, axis=1)
        q = q * spatial_interaction
        k = k * spatial_interaction
        v = v * spatial_interaction

        def split_heads(t):
            return t.reshape(b, heads, c // heads, h * w)
        q, k, v = (split_heads(q), split_heads(k), split_heads(v))
        q = q / jnp.maximum(jnp.linalg.norm(q, axis=-1, keepdims=True), EPS_NORM)
        k = k / jnp.maximum(jnp.linalg.norm(k, axis=-1, keepdims=True), EPS_NORM)
        attn = jnp.einsum('bhcn,bhdn->bhcd', q, k) * temperature[None]
        attn = jax.nn.softmax(attn, axis=-1)
        out = jnp.einsum('bhcd,bhdn->bhcn', attn, v)
        out = out.reshape(b, c, h, w)
        out = jnp.einsum('bchw,oc->bohw', out, w_proj)
        return out

    def _L0_ffn_ref(x, gate_w, gate_b, w1, b1, w2, b2):
        import jax, jax.numpy as jnp
        import numpy as np
        NUM_EXPERTS = 4
        TOP_K = 2
        DIM = 192
        HID = 4 * DIM
        scores = jnp.einsum('bsd,de->bse', x, gate_w) + gate_b
        probs = jax.nn.softmax(scores, axis=-1)
        topk_vals, topk_idx = jax.lax.top_k(probs, TOP_K)
        mask = jnp.sum(jax.nn.one_hot(topk_idx, NUM_EXPERTS, dtype=probs.dtype), axis=-2)
        masked = probs * mask
        masked = masked / (jnp.sum(masked, axis=-1, keepdims=True) + 1e-09)
        h = jax.nn.gelu(jnp.einsum('bsd,edh->ebsh', x, w1) + b1[:, None, None, :], approximate=False)
        y = jnp.einsum('ebsh,ehd->ebsd', h, w2) + b2[:, None, None, :]
        out = jnp.einsum('bse,ebsd->bsd', masked, y)
        return out

    def _gn(v, G=32, eps=1e-05):
        B_, C_, H_, W_ = v.shape
        g = v.reshape(B_, G, C_ // G, H_, W_)
        m = jnp.mean(g, axis=(2, 3, 4), keepdims=True)
        s = jnp.var(g, axis=(2, 3, 4), keepdims=True)
        return ((g - m) / jnp.sqrt(s + eps)).reshape(v.shape)

    def _ln_c(v, eps=1e-06):
        m = jnp.mean(v, axis=1, keepdims=True)
        s = jnp.var(v, axis=1, keepdims=True)
        return (v - m) / jnp.sqrt(s + eps)

    def _ln_t(v, eps=1e-05):
        m = jnp.mean(v, axis=-1, keepdims=True)
        s = jnp.var(v, axis=-1, keepdims=True)
        return (v - m) / jnp.sqrt(s + eps)

    def _to_tokens(v):
        B_, C_, H_, W_ = v.shape
        return v.reshape(B_, C_, H_ * W_).transpose(0, 2, 1)

    def _from_tokens(t, like):
        B_, C_, H_, W_ = like.shape
        return t.transpose(0, 2, 1).reshape(B_, C_, H_, W_)
    x = x + _L0_conv_ref(_ln_c(x), L0_conv_spatial_interaction, L0_conv_ln_w, L0_conv_ln_b, L0_conv_w_qkv, L0_conv_w_dw, L0_conv_w_proj, L0_conv_temperature)
    t = _to_tokens(x)
    t = t + _L0_ffn_ref(_ln_t(t), L0_ffn_gate_w, L0_ffn_gate_b, L0_ffn_w1, L0_ffn_b1, L0_ffn_w2, L0_ffn_b2)
    x = _from_tokens(t, x)
    return x

_drawn_inputs = setup_inputs


def setup_inputs(seed=0):
    import zlib

    import numpy as np

    out = dict(_drawn_inputs(seed))
    spreads = {'L0_conv_ln_w': (1.0, 0.2),
     'L0_conv_ln_b': (0.0, 0.296),
     'L0_conv_temperature': (1.0, 0.6),
     'L0_ffn_gate_b': (0.0, 0.1),
     'L0_ffn_b1': (0.0, 0.1),
     'L0_ffn_b2': (0.0, 0.1)}
    factors = {}
    for name, (base, spread) in spreads.items():
        noise = np.random.default_rng([zlib.crc32(name.encode()), seed]).standard_normal(out[name].shape)
        drawn = base * np.exp(spread * noise) if base else spread * noise
        out[name] = jnp.asarray(drawn.astype(out[name].dtype))
    for name, factor in factors.items():
        out[name] = (out[name] * factor).astype(out[name].dtype)
    return out
```

```python
import concourse.bass as bass
from concourse import mybir
from contextlib import ExitStack

FP32 = mybir.dt.float32
F32R = mybir.dt.float32r
ALU = mybir.AluOpType
ACT = mybir.ActivationFunctionType
AX = mybir.AxisListType.X

C = 192
H = W = 128
ROWS = 4
TOK = ROWS * W
NB = H // ROWS
CA = 128
CB = C - CA
G2 = C // 2
HEADS = 8
HD = C // HEADS
E = 4
HID = 4 * C
CH = HID // 128
NCH = E * CH
LAG = 2
ZT = [(0, 128), (128, 128), (256, 128), (384, G2), (480, G2)]
QK = 3
KX = 3
PE_TAPS = [0, 1, 2]
DVE_TAPS = [3, 4, 5, 6, 7, 8]
EPS_C, EPS_LN, EPS_NORM, EPS_GATE = 1e-6, 1e-5, 1e-12, 1e-9
NEG = -1e30
E_BASE = 2.718281828459045


class Step:

    def __init__(self, j, c):
        self.j, self.c = j, c

    def __add__(self, n):
        return Step(self.j, self.c + n)

    def __sub__(self, n):
        return Step(self.j, self.c - n)

    @property
    def static(self):
        return isinstance(self.j, int)

    @property
    def val(self):
        return 2 * self.j + self.c

    @property
    def half(self):
        return self.j + self.c // 2

    @property
    def par(self):
        return self.c % 2

    def within(self, lo, hi):
        return not self.static or lo <= self.val <= hi


def wait(eng, sem, value):
    if isinstance(value, int) and value <= 0:
        return
    eng.wait_ge(sem, value)


def steps(eng, emit, first, last, lo, hi):
    assert (hi - lo) % 2 == 1
    for n in range(first, lo):
        emit(Step(0, n))
    with eng.Fori(0, (hi - lo + 1) // 2) as j:
        for u in (0, 1):
            emit(Step(j, lo + u))
    for n in range(hi + 1, last + 1):
        emit(Step(0, n))


def build(nc, x, spat, ln_w, ln_b, w_qkv, w_dw, w_proj, temperature, gate_w, gate_b, w1, b1, w2, b2, out):
    top = ExitStack()
    with top:
        def sb(stack, name, shape, dt=FP32):
            return stack.enter_context(nc.sbuf_tensor(name, shape, dt))

        def sem(name):
            return top.enter_context(nc.semaphore(name))

        xtok_dram = nc.dram_tensor("xtok_scratch", (H, W, C), FP32, kind="Internal").ap()
        v_dram = nc.dram_tensor("v_scratch", (C, H + 2, W), FP32, kind="Internal").ap()
        v_view = v_dram.rearrange("(g p) r w -> p g r w", g=2)
        x_view = x.rearrange("a c h w -> (a c) (h w)")
        out_view = out.rearrange("a c h w -> (a c) (h w)")
        s_view = spat.rearrange("a b h w -> (a b h) w")

        ident = sb(top, "ident", [128, 128])
        w1_ah = sb(top, "w1_ah", [CA, NCH * 128], F32R)
        w1_al = sb(top, "w1_al", [CA, NCH * 128], F32R)
        w1_ch = sb(top, "w1_ch", [128, NCH * 128], F32R)
        w1_cl = sb(top, "w1_cl", [128, NCH * 128], F32R)
        w2_hl = sb(top, "w2_hl", [128, NCH, 2 * C], F32R)
        b1_col = sb(top, "b1_col", [128, NCH])
        b2_row = sb(top, "b2_row", [E, C])
        gate_raw = sb(top, "gate_raw", [128, 2, E])
        gate_r = sb(top, "gate_r", [128, 4, E], F32R)
        gate_bb = sb(top, "gate_bb", [128, E])
        wdw_v = sb(top, "wdw_v", [G2, 2, 9])
        s_tok = sb(top, "s_tok", [128, H])
        mt = sb(top, "mt", [G2, 2, C])
        xh_a = sb(top, "xh_a", [CA, 2, TOK], F32R)
        xl_a = sb(top, "xl_a", [CA, 2, TOK], F32R)
        x_c = sb(top, "x_c", [128, 2, TOK], F32R)
        tn = sb(top, "tn", [128, ROWS, 2 * 128])
        xtok = sb(top, "xtok", [128, 2, ROWS, C])
        stat = sb(top, "stat", [128, 2, ROWS, 6])
        mv = sb(top, "mv", [128, 2, ROWS, 2])
        rstd = sb(top, "rstd", [128, 2, ROWS])
        pw = sb(top, "pw", [128, 3, ROWS])
        pause = sb(top, "pause", [128, 2])
        small = sb(top, "small", [128, 6, ROWS])

        banks = [top.enter_context(nc.psum_tensor(f"bank{n}", [128, 512], FP32)) for n in range(8)]

        p1 = ExitStack()
        with p1:
            stage = sb(p1, "stage", [128, NCH * 128])
            wn = stage[:, 0:5 * C].rearrange("p (t c) -> p t c", t=5)
            wp = stage[:, 5 * C:5 * C + 5 * 256].rearrange("p (t c) -> p t c", t=5)
            wtmp = stage[:, 5 * (C + 256):5 * (C + 256) + C]
            lnw_bb = sb(p1, "lnw_bb", [128, C])
            lnb_bb = sb(p1, "lnb_bb", [128, C])
            bz = sb(p1, "bz", [128, 5])
            wq_ah = sb(p1, "wq_ah", [CA, 3 * C], F32R)
            wq_al = sb(p1, "wq_al", [CA, 3 * C], F32R)
            wq_ch = sb(p1, "wq_ch", [128, 3 * C], F32R)
            wq_cl = sb(p1, "wq_cl", [128, 3 * C], F32R)
            wdw = sb(p1, "wdw", [128, QK, 9])
            diag = sb(p1, "diag", [128, QK, len(PE_TAPS), 128])
            wpr = sb(p1, "wpr", [128, 2, C])
            wpt = sb(p1, "wpt", [G2, 2, C])
            s_rows = sb(p1, "s_rows", [128, W])
            zero = sb(p1, "zero", [G2, 2, 2, W])
            xc_a = sb(p1, "xc_a", [CA, 2, TOK])
            xc_b = sb(p1, "xc_b", [CB, 2, TOK])
            zwin = [sb(p1, f"zwin{p}", [128, QK, 6, W + 2]) for p in (0, 1)]
            zv = sb(p1, "zv", [G2, 2, TOK])
            s_bc = sb(p1, "s_bc", [128, 2, ROWS, W])
            acc = sb(p1, "acc", [128, QK, ROWS, W])
            qs = sb(p1, "qs", [128, 2, QK, ROWS, W])
            junk = xl_a[:, 1, :]
            qk_tok = sb(p1, "qk_tok", [128, 2, 2 * C])
            nrm = sb(p1, "nrm", [128, QK, NB + 1])
            n2 = sb(p1, "n2", [128, 4, QK])
            rn_row = sb(p1, "rn_row", [QK, 128])
            sel = sb(p1, "sel", [QK, QK, G2])
            rb = sb(p1, "rb", [G2, 2 * C])
            temp = sb(p1, "temp", [G2, 2])
            mask = sb(p1, "mask", [G2, 2, E, HD])
            attn = sb(p1, "attn", [G2, 4, 2, G2])
            acol = sb(p1, "acol", [G2, 6, 2])

            tp = banks[0:2]
            zb = banks[2:4]
            db = banks[4:6]
            qb = banks[6]
            gb = banks[7]

            ld_w = sem("ld_w")
            ld_zero = sem("ld_zero")
            ld_x = [sem("ld_x0"), sem("ld_x1")]
            ld_s = [sem("ld_s0"), sem("ld_s1")]
            st_xt = [sem("st_xt0"), sem("st_xt1")]
            st_v = sem("st_v")
            ld_e = sem("ld_e")
            e_hi, e_lo = sem("e_hi"), sem("e_lo")
            const = sem("const")
            su_v, su_t, su_a = sem("su_v"), sem("su_t"), sem("su_a")
            xt_t, xt_a = sem("xt_t"), sem("xt_a")
            stats = sem("stats")
            r_link, r_ok = sem("r_link"), sem("r_ok")
            tn_ok = sem("tn_ok")
            ac_t = sem("ac_t")
            hi_ok, lo_ok = sem("hi_ok"), sem("lo_ok")
            z_t, z_a = sem("z_t"), sem("z_a")
            carry = sem("carry")
            dw_t, dw_l = sem("dw_t"), sem("dw_l")
            qs_ok, sq_ok = sem("qs_ok"), sem("sq_ok")
            q_t, q_a, gr_t = sem("q_t"), sem("q_a"), sem("gr_t")
            row_z = sem("row_z")
            at_v, at_t, at_a, at_p = sem("at_v"), sem("at_t"), sem("at_a"), sem("at_p")

            FIRST, LAST, LO, HI = -2, NB + 2, 3, NB - 6

            def slots(n):
                if n.static and n.val == 0:
                    return 1, ROWS
                if n.static and n.val == NB:
                    return 0, 1
                return 0, ROWS

            n_dve = len(DVE_TAPS)
            blk = p1.enter_context(nc.Block())
            N_LD_W = 26

            @blk.sync
            def _(sp):
                def load_x(b):
                    if b.within(0, NB - 1):
                        wait(sp, xt_t, b.val - 1)
                        cols = bass.ds(b.val * TOK, TOK)
                        sp.dma_start(xc_a[:, b.par, :], x_view[0:CA, cols]).then_inc(ld_x[b.par], 16)
                        sp.dma_start(xc_b[:, b.par, :], x_view[CA:C, cols]).then_inc(ld_x[b.par], 16)

                n_w = [0]

                def load_w(dst, src):
                    n_w[0] += 1
                    sp.dma_start(dst, src).then_inc(ld_w, 16)

                load_x(Step(0, 0))
                for ct, (o, m) in enumerate(ZT):
                    load_w(wn[0:m, ct, :], w_qkv[o:o + m, :])
                load_w(lnw_bb[:, :], ln_w.rearrange("(a c) -> a c", a=1).to_broadcast([128, C]))
                load_w(lnb_bb[:, :], ln_b.rearrange("(a c) -> a c", a=1).to_broadcast([128, C]))
                dw_rows = w_dw.rearrange("o a y x -> o (a y x)")
                load_w(wdw[:, :, :], dw_rows[0:QK * 128, :].rearrange("(t p) k -> p t k", p=128))
                load_w(wdw_v[:, :, :], dw_rows[2 * C:3 * C, :].rearrange("(t p) k -> p t k", p=G2))
                load_w(s_rows[:, :], s_view)
                load_w(wpr[:, 0, :], w_proj[0:CA, :])
                load_w(wpr[0:CB, 1, :], w_proj[CA:C, :])
                load_w(gate_raw[:, 0, :], gate_w[0:CA, :])
                load_w(gate_raw[0:CB, 1, :], gate_w[CA:C, :])
                load_w(gate_raw[CB:128, 1, :], gate_w[CA:C, :])
                load_w(gate_bb[:, :], gate_b.rearrange("(a c) -> a c", a=1).to_broadcast([128, E]))
                for h in range(HEADS):
                    load_w(temp[HD * (h % 4):HD * (h % 4) + HD, h // 4:h // 4 + 1],
                           temperature[h:h + 1, :, 0].to_broadcast([HD, 1]))
                load_w(b2_row[:, :], b2)
                with nc.allow_non_contiguous_dma(reason="24 columns of biases, once"):
                    load_w(b1_col[:, :], b1.rearrange("e (m p) -> p (e m)", p=128))
                assert n_w[0] == N_LD_W, n_w
                load_x(Step(0, 1))
                sp.wait_ge(const, 7)
                sp.dma_start(v_view[:, :, 0, :], zero[:, 0, :, :]).then_inc(ld_zero, 16)
                sp.dma_start(v_view[:, :, H + 1, :], zero[:, 1, :, :]).then_inc(ld_zero, 16)
                w1_rows = w1.rearrange("e c h -> c e h")
                w2_rows = w2.rearrange("e (m p) d -> p (e m) d", p=128)

                def stage_piece(n):
                    wait(sp, e_lo, n)
                    if n == 0:
                        dst = stage[:, :].rearrange("p (e h) -> p e h", e=E)
                        sp.dma_start(dst, w1_rows[0:CA]).then_inc(ld_e, 32)
                    elif n == 1:
                        for o in (0, CB):
                            dst = stage[o:o + CB, :].rearrange("p (e h) -> p e h", e=E)
                            sp.dma_start(dst, w1_rows[CA:C]).then_inc(ld_e, 16)
                    else:
                        k = NCH // 2
                        dst = stage[:, 0:k * C].rearrange("p (m d) -> p m d", d=C)
                        sp.dma_start(dst, w2_rows[:, (n - 2) * k:(n - 1) * k, :]).then_inc(ld_e, 32)

                def step(i):
                    load_x(i + 4)
                    b = i + 2
                    if b.within(0, NB - 1):
                        sp.wait_ge(xt_a, 2 * b.val + 2)
                        sp.dma_start(xtok_dram[bass.ds(b.val * ROWS, ROWS), :, :].rearrange("r p c -> p r c"),
                                     xtok[:, b.par, :, :]).then_inc(st_xt[b.par], 16)
                    n = i + 1
                    if n.within(0, NB):
                        wait(sp, qs_ok, QK * (n.val - 1))
                        lo, hi = slots(n)
                        rows = s_view[bass.ds(n.val * ROWS - 1 + lo, hi - lo), :].rearrange("r w -> (r w)")
                        sp.dma_start(s_bc[:, n.par, lo:hi, :].rearrange("p r w -> p (r w)"),
                                     rows.rearrange("(a n) -> a n", a=1).to_broadcast([128, (hi - lo) * W]))\
                          .then_inc(ld_s[n.par], 16)
                    if i.within(0, NB - 1):
                        sp.wait_ge(z_a, 5 * i.val + 5)
                        sp.dma_start(v_view[:, :, bass.ds(i.val * ROWS + 1, ROWS), :].rearrange("p g r w -> p g (r w)"),
                                     zv[:, :, :]).then_inc(st_v, 16)
                    if i.static and i.val == 0:
                        stage_piece(0)

                steps(sp, step, FIRST, LAST, LO, HI)
                for n in range(1, 4):
                    stage_piece(n)
                sp.wait_ge(ld_zero, 32)
                for p in (0, 1):
                    sp.wait_ge(st_xt[p], 16 * NB // 2)
                sp.wait_ge(st_v, 16 * NB)

            @blk.gpsimd
            def _(pool):
                nc.gpsimd.memset(ident[:, :], 0.0).then_inc(const, 1)
                nc.gpsimd.memset(zero[:, :, :, :], 0.0).then_inc(const, 1)
                nc.gpsimd.memset(zwin[0][:, :, :, :], 0.0).then_inc(const, 1)
                nc.gpsimd.memset(zwin[1][:, :, :, :], 0.0).then_inc(const, 1)
                nc.gpsimd.memset(pw[:, 0, :], -0.5).then_inc(const, 1)
                nc.gpsimd.memset(pw[:, 1, :], EPS_C).then_inc(const, 1)
                nc.gpsimd.memset(pw[:, 2, :], EPS_LN).then_inc(const, 1)
                pool.wait_ge(const, 7)
                nc.gpsimd.affine_select(out=ident[:, :], in_=ident[:, :], compare_op=ALU.not_equal, fill=1.0,
                                        base=0, pattern=[[-1, 128]], channel_multiplier=1).then_inc(const, 1)
                nc.gpsimd.memset(sel[:, :, :], 0.0).then_inc(const, 1)
                nc.gpsimd.memset(mask[:, :, :, :], 0.0).then_inc(const, 1)
                pool.wait_ge(const, 10)
                nc.gpsimd.affine_select(out=sel[:, :, :], in_=sel[:, :, :], compare_op=ALU.not_equal, fill=1.0,
                                        base=0, pattern=[[-1, QK], [0, G2]], channel_multiplier=1).then_inc(const, 1)
                nc.gpsimd.affine_select(out=mask[:, :, :, :], in_=mask[:, :, :, :], compare_op=ALU.is_ge, fill=NEG,
                                        base=0, pattern=[[0, 2], [-HD, E], [0, HD]], channel_multiplier=1).then_inc(const, 1)
                pool.wait_ge(const, 12)
                nc.gpsimd.affine_select(out=mask[:, :, :, :], in_=mask[:, :, :, :], compare_op=ALU.is_ge, fill=NEG,
                                        base=HD - 1, pattern=[[0, 2], [HD, E], [0, HD]], channel_multiplier=-1).then_inc(const, 1)

                links = 5

                def step(i):
                    n = i - 1
                    if n.within(0, NB):
                        lo, hi = slots(n)
                        wait(pool, ld_s[n.par], 16 * n.half + 16)
                        wait(pool, q_t, ROWS * (n.val - 1) - 1)
                        wait(pool, sq_ok, QK * (n.val - 1))
                        for ct in range(QK):
                            pool.wait_ge(dw_l, n_dve * (QK * n.val + ct + 1))
                            nc.gpsimd.tensor_tensor(qs[:, n.par, ct, lo:hi, :], acc[:, ct, lo:hi, :],
                                                    s_bc[:, n.par, lo:hi, :], ALU.mult).then_inc(qs_ok, 1)
                    b = i + 2
                    if b.within(0, NB - 1):
                        var = mv[:, b.par, :, 1]
                        t = [small[:, k, :] for k in range(4)]
                        pool.wait_ge(stats, b.val + 1)
                        base = links * b.val

                        def link(k, ins):
                            ins.then_inc(r_link, 1)
                            pool.wait_ge(r_link, base + k)

                        link(1, nc.gpsimd.tensor_tensor(t[0], var, pw[:, 1, :], ALU.add))
                        link(2, nc.gpsimd.tensor_tensor(t[1], t[0], pw[:, 0, :], ALU.pow))
                        link(3, nc.gpsimd.tensor_tensor(t[2], t[1], t[1], ALU.mult))
                        link(4, nc.gpsimd.tensor_tensor(t[3], t[2], var, ALU.mult))
                        link(5, nc.gpsimd.tensor_tensor(t[0], t[3], pw[:, 2, :], ALU.add))
                        nc.gpsimd.tensor_tensor(t[2], t[0], pw[:, 0, :], ALU.pow).then_inc(r_ok, 1)
                        pool.wait_ge(r_ok, 2 * b.val + 1)
                        if not (b.static and b.val < 2):
                            pool.wait_ge(tn_ok, b.val - 1)
                        nc.gpsimd.tensor_tensor(rstd[:, b.par, :], t[2], t[1], ALU.mult).then_inc(r_ok, 1)
                        pool.wait_ge(r_ok, 2 * b.val + 2)
                    if i.static and i.val == NB:
                        pool.wait_ge(dw_l, n_dve * QK * (NB - 1))
                        pool.wait_ge(dw_t, QK * (NB - 1))
                        nc.gpsimd.memset(zwin[NB % 2][:, :, 2, 1:W + 1], 0.0).then_inc(row_z, 1)

                steps(pool, step, FIRST, LAST, LO, HI)
                pool.wait_ge(at_v, 1)
                nc.gpsimd.tensor_scalar(n2[:, 1, :], pw[:, 0, 0:QK], -1.0, 0.0, ALU.mult, ALU.add).then_inc(at_p, 1)
                pool.wait_ge(at_p, 1)
                nc.gpsimd.tensor_tensor(n2[:, 2, :], n2[:, 0, :], n2[:, 1, :], ALU.pow).then_inc(at_p, 1)

            @blk.scalar
            def _(act):
                act.wait_ge(ld_w, 16 * N_LD_W)
                nc.scalar.activation(gate_r[:, 0, :], gate_raw[:, 0, :], ACT.Copy).then_inc(su_a, 1)
                nc.scalar.activation(gate_r[:, 2, :], gate_raw[:, 1, :], ACT.Copy).then_inc(su_a, 1)
                for ct, (o, m) in enumerate(ZT):
                    act.wait_ge(su_t, 2 * ct + 2)
                    nc.scalar.activation(wq_ah[:, o:o + m], zb[ct % 2][:, 0:m], ACT.Copy).then_inc(su_a, 1)
                    nc.scalar.activation(wq_ch[:, o:o + m], zb[ct % 2][:, 128:128 + m], ACT.Copy).then_inc(su_a, 1)
                act.wait_ge(su_t, 11)
                nc.scalar.activation(s_tok[:, :], db[0][:, 0:128], ACT.Copy).then_inc(su_a, 1)
                act.wait_ge(su_t, 12)
                nc.scalar.activation(wpt[:, :, :], db[1][0:G2, 0:2 * C].rearrange("p (g o) -> p g o", g=2), ACT.Copy)\
                    .then_inc(su_a, 1)
                act.wait_ge(const, 7)

                def copy_q(n, t):
                    lo, hi = slots(n)
                    if lo <= t < hi:
                        c = ROWS * n.val - 1 + t
                        act.wait_ge(q_t, c + 1)
                        wait(act, gr_t, c - 1)
                        nc.scalar.activation(qk_tok[:, t % 2, :], qb[:, 0:2 * C], ACT.Copy).then_inc(q_a, 1)

                def copy_z(i, ct):
                    c = 5 * i.val + ct
                    m = ZT[ct][1]
                    act.wait_ge(z_t, c + 1)
                    if ct < QK:
                        wait(act, dw_l, n_dve * (QK * (i.val - 2) + ct + 1))
                        wait(act, dw_t, QK * (i.val - 2) + ct + 1)
                        nc.scalar.activation(zwin[i.par][:, ct, 2:6, 1:W + 1],
                                             zb[(i.par + ct) % 2][:, :].rearrange("p (r w) -> p r w", w=W),
                                             ACT.Identity, bias=bz[:, ct:ct + 1]).then_inc(z_a, 1)
                    else:
                        if ct == QK:
                            wait(act, st_v, 16 * i.val)
                        nc.scalar.activation(zv[:, ct - QK, :], zb[(i.par + ct) % 2][0:m, :], ACT.Identity,
                                             bias=bz[0:m, ct:ct + 1]).then_inc(z_a, 1)

                def step(i):
                    if i.within(0, NB - 1):
                        act.wait_ge(ac_t, 2 * i.val + 1)
                        wait(act, z_t, 5 * i.val)
                        nc.scalar.activation(xh_a[:, 0, :], tp[0][:, :], ACT.Copy).then_inc(hi_ok, 1)
                        act.wait_ge(ac_t, 2 * i.val + 2)
                        nc.scalar.activation(x_c[:, 0, :], tp[1][:, :], ACT.Copy).then_inc(hi_ok, 1)
                    if i.within(1, NB):
                        act.wait_ge(z_a, 5 * i.val)
                        wait(act, dw_l, n_dve * QK * (i.val - 1))
                        wait(act, dw_t, QK * (i.val - 1))
                        nc.scalar.activation(zwin[i.par][:, :, 0:2, 1:W + 1], zwin[1 - i.par][:, :, 4:6, 1:W + 1],
                                             ACT.Copy).then_inc(carry, 1)
                    n = i - 2
                    if n.within(0, NB):
                        lo, hi = slots(n)
                        for ct in range(QK):
                            act.wait_ge(qs_ok, QK * n.val + ct + 1)
                            wait(act, sq_ok, QK * n.val + ct)
                            nc.scalar.activation(junk[:, lo * W:hi * W], qs[:, n.par, ct, lo:hi, :].rearrange("p r w -> p (r w)"),
                                                 ACT.Square, accum_out=nrm[:, ct, bass.ds(n.val, 1)]).then_inc(sq_ok, 1)
                        copy_q(n, 0)
                        copy_q(n, 1)
                    b = i + 2
                    if b.within(0, NB - 1):
                        for k in (0, 1):
                            act.wait_ge(xt_t, b.val + 1)
                            if k == 0:
                                wait(act, st_xt[b.par], 16 * b.half)
                                wait(act, tn_ok, b.val - 1)
                            nc.scalar.activation(xtok[:, b.par, 2 * k:2 * k + 2, :],
                                                 tp[k][:, 0:2 * C].rearrange("p (r c) -> p r c", c=C),
                                                 ACT.Copy).then_inc(xt_a, 1)
                    if n.within(0, NB):
                        copy_q(n, 2)
                        copy_q(n, 3)
                    if i.within(0, NB - 1):
                        for ct in range(5):
                            copy_z(i, ct)

                steps(act, step, FIRST, LAST, LO, HI)
                k = NCH // 2
                for n in range(4):
                    act.wait_ge(ld_e, 32 * n + 32)
                    if n < 2:
                        src, dst = stage[:, :], (w1_ah, w1_ch)[n][:, :]
                    else:
                        src = stage[:, 0:k * C].rearrange("p (m d) -> p m d", d=C)
                        dst = w2_hl[:, (n - 2) * k:(n - 1) * k, 0:C]
                    nc.scalar.activation(dst, src, ACT.Copy).then_inc(e_hi, 1)
                act.wait_ge(at_t, 1)
                nc.scalar.activation(rn_row[:, :], db[0][0:QK, 0:128], ACT.Copy).then_inc(at_a, 1)
                act.wait_ge(at_t, 2)
                nc.scalar.activation(rb[:, :], db[1][0:G2, 0:2 * C], ACT.Copy).then_inc(at_a, 1)
                act.wait_ge(at_v, 12)
                for g in (0, 1):
                    nc.scalar.activation(attn[:, 2, g, :], attn[:, 1, g, :], ACT.Exp, bias=acol[:, 2, g:g + 1],
                                         accum_out=acol[:, 3, g:g + 1]).then_inc(at_a, 1)
                act.wait_ge(at_t, 3)
                nc.scalar.activation(mt[:, :, :], db[0][0:G2, 0:2 * C].rearrange("p (g o) -> p g o", g=2), ACT.Copy)\
                    .then_inc(at_a, 1)

            @blk.vector
            def _(dve):
                dve.wait_ge(ld_w, 16 * N_LD_W)
                n_v = [0]

                def link(ins):
                    n_v[0] += 1
                    ins.then_inc(su_v, 1)
                    dve.wait_ge(su_v, n_v[0])

                for ct, (o, m) in enumerate(ZT):
                    nc.vector.tensor_tensor(wp[0:m, ct, 0:C], wn[0:m, ct, :], lnw_bb[0:m, :], ALU.mult)
                    nc.vector.tensor_tensor(wp[0:m, ct, C:256], wn[0:m, ct, CA:C], lnw_bb[0:m, CA:C], ALU.mult)
                    link(nc.vector.tensor_tensor(wtmp[0:m, :], wn[0:m, ct, :], lnb_bb[0:m, :], ALU.mult))
                    link(nc.vector.reduce_sum(bz[0:m, ct:ct + 1], wtmp[0:m, :], AX))
                dve.wait_ge(su_a, 2)
                link(nc.vector.tensor_tensor(gate_r[:, 1, :], gate_raw[:, 0, :], gate_r[:, 0, :].bitcast(FP32), ALU.subtract))
                link(nc.vector.tensor_tensor(gate_r[:, 3, :], gate_raw[:, 1, :], gate_r[:, 2, :].bitcast(FP32), ALU.subtract))
                dve.wait_ge(const, 8)
                for ct in range(QK):
                    for k, tap in enumerate(PE_TAPS):
                        link(nc.vector.tensor_scalar(diag[:, ct, k, :], ident[:, :], wdw[:, ct, tap:tap + 1], None, ALU.mult))
                for ct, (o, m) in enumerate(ZT):
                    dve.wait_ge(su_a, 2 * ct + 4)
                    link(nc.vector.tensor_tensor(wq_al[:, o:o + m], zb[ct % 2][:, 0:m], wq_ah[:, o:o + m].bitcast(FP32), ALU.subtract))
                    link(nc.vector.tensor_tensor(wq_cl[:, o:o + m], zb[ct % 2][:, 128:128 + m], wq_ch[:, o:o + m].bitcast(FP32), ALU.subtract))

                def chain(n, ct):
                    lo, hi = slots(n)
                    if ct == 0:
                        if n.within(0, NB - 1):
                            dve.wait_ge(z_a, 5 * n.val + QK)
                        wait(dve, carry, n.val)
                        if n.static and n.val == NB:
                            dve.wait_ge(row_z, 1)
                    wait(dve, qs_ok, QK * (n.val - 1) + ct + 1)
                    dve.wait_ge(dw_t, QK * n.val + ct + 1)
                    a = acc[:, ct, lo:hi, :]
                    for k, tap in enumerate(DVE_TAPS):
                        ky, kx = divmod(tap, KX)
                        before = db[(n.par + ct) % 2][:, lo * W:hi * W].rearrange("p (r w) -> p r w", w=W) if k == 0 else a
                        if k:
                            dve.wait_ge(dw_l, n_dve * (QK * n.val + ct) + k)
                        ins = nc.vector.scalar_tensor_tensor(
                            out=a, in0=zwin[n.par][:, ct, ky + lo:ky + hi, kx:kx + W], scalar=wdw[:, ct, tap:tap + 1],
                            in1=before, op0=ALU.mult, op1=ALU.add)
                        ins.then_inc(dw_l, 1)

                def step(i):
                    if i.within(0, NB - 1):
                        dve.wait_ge(hi_ok, 2 * i.val + 1)
                        nc.vector.tensor_tensor(xl_a[:, 0, :], tp[0][:, :], xh_a[:, 0, :].bitcast(FP32), ALU.subtract).then_inc(lo_ok, 1)
                        dve.wait_ge(hi_ok, 2 * i.val + 2)
                        nc.vector.tensor_tensor(x_c[CB:128, 0, :], tp[1][CB:128, :], x_c[CB:128, 0, :].bitcast(FP32), ALU.subtract)\
                            .then_inc(lo_ok, 1)
                    n = i - 1
                    if n.within(0, NB):
                        chain(n, 0)
                        chain(n, 1)
                    b = i + 1
                    if b.within(0, NB - 1):
                        wait(dve, ac_t, 2 * b.val)
                        dve.wait_ge(r_ok, 2 * b.val + 2)
                        for t in range(ROWS):
                            nc.vector.tensor_scalar(tn[:, t, 0:C], xtok[:, b.par, t, :], mv[:, b.par, t, 0:1],
                                                    rstd[:, b.par, t:t + 1], ALU.subtract, ALU.mult)
                            last = nc.vector.tensor_scalar(tn[:, t, C:256], xtok[:, b.par, t, CA:C], mv[:, b.par, t, 0:1],
                                                           rstd[:, b.par, t:t + 1], ALU.subtract, ALU.mult)
                        last.then_inc(tn_ok, 1)
                    if n.within(0, NB):
                        chain(n, 2)
                    b = i + 2
                    if b.within(0, NB - 1):
                        dve.wait_ge(xt_a, 2 * b.val + 2)
                        wait(dve, r_ok, 2 * b.val - 2)
                        for t in range(ROWS):
                            last = nc.vector.bn_stats(stat[:, b.par, t, :], xtok[:, b.par, t, :])
                        last.then_inc(su_v, 1)
                        dve.wait_ge(su_v, n_v[0] + b.val + 1)
                        nc.vector.memset(pause[:, 0:1], 0.0)
                        for t in range(ROWS):
                            last = nc.vector.bn_aggr(mv[:, b.par, t, :], stat[:, b.par, t, :])
                        last.then_inc(stats, 1)

                steps(dve, step, FIRST, LAST, LO, HI)
                k = NCH // 2
                for n in range(4):
                    dve.wait_ge(e_hi, n + 1)
                    if n < 2:
                        src, hi, dst = stage[:, :], (w1_ah, w1_ch)[n][:, :], (w1_al, w1_cl)[n][:, :]
                    else:
                        src = stage[:, 0:k * C].rearrange("p (m d) -> p m d", d=C)
                        hi, dst = (w2_hl[:, (n - 2) * k:(n - 1) * k, o:o + C] for o in (0, C))
                    nc.vector.tensor_tensor(dst, src, hi.bitcast(FP32), ALU.subtract).then_inc(e_lo, 1)
                dve.wait_ge(sq_ok, QK * (NB + 1))
                nc.vector.reduce_sum(n2[:, 0, :], nrm[:, :, :], AX).then_inc(at_v, 1)
                dve.wait_ge(at_p, 2)
                nc.vector.tensor_scalar(n2[:, 3, :], n2[:, 2, :], EPS_NORM, None, ALU.max).then_inc(at_v, 1)
                dve.wait_ge(at_v, 2)
                nc.vector.reciprocal(n2[:, 1, :], n2[:, 3, :]).then_inc(at_v, 1)
                dve.wait_ge(at_a, 2)
                for g in (0, 1):
                    nc.vector.tensor_tensor(attn[:, 0, g, :], rb[:, G2 * g:G2 * g + G2], ident[0:G2, 0:G2], ALU.mult).then_inc(at_v, 1)
                dve.wait_ge(at_v, 5)
                nc.vector.reduce_sum(acol[:, 0, :], attn[:, 0, :, :], AX).then_inc(at_v, 1)
                dve.wait_ge(at_v, 6)
                nc.vector.tensor_tensor(acol[:, 1, :], acol[:, 0, :], temp[:, :], ALU.mult).then_inc(at_v, 1)
                dve.wait_ge(at_v, 7)
                dve.wait_ge(gr_t, H)
                dve.wait_ge(const, 13)
                for g in (0, 1):
                    nc.vector.scalar_tensor_tensor(out=attn[:, 0, g, :], in0=gb[0:G2, G2 * g:G2 * g + G2], scalar=acol[:, 1, g:g + 1],
                                                   in1=rb[:, C + G2 * g:C + G2 * g + G2], op0=ALU.mult, op1=ALU.mult).then_inc(at_v, 1)
                dve.wait_ge(at_v, 9)
                nc.vector.tensor_tensor(attn[:, 1, :, :].rearrange("p g c -> p (g c)"), attn[:, 0, :, :].rearrange("p g c -> p (g c)"),
                                        mask[:, :, :, :].rearrange("p g h c -> p (g h c)"), ALU.add).then_inc(at_v, 1)
                dve.wait_ge(at_v, 10)
                nc.vector.tensor_reduce(out=acol[:, 4, :], in_=attn[:, 1, :, :], axis=AX, op=ALU.max).then_inc(at_v, 1)
                dve.wait_ge(at_v, 11)
                nc.vector.tensor_scalar(acol[:, 2, :], acol[:, 4, :], -1.0, None, ALU.mult).then_inc(at_v, 1)
                dve.wait_ge(at_a, 4)
                nc.vector.reciprocal(acol[:, 5, :], acol[:, 3, :]).then_inc(at_v, 1)
                dve.wait_ge(at_v, 13)
                for g in (0, 1):
                    nc.vector.tensor_scalar(attn[:, 3, g, :], attn[:, 2, g, :], acol[:, 5, g:g + 1], None, ALU.mult).then_inc(at_v, 1)

            @blk.tensor
            def _(pe):
                pe.wait_ge(const, 8)
                for ct, (o, m) in enumerate(ZT):
                    pe.wait_ge(su_v, 2 * ct + 2)
                    if ct >= 2:
                        pe.wait_ge(su_v, 10 + 2 + QK * len(PE_TAPS) + 2 * (ct - 1))
                    nc.tensor.transpose(zb[ct % 2][:, 0:m], wp[0:m, ct, 0:CA], ident[0:m, 0:m]).then_inc(su_t, 1)
                    nc.tensor.transpose(zb[ct % 2][:, 128:128 + m], wp[0:m, ct, CA:256], ident[0:m, 0:m]).then_inc(su_t, 1)
                nc.tensor.transpose(db[0][:, 0:128], s_rows[:, :], ident[:, :]).then_inc(su_t, 1)
                for g in (0, 1):
                    nc.tensor.transpose(db[1][0:G2, g * C:g * C + CA], wpr[:, 0, G2 * g:G2 * g + G2], ident[:, :])
                    last = nc.tensor.transpose(db[1][0:G2, g * C + CA:g * C + C], wpr[0:CB, 1, G2 * g:G2 * g + G2], ident[0:CB, 0:CB])
                last.then_inc(su_t, 1)
                n_su_v = 10 + 2 + QK * len(PE_TAPS) + 10
                pe.wait_ge(su_v, n_su_v)
                pe.wait_ge(su_a, 14)

                def dw(n, ct):
                    lo, hi = slots(n)
                    if ct == 0:
                        if n.within(0, NB - 1):
                            pe.wait_ge(z_a, 5 * n.val + QK)
                        wait(pe, carry, n.val)
                        if n.static and n.val == NB:
                            pe.wait_ge(row_z, 1)
                    wait(pe, dw_l, len(DVE_TAPS) * (QK * n.val + ct - 2) + 1)
                    for k, tap in enumerate(PE_TAPS):
                        ky, kx = divmod(tap, KX)
                        last = nc.tensor.matmul(db[(n.par + ct) % 2][:, lo * W:hi * W].rearrange("p (r w) -> p r w", w=W),
                                                diag[:, ct, k, :], zwin[n.par][:, ct, ky + lo:ky + hi, kx:kx + W],
                                                start=(k == 0), stop=(k == len(PE_TAPS) - 1))
                    last.then_inc(dw_t, 1)

                def tile_no(n, t):
                    return ROWS * n.val - 1 + t

                def q_tr(n, t):
                    lo, hi = slots(n)
                    if lo <= t < hi:
                        c = tile_no(n, t)
                        if t == lo:
                            pe.wait_ge(qs_ok, QK * n.val + QK)
                        wait(pe, q_a, c)
                        for ct in range(QK):
                            last = nc.tensor.transpose(qb[:, ct * 128:ct * 128 + 128], qs[:, n.par, ct, t, :], ident[:, :])
                        last.then_inc(q_t, 1)

                def gram(n, t):
                    lo, hi = slots(n)
                    if lo <= t < hi:
                        c = tile_no(n, t)
                        pe.wait_ge(q_a, c + 1)
                        first = n.static and n.val == 0 and t == lo
                        final = n.static and n.val == NB
                        for g in (0, 1):
                            last = nc.tensor.matmul(gb[0:G2, g * G2:g * G2 + G2], qk_tok[:, t % 2, G2 * g:G2 * g + G2],
                                                    qk_tok[:, t % 2, C + G2 * g:C + G2 * g + G2],
                                                    start=(first and g == 0), stop=final, skip_group_check=True)
                        last.then_inc(gr_t, 1)

                def z(i, ct):
                    o, m = ZT[ct]
                    c = 5 * i.val + ct
                    if ct == 0:
                        pe.wait_ge(lo_ok, 2 * i.val + 2)
                    wait(pe, z_a, c - 1)
                    dst = zb[(i.par + ct) % 2][0:m, :]
                    ops = [(wq_ah, xh_a), (wq_al, xh_a), (wq_ah, xl_a), (wq_ch, x_c), (wq_cl, x_c)]
                    for k, (w, v) in enumerate(ops):
                        last = nc.tensor.matmul(dst, w[:, o:o + m], v[:, 0, :], start=(k == 0), stop=(k == 4))
                    last.then_inc(z_t, 1)

                def step(i):
                    if i.within(0, NB - 1):
                        pe.wait_ge(tn_ok, i.val + 1)
                        wait(pe, xt_a, 2 * min(i.val + 2, NB) if i.static else 2 * i.val + 4)
                        for h in (0, 1):
                            for t in range(ROWS):
                                last = nc.tensor.transpose(tp[h][:, t * 128:t * 128 + 128], tn[:, t, h * 128:h * 128 + 128], ident[:, :])
                            last.then_inc(ac_t, 1)
                    n, m = i - 1, i - 2
                    has_n, has_m = n.within(0, NB), m.within(0, NB)
                    if has_n:
                        dw(n, 0)
                    if has_m:
                        q_tr(m, 0)
                    if has_n:
                        dw(n, 1)
                    if has_m:
                        q_tr(m, 1)
                        gram(m, 0)
                    b = i + 2
                    if b.within(0, NB - 1):
                        pe.wait_ge(ld_x[b.par], 32 * b.half + 32)
                        if i.static:
                            wait(pe, lo_ok, 2 * i.val + 2)
                            wait(pe, xt_a, 2 * b.val)
                        else:
                            pe.wait_ge(lo_ok, 2 * i.val + 2)
                        for t in range(ROWS):
                            cols = slice(t * 128, t * 128 + 128)
                            o = t % 2 * C
                            nc.tensor.transpose(tp[t // 2][:, o:o + CA], xc_a[:, b.par, cols], ident[:, :])
                            last = nc.tensor.transpose(tp[t // 2][:, o + CA:o + C], xc_b[:, b.par, cols], ident[0:CB, 0:CB])
                        last.then_inc(xt_t, 1)
                    if has_m:
                        q_tr(m, 2)
                        gram(m, 1)
                    if has_n:
                        dw(n, 2)
                    if has_m:
                        q_tr(m, 3)
                        gram(m, 2)
                    if i.within(0, NB - 1):
                        z(i, 0)
                    if has_m:
                        gram(m, 3)
                    if i.within(0, NB - 1):
                        for ct in range(1, 5):
                            z(i, ct)

                steps(pe, step, FIRST, LAST, LO, HI)
                pe.wait_ge(at_v, 3)
                nc.tensor.transpose(db[0][0:QK, 0:128], n2[:, 1, :], ident[:, :]).then_inc(at_t, 1)
                pe.wait_ge(at_a, 1)
                pe.wait_ge(const, 12)
                for ct in range(QK):
                    last = nc.tensor.matmul(db[1][0:G2, ct * 128:ct * 128 + 128], sel[:, ct, :], rn_row[:, :], start=True, stop=True)
                last.then_inc(at_t, 1)
                pe.wait_ge(at_v, 15)
                for g in (0, 1):
                    last = nc.tensor.matmul(db[0][0:G2, g * C:g * C + C], attn[:, 3, g, :], wpt[:, g, :], start=True, stop=True)
                last.then_inc(at_t, 1)

        p2 = ExitStack()
        with p2:
            vwin = sb(p2, "vwin", [G2, 2, 2, 6, W + 2])
            vd = sb(p2, "vd", [G2, 2, ROWS, W])
            y_acc = sb(p2, "y_acc", [128, 2, ROWS, 2 * C])
            hf = sb(p2, "hf", [128, 3, TOK])
            hh = sb(p2, "hh", [128, 3, TOK], F32R)
            hl = sb(p2, "hl", [128, 3, TOK], F32R)
            fin = sb(p2, "fin", [128, ROWS, C])
            fin_a = sb(p2, "fin_a", [CA, TOK])
            fin_b = sb(p2, "fin_b", [CB, TOK])
            sc = sb(p2, "sc", [128, 8, ROWS, E])
            cmp_ = sb(p2, "cmp", [128, 4, ROWS, E, E])
            col = sb(p2, "col", [128, 6, ROWS])
            tri = sb(p2, "tri", [128, ROWS, E, E])
            e_base = sb(p2, "e_base", [128, ROWS, E])
            gm = sb(p2, "gm", [128, 2, ROWS, E])
            gmt = sb(p2, "gmt", [E, TOK])

            lb = banks[0:2]
            yb = banks[2:6]
            mb = banks[6:8]

            c2 = sem("c2")
            ld_xt = [sem("ld_xt0"), sem("ld_xt1")]
            ld_v = [sem("ld_v0"), sem("ld_v1")]
            st_out = sem("st_out")
            vd_l, vd_ok = sem("vd_l"), sem("vd_ok")
            co_t = sem("co_t")
            x1_ok, bn_l, mv2, r2_l, r2_ok, tn2, ac2 = (sem(s) for s in ("x1_ok", "bn_l", "mv2", "r2_l", "r2_ok", "tn2", "ac2"))
            hi2, lo2, g_t, g_v, g_p, g_l, gm_ok = (sem(s) for s in ("hi2", "lo2", "g_t", "g_v", "g_p", "g_l", "gm_ok"))
            gt_t, gt_a, b2_t, b2_a = (sem(s) for s in ("gt_t", "gt_a", "b2_t", "b2_a"))
            l1, gelu, hh_ok, hl_ok, y_t, y_v = (sem(s) for s in ("l1", "gelu", "hh_ok", "hl_ok", "y_t", "y_v"))
            fin_ok, ot_t, ot_a = sem("fin_ok"), sem("ot_t"), sem("ot_a")

            FIRST2, LAST2, LO2, HI2 = -1, NB, 1, NB - 4
            TAPS_AT = {0: 1, 1: 1, 3: 2, 4: 1, 5: 2, 6: 1, 7: 2, 9: 2, 10: 1, 11: 2, 12: 1, 13: 2}
            assert sum(TAPS_AT.values()) == 18
            PROJ_AT, X1_AT, TN_AT, AC_AT, HI_AT, LO_AT, SCORE_AT = 14, 15, 17, 18, 19, 20, 21
            GT_AT, B2_AT, B2C_AT, OUT_AT, OUTC_AT = 4, 5, 6, 8, 9
            GATE_V, GATE_L = 3, 10

            blk = p2.enter_context(nc.Block())

            @blk.sync
            def _(sp):
                def load(b):
                    if not b.within(0, NB - 1):
                        return
                    wait(sp, x1_ok, ROWS * (b.val - 1))
                    sp.dma_start(xtok[:, b.par, :, :], xtok_dram[bass.ds(b.val * ROWS, ROWS), :, :].rearrange("r p c -> p r c"))\
                        .then_inc(ld_xt[b.par], 16)
                    for g in (0, 1):
                        sp.dma_start(vwin[:, b.par, g, :, 1:W + 1], v_view[:, g, bass.ds(b.val * ROWS, 6), :]).then_inc(ld_v[b.par], 16)

                def step(i):
                    load(i + 2)
                    b = i - 1
                    if b.within(0, NB - 1):
                        cols = bass.ds(b.val * TOK, TOK)
                        sp.wait_ge(ot_a, 2 * b.val + 1)
                        sp.dma_start(out_view[0:CA, cols], fin_a[:, :]).then_inc(st_out, 16)
                        sp.wait_ge(ot_a, 2 * b.val + 2)
                        sp.dma_start(out_view[CA:C, cols], fin_b[:, :]).then_inc(st_out, 16)

                sp.wait_ge(c2, 1)
                load(Step(0, 0))
                steps(sp, step, FIRST2, LAST2, LO2, HI2)
                sp.wait_ge(st_out, 32 * NB)

            @blk.gpsimd
            def _(pool):
                nc.gpsimd.memset(vwin[:, :, :, :, :], 0.0).then_inc(c2, 1)
                nc.gpsimd.memset(tri[:, :, :, :], 1.0).then_inc(c2, 1)
                nc.gpsimd.memset(e_base[:, :, :], E_BASE).then_inc(c2, 1)
                pool.wait_ge(c2, 3)
                nc.gpsimd.affine_select(out=tri[:, :, :, :], in_=tri[:, :, :, :], compare_op=ALU.is_gt, fill=0.0,
                                        base=0, pattern=[[0, ROWS], [1, E], [-1, E]], channel_multiplier=0).then_inc(c2, 1)

                def step(i):
                    b = i - 1
                    if b.within(0, NB - 1):
                        pool.wait_ge(y_v, 4 * E * b.val + 4 * E)
                        wait(pool, ot_t, 2 * b.val)
                        nc.gpsimd.tensor_tensor(fin[:, :, :], y_acc[:, b.par, :, 0:C], y_acc[:, b.par, :, C:2 * C], ALU.add)\
                            .then_inc(fin_ok, 1)
                    b = i + 1
                    if b.within(0, NB - 1):
                        pool.wait_ge(mv2, b.val + 1)
                        nc.gpsimd.tensor_tensor(small[:, 4, :], mv[:, 0, :, 1], pw[:, 2, :], ALU.add).then_inc(r2_l, 1)
                        pool.wait_ge(r2_l, b.val + 1)
                        nc.gpsimd.tensor_tensor(rstd[:, 0, :], small[:, 4, :], pw[:, 0, :], ALU.pow).then_inc(r2_ok, 1)
                        pool.wait_ge(g_v, GATE_V * b.val + 3)
                        nc.gpsimd.tensor_tensor(sc[:, 2, :, :], e_base[:, :, :], sc[:, 1, :, :], ALU.pow).then_inc(g_p, 1)

                steps(pool, step, FIRST2, LAST2, LO2, HI2)

            @blk.scalar
            def _(act):
                def chunk(i, k):
                    c = NCH * i.val + k
                    act.wait_ge(l1, c + 1)
                    wait(act, hl_ok, c - 2)
                    nc.scalar.activation(hf[:, k % 3, :], lb[k % 2][:, :], ACT.Gelu, bias=b1_col[:, k:k + 1]).then_inc(gelu, 1)
                    act.wait_ge(gelu, c + 1)
                    wait(act, y_t, ROWS * (c - 2))
                    nc.scalar.activation(hh[:, k % 3, :], hf[:, k % 3, :], ACT.Copy).then_inc(hh_ok, 1)

                def step(i):
                    cur, nxt, old = i.within(0, NB - 1), (i + 1).within(0, NB - 1), (i - 1).within(0, NB - 1)
                    for k in range(NCH):
                        if cur:
                            chunk(i, k)
                        if k == GT_AT and cur:
                            act.wait_ge(gt_t, i.val + 1)
                            wait(act, b2_t, 2 * i.val)
                            nc.scalar.activation(gmt[:, :], mb[0][0:E, :], ACT.Copy).then_inc(gt_a, 1)
                        if k == B2C_AT and cur:
                            for h in (0, 1):
                                act.wait_ge(b2_t, 2 * i.val + h + 1)
                                wait(act, fin_ok, i.val - 1)
                                nc.scalar.activation(y_acc[:, i.par, 2 * h:2 * h + 2, C:2 * C],
                                                     mb[h][:, 0:2 * C].rearrange("p (t c) -> p t c", c=C), ACT.Copy).then_inc(b2_a, 1)
                        if k == OUTC_AT and old:
                            b = i - 1
                            act.wait_ge(ot_t, 2 * b.val + 1)
                            wait(act, st_out, 32 * b.val)
                            nc.scalar.activation(fin_a[:, :], mb[0][:, :], ACT.Copy).then_inc(ot_a, 1)
                            act.wait_ge(ot_t, 2 * b.val + 2)
                            nc.scalar.activation(fin_b[:, :], mb[1][0:CB, :], ACT.Copy).then_inc(ot_a, 1)
                        if k == HI_AT and nxt:
                            b = i + 1
                            act.wait_ge(ac2, 2 * b.val + 1)
                            wait(act, l1, NCH * (b.val - 1))
                            nc.scalar.activation(xh_a[:, b.par, :], mb[0][:, :], ACT.Copy).then_inc(hi2, 1)
                            act.wait_ge(ac2, 2 * b.val + 2)
                            nc.scalar.activation(x_c[:, b.par, :], mb[1][:, :], ACT.Copy).then_inc(hi2, 1)

                steps(act, step, FIRST2, LAST2, LO2, HI2)

            @blk.vector
            def _(dve):
                def tap(b, n):
                    g, k = divmod(n, 9)
                    ky, kx = divmod(k, KX)
                    src = vwin[:, b.par, g, ky:ky + ROWS, kx:kx + W]
                    if n == 0:
                        dve.wait_ge(ld_v[b.par], 32 * b.half + 32)
                        wait(dve, co_t, 2 * b.val)
                    if k == 0:
                        ins = nc.vector.tensor_scalar(vd[:, g, :, :], src, wdw_v[:, g, 0:1], None, ALU.mult)
                    else:
                        dve.wait_ge(vd_l, 18 * b.val + n)
                        ins = nc.vector.scalar_tensor_tensor(out=vd[:, g, :, :], in0=src, scalar=wdw_v[:, g, k:k + 1],
                                                             in1=vd[:, g, :, :], op0=ALU.mult, op1=ALU.add)
                    ins.then_inc(vd_l, 1)

                def expert_sum(s, e):
                    ex = E * s.val + e
                    if e == 0:
                        dve.wait_ge(gm_ok, s.val + 1)
                        dve.wait_ge(b2_a, 2 * s.val + 2)
                        dve.wait_ge(x1_ok, ROWS * s.val + ROWS)
                    else:
                        dve.wait_ge(y_v, 4 * ex)
                    for t in range(ROWS):
                        dve.wait_ge(y_t, ROWS * (NCH * s.val + CH * e + CH - 1) + t + 1)
                        nc.vector.scalar_tensor_tensor(out=y_acc[:, s.par, t, :], in0=yb[t][:, 0:2 * C], scalar=gm[:, s.par, t, e:e + 1],
                                                       in1=y_acc[:, s.par, t, :], op0=ALU.mult, op1=ALU.add).then_inc(y_v, 1)

                def gate_1(b):
                    base = GATE_V * b.val
                    dve.wait_ge(g_t, b.val + 1)
                    nc.vector.tensor_tensor(sc[:, 0, :, :], mb[0][:, 0:ROWS * E].rearrange("p (t e) -> p t e", e=E),
                                            gate_bb[:, None, :].to_broadcast([128, ROWS, E]), ALU.add).then_inc(g_v, 1)
                    dve.wait_ge(g_v, base + 1)
                    nc.vector.tensor_reduce(out=col[:, 0, :], in_=sc[:, 0, :, :], axis=AX, op=ALU.max).then_inc(g_v, 1)
                    dve.wait_ge(g_v, base + 2)
                    wait(dve, gm_ok, b.val)
                    nc.vector.tensor_tensor(sc[:, 1, :, :], sc[:, 0, :, :], col[:, 0, :, None].to_broadcast([128, ROWS, E]),
                                            ALU.subtract).then_inc(g_v, 1)

                def gate_2(b):
                    base = GATE_V * b.val
                    dve.wait_ge(g_p, b.val + 1)
                    p = sc[:, 2, :, :]
                    other = p[:, :, None, :].to_broadcast([128, ROWS, E, E])
                    own = p[:, :, :, None].to_broadcast([128, ROWS, E, E])
                    k = [0]

                    def link(ins):
                        k[0] += 1
                        ins.then_inc(g_l, 1)
                        dve.wait_ge(g_l, GATE_L * b.val + k[0])

                    link(nc.vector.tensor_tensor(cmp_[:, 0], other, own, ALU.is_gt))
                    link(nc.vector.tensor_tensor(cmp_[:, 1], other, own, ALU.is_equal))
                    link(nc.vector.reduce_sum(col[:, 1, :], p, AX))
                    link(nc.vector.tensor_tensor(cmp_[:, 2], cmp_[:, 1], tri[:, :, :, :], ALU.mult))
                    link(nc.vector.tensor_tensor(cmp_[:, 3], cmp_[:, 2], cmp_[:, 0], ALU.add))
                    link(nc.vector.reduce_sum(sc[:, 3, :, :], cmp_[:, 3], AX))
                    link(nc.vector.scalar_tensor_tensor(out=sc[:, 4, :, :], in0=sc[:, 3, :, :], scalar=1.5, in1=p,
                                                        op0=ALU.is_lt, op1=ALU.mult))
                    link(nc.vector.reduce_sum(col[:, 2, :], sc[:, 4, :, :], AX))
                    link(nc.vector.scalar_tensor_tensor(out=col[:, 3, :], in0=col[:, 1, :], scalar=EPS_GATE, in1=col[:, 2, :],
                                                        op0=ALU.mult, op1=ALU.add))
                    link(nc.vector.reciprocal(col[:, 4, :], col[:, 3, :]))
                    assert k[0] == GATE_L
                    wait(dve, y_v, 4 * E * (b.val - 1))
                    nc.vector.tensor_tensor(gm[:, b.par, :, :], sc[:, 4, :, :], col[:, 4, :, None].to_broadcast([128, ROWS, E]),
                                            ALU.mult).then_inc(gm_ok, 1)

                def step(i):
                    cur, nxt, old = i.within(0, NB - 1), (i + 1).within(0, NB - 1), (i - 1).within(0, NB - 1)
                    taps = 0
                    for k in range(NCH):
                        e, m = divmod(k - LAG, CH)
                        if m == 0 and e > 0 and cur:
                            expert_sum(i, e - 1)
                        if k == LAG and old:
                            expert_sum(i - 1, E - 1)
                        if cur:
                            c = NCH * i.val + k
                            dve.wait_ge(hh_ok, c + 1)
                            wait(dve, y_t, ROWS * (c - 2))
                            nc.vector.tensor_tensor(hl[:, k % 3, :], hf[:, k % 3, :], hh[:, k % 3, :].bitcast(FP32), ALU.subtract)\
                                .then_inc(hl_ok, 1)
                        if k == 1 and cur:
                            gate_2(i)
                        b = i + 1
                        if nxt:
                            for _ in range(TAPS_AT.get(k, 0)):
                                tap(b, taps)
                                taps += 1
                            if k == X1_AT:
                                dve.wait_ge(ld_xt[b.par], 16 * b.half + 16)
                                wait(dve, fin_ok, b.val - 1)
                                for t in range(ROWS):
                                    dve.wait_ge(co_t, 2 * b.val + t // 2 + 1)
                                    nc.vector.scalar_tensor_tensor(
                                        out=y_acc[:, b.par, t, 0:C], in0=mb[t // 2][:, t % 2 * C:t % 2 * C + C],
                                        scalar=s_tok[:, bass.ds(b.val * ROWS + t, 1)], in1=xtok[:, b.par, t, :],
                                        op0=ALU.mult, op1=ALU.add).then_inc(x1_ok, 1)
                                dve.wait_ge(x1_ok, ROWS * b.val + ROWS)
                                for t in range(ROWS):
                                    last = nc.vector.bn_stats(stat[:, 0, t, :], y_acc[:, b.par, t, 0:C])
                                last.then_inc(bn_l, 1)
                                dve.wait_ge(bn_l, b.val + 1)
                                nc.vector.memset(pause[:, 1:2], 0.0)
                                for t in range(ROWS):
                                    last = nc.vector.bn_aggr(mv[:, 0, t, :], stat[:, 0, t, :])
                                last.then_inc(mv2, 1)
                            if k == TN_AT:
                                dve.wait_ge(r2_ok, b.val + 1)
                                wait(dve, ac2, 2 * b.val)
                                for t in range(ROWS):
                                    for o, n, s0 in ((0, C, 0), (C, CB, CA)):
                                        last = nc.vector.tensor_scalar(tn[:, t, o:o + n], y_acc[:, b.par, t, s0:s0 + n], mv[:, 0, t, 0:1],
                                                                       rstd[:, 0, t:t + 1], ALU.subtract, ALU.mult)
                                last.then_inc(tn2, 1)
                            if k == LO_AT:
                                dve.wait_ge(hi2, 2 * b.val + 2)
                                nc.vector.tensor_tensor(xl_a[:, b.par, :], mb[0][:, :], xh_a[:, b.par, :].bitcast(FP32), ALU.subtract).then_inc(lo2, 1)
                                nc.vector.tensor_tensor(x_c[CB:128, b.par, :], mb[1][CB:128, :], x_c[CB:128, b.par, :].bitcast(FP32), ALU.subtract)\
                                    .then_inc(lo2, 1)
                            if k == NCH - 1:
                                gate_1(b)

                dve.wait_ge(c2, 4)
                steps(dve, step, FIRST2, LAST2, LO2, HI2)

            @blk.tensor
            def _(pe):
                def first(i, k):
                    c = NCH * i.val + k
                    if k == 0:
                        pe.wait_ge(lo2, 2 * i.val + 2)
                    wait(pe, gelu, c - 1)
                    ops = [(w1_ah, xh_a), (w1_al, xh_a), (w1_ah, xl_a), (w1_ch, x_c), (w1_cl, x_c)]
                    for n, (w, v) in enumerate(ops):
                        last = nc.tensor.matmul(lb[k % 2][:, :], w[:, k * 128:k * 128 + 128], v[:, i.par, :], start=(n == 0), stop=(n == 4))
                    last.then_inc(l1, 1)

                def second(s, k):
                    c = NCH * s.val + k
                    e, m = divmod(k, CH)
                    ex = E * s.val + e
                    pe.wait_ge(hl_ok, c + 1)
                    for t in range(ROWS):
                        if m == 0:
                            wait(pe, y_v, 4 * (ex - 1) + t + 1)
                        cols = slice(t * 128, t * 128 + 128)
                        nc.tensor.matmul(yb[t][:, 0:2 * C], hh[:, k % 3, cols], w2_hl[:, k, :], start=(m == 0), stop=False, skip_group_check=True)
                        last = nc.tensor.matmul(yb[t][:, 0:C], hl[:, k % 3, cols], w2_hl[:, k, 0:C], start=False, stop=(m == CH - 1), skip_group_check=True)
                        last.then_inc(y_t, 1)

                def step(i):
                    cur, nxt, old = i.within(0, NB - 1), (i + 1).within(0, NB - 1), (i - 1).within(0, NB - 1)
                    for k in range(NCH):
                        if cur:
                            first(i, k)
                        if k < LAG:
                            if old:
                                second(i - 1, NCH - LAG + k)
                        elif cur:
                            second(i, k - LAG)
                        if cur and k == GT_AT:
                            pe.wait_ge(gm_ok, i.val + 1)
                            for t in range(ROWS):
                                last = nc.tensor.transpose(mb[0][0:E, t * 128:t * 128 + 128], gm[:, i.par, t, :], ident[:, :])
                            last.then_inc(gt_t, 1)
                        if cur and k == B2_AT:
                            pe.wait_ge(gt_a, i.val + 1)
                            for t in range(ROWS):
                                last = nc.tensor.matmul(mb[t // 2][:, t % 2 * C:t % 2 * C + C], gmt[:, t * 128:t * 128 + 128], b2_row[:, :],
                                                        start=True, stop=True)
                                if t % 2:
                                    last.then_inc(b2_t, 1)
                        if old and k == OUT_AT:
                            b = i - 1
                            pe.wait_ge(fin_ok, b.val + 1)
                            if cur:
                                pe.wait_ge(b2_a, 2 * i.val + 2)
                            for t in range(ROWS):
                                last = nc.tensor.transpose(mb[0][:, t * 128:t * 128 + 128], fin[:, t, 0:CA], ident[:, :])
                            last.then_inc(ot_t, 1)
                            for t in range(ROWS):
                                last = nc.tensor.transpose(mb[1][0:CB, t * 128:t * 128 + 128], fin[:, t, CA:C], ident[:, :])
                            last.then_inc(ot_t, 1)
                        if nxt and k == PROJ_AT:
                            b = i + 1
                            pe.wait_ge(vd_l, 18 * b.val + 18)
                            if old:
                                pe.wait_ge(ot_a, 2 * (i - 1).val + 2)
                            elif cur:
                                pe.wait_ge(b2_a, 2 * i.val + 2)
                            for t in range(ROWS):
                                for g in (0, 1):
                                    last = nc.tensor.matmul(mb[t // 2][:, t % 2 * C:t % 2 * C + C], vd[:, g, t, :], mt[:, g, :],
                                                            start=(g == 0), stop=(g == 1))
                                if t % 2:
                                    last.then_inc(co_t, 1)
                        if nxt and k == AC_AT:
                            b = i + 1
                            pe.wait_ge(tn2, b.val + 1)
                            for h in (0, 1):
                                for t in range(ROWS):
                                    last = nc.tensor.transpose(mb[h][:, t * 128:t * 128 + 128], tn[:, t, h * 128:h * 128 + 128], ident[:, :])
                                last.then_inc(ac2, 1)
                        if nxt and k == SCORE_AT:
                            b = i + 1
                            pe.wait_ge(lo2, 2 * b.val + 2)
                            ops = [(xh_a, 0), (xh_a, 1), (xl_a, 0), (x_c, 2), (x_c, 3)]
                            for t in range(ROWS):
                                for n, (v, w) in enumerate(ops):
                                    last = nc.tensor.matmul(mb[0][:, t * E:t * E + E], v[:, b.par, t * 128:t * 128 + 128], gate_r[:, w, :],
                                                            start=(n == 0), stop=(n == 4))
                            last.then_inc(g_t, 1)

                steps(pe, step, FIRST2, LAST2, LO2, HI2)
    return nc


_INS = ["x", "L0_conv_spatial_interaction", "L0_conv_ln_w", "L0_conv_ln_b", "L0_conv_w_qkv", "L0_conv_w_dw",
        "L0_conv_w_proj", "L0_conv_temperature", "L0_ffn_gate_w", "L0_ffn_gate_b", "L0_ffn_w1", "L0_ffn_b1",
        "L0_ffn_w2", "L0_ffn_b2"]


def kernel(**inputs):
    import numpy as _np
    import concourse.bacc as _bacc
    from concourse import mybir as _mybir
    from concourse.bass_utils import run_bass_kernel_spmd as _run

    nc = _bacc.Bacc("TRN2", target_bir_lowering=False, num_devices=1)
    arrays, args = {}, []
    for name in _INS:
        a = _np.ascontiguousarray(inputs[name])
        arrays[f"in_{name}_dram"] = a
        args.append(nc.dram_tensor(f"in_{name}_dram", a.shape, _mybir.dt.from_np(a.dtype), kind="ExternalInput").ap())
    out = nc.dram_tensor("out_0_dram", (1, C, H, W), _mybir.dt.float32, kind="ExternalOutput").ap()
    build(nc, *args, out)
    r = _run(nc, [arrays], core_ids=[0])
    return r.results[0]["out_0_dram"]
```

```python
import concourse.bass as bass
from concourse import mybir
from contextlib import ExitStack

FP32 = mybir.dt.float32
F32R = mybir.dt.float32r
ALU = mybir.AluOpType
ACT = mybir.ActivationFunctionType
AX = mybir.AxisListType.X

C = 192
H = W = 128
ROWS = 4
TOK = ROWS * W
NB = H // ROWS
CA = 128
CB = C - CA
G2 = C // 2
HEADS = 8
HD = C // HEADS
E = 4
HID = 4 * C
CH = HID // 128
NCH = E * CH
LAG = 2
ZT = [(0, 128), (128, 128), (256, 128), (384, G2), (480, G2)]
QK = 3
KX = 3
PE_TAPS = [0, 1, 2]
DVE_TAPS = [3, 4, 5, 6, 7, 8]
EPS_C, EPS_LN, EPS_NORM, EPS_GATE = 1e-6, 1e-5, 1e-12, 1e-9
NEG = -1e30
E_BASE = 2.718281828459045


class Step:

    def __init__(self, j, c):
        self.j, self.c = j, c

    def __add__(self, n):
        return Step(self.j, self.c + n)

    def __sub__(self, n):
        return Step(self.j, self.c - n)

    @property
    def static(self):
        return isinstance(self.j, int)

    @property
    def val(self):
        return 2 * self.j + self.c

    @property
    def half(self):
        return self.j + self.c // 2

    @property
    def par(self):
        return self.c % 2

    def within(self, lo, hi):
        return not self.static or lo <= self.val <= hi


def wait(eng, sem, value):
    if isinstance(value, int) and value <= 0:
        return
    eng.wait_ge(sem, value)


def steps(eng, emit, first, last, lo, hi):
    assert (hi - lo) % 2 == 1
    for n in range(first, lo):
        emit(Step(0, n))
    with eng.Fori(0, (hi - lo + 1) // 2) as j:
        for u in (0, 1):
            emit(Step(j, lo + u))
    for n in range(hi + 1, last + 1):
        emit(Step(0, n))


def build(nc, x, spat, ln_w, ln_b, w_qkv, w_dw, w_proj, temperature, gate_w, gate_b, w1, b1, w2, b2, out):
    top = ExitStack()
    with top:
        def sb(stack, name, shape, dt=FP32):
            return stack.enter_context(nc.sbuf_tensor(name, shape, dt))

        def sem(name):
            return top.enter_context(nc.semaphore(name))

        xtok_dram = nc.dram_tensor("xtok_scratch", (H, W, C), FP32, kind="Internal").ap()
        v_dram = nc.dram_tensor("v_scratch", (C, H + 2, W), FP32, kind="Internal").ap()
        v_view = v_dram.rearrange("(g p) r w -> p g r w", g=2)
        x_view = x.rearrange("a c h w -> (a c) (h w)")
        out_view = out.rearrange("a c h w -> (a c) (h w)")
        s_view = spat.rearrange("a b h w -> (a b h) w")

        ident = sb(top, "ident", [128, 128])
        w1_ah = sb(top, "w1_ah", [CA, NCH * 128], F32R)
        w1_al = sb(top, "w1_al", [CA, NCH * 128], F32R)
        w1_ch = sb(top, "w1_ch", [128, NCH * 128], F32R)
        w1_cl = sb(top, "w1_cl", [128, NCH * 128], F32R)
        w2_hl = sb(top, "w2_hl", [128, NCH, 2 * C], F32R)
        b1_col = sb(top, "b1_col", [128, NCH])
        b2_row = sb(top, "b2_row", [E, C])
        gate_raw = sb(top, "gate_raw", [128, 2, E])
        gate_r = sb(top, "gate_r", [128, 4, 128], F32R)
        gate_bb = sb(top, "gate_bb", [128, E])
        wdw_v = sb(top, "wdw_v", [G2, 2, 9])
        s_tok = sb(top, "s_tok", [128, H])
        mt = sb(top, "mt", [G2, 2, C])
        xh_a = sb(top, "xh_a", [CA, 2, TOK], F32R)
        xl_a = sb(top, "xl_a", [CA, 2, TOK], F32R)
        x_c = sb(top, "x_c", [128, 2, TOK], F32R)
        tn = sb(top, "tn", [128, ROWS, 2 * 128])
        xtok = sb(top, "xtok", [128, 2, ROWS, C])
        stat = sb(top, "stat", [128, 2, ROWS, 6])
        mv = sb(top, "mv", [128, 2, ROWS, 2])
        rstd = sb(top, "rstd", [128, 2, ROWS])
        pw = sb(top, "pw", [128, 3, ROWS])
        pause = sb(top, "pause", [128, 2])
        small = sb(top, "small", [128, 6, ROWS])

        banks = [top.enter_context(nc.psum_tensor(f"bank{n}", [128, 512], FP32)) for n in range(8)]

        p1 = ExitStack()
        with p1:
            stage = sb(p1, "stage", [128, NCH * 128])
            wn = stage[:, 0:5 * C].rearrange("p (t c) -> p t c", t=5)
            wp = stage[:, 5 * C:5 * C + 5 * 256].rearrange("p (t c) -> p t c", t=5)
            wtmp = stage[:, 5 * (C + 256):5 * (C + 256) + C]
            lnw_bb = sb(p1, "lnw_bb", [128, C])
            lnb_bb = sb(p1, "lnb_bb", [128, C])
            bz = sb(p1, "bz", [128, 5])
            wq_ah = sb(p1, "wq_ah", [CA, 3 * C], F32R)
            wq_al = sb(p1, "wq_al", [CA, 3 * C], F32R)
            wq_ch = sb(p1, "wq_ch", [128, 3 * C], F32R)
            wq_cl = sb(p1, "wq_cl", [128, 3 * C], F32R)
            wdw = sb(p1, "wdw", [128, QK, 9])
            diag = sb(p1, "diag", [128, QK, len(PE_TAPS), 128])
            wpr = sb(p1, "wpr", [128, 2, C])
            wpt = sb(p1, "wpt", [G2, 2, C])
            s_rows = sb(p1, "s_rows", [128, W])
            zero = sb(p1, "zero", [G2, 2, 2, W])
            xc_a = sb(p1, "xc_a", [CA, 2, TOK])
            xc_b = sb(p1, "xc_b", [CB, 2, TOK])
            zwin = [sb(p1, f"zwin{p}", [128, QK, 6, W + 2]) for p in (0, 1)]
            zv = sb(p1, "zv", [G2, 2, TOK])
            s_bc = sb(p1, "s_bc", [128, 2, ROWS, W])
            acc = sb(p1, "acc", [128, QK, ROWS, W])
            qs = sb(p1, "qs", [128, 2, QK, ROWS, W])
            junk = xl_a[:, 1, :]
            qk_tok = sb(p1, "qk_tok", [128, 2, 2 * C])
            nrm = sb(p1, "nrm", [128, QK, NB + 1])
            n2 = sb(p1, "n2", [128, 4, QK])
            rn_row = sb(p1, "rn_row", [QK, 128])
            sel = sb(p1, "sel", [QK, QK, G2])
            rb = sb(p1, "rb", [G2, 2 * C])
            temp = sb(p1, "temp", [G2, 2])
            mask = sb(p1, "mask", [G2, 2, E, HD])
            attn = sb(p1, "attn", [G2, 4, 2, G2])
            acol = sb(p1, "acol", [G2, 6, 2])

            tp = banks[0:2]
            zb = banks[2:4]
            db = banks[4:6]
            qb = banks[6]
            gb = banks[7]

            ld_w = sem("ld_w")
            ld_zero = sem("ld_zero")
            ld_x = [sem("ld_x0"), sem("ld_x1")]
            ld_s = [sem("ld_s0"), sem("ld_s1")]
            st_xt = [sem("st_xt0"), sem("st_xt1")]
            st_v = sem("st_v")
            ld_e = sem("ld_e")
            e_hi, e_lo = sem("e_hi"), sem("e_lo")
            const = sem("const")
            su_v, su_t, su_a = sem("su_v"), sem("su_t"), sem("su_a")
            xt_t, xt_a = sem("xt_t"), sem("xt_a")
            stats = sem("stats")
            r_link, r_ok = sem("r_link"), sem("r_ok")
            tn_ok, tn_dup = sem("tn_ok"), sem("tn_dup")
            ac_t = sem("ac_t")
            hi_ok, lo_ok = sem("hi_ok"), sem("lo_ok")
            z_t, z_a = sem("z_t"), sem("z_a")
            carry = sem("carry")
            dw_t, dw_l = sem("dw_t"), [sem(f"dw_l{ct}") for ct in range(QK)]
            qs_ok, sq_ok = sem("qs_ok"), sem("sq_ok")
            q_t, q_a, gr_t = sem("q_t"), sem("q_a"), sem("gr_t")
            row_z = sem("row_z")
            at_v, at_t, at_a, at_p = sem("at_v"), sem("at_t"), sem("at_a"), sem("at_p")

            FIRST, LAST, LO, HI = -2, NB + 2, 3, NB - 6

            def slots(n):
                if n.static and n.val == 0:
                    return 1, ROWS
                if n.static and n.val == NB:
                    return 0, 1
                return 0, ROWS

            n_dve = len(DVE_TAPS)
            blk = p1.enter_context(nc.Block())
            N_LD_W = 26

            @blk.sync
            def _(sp):
                def load_x(b):
                    if b.within(0, NB - 1):
                        wait(sp, xt_t, b.val - 1)
                        cols = bass.ds(b.val * TOK, TOK)
                        sp.dma_start(xc_a[:, b.par, :], x_view[0:CA, cols]).then_inc(ld_x[b.par], 16)
                        sp.dma_start(xc_b[:, b.par, :], x_view[CA:C, cols]).then_inc(ld_x[b.par], 16)

                n_w = [0]

                def load_w(dst, src):
                    n_w[0] += 1
                    sp.dma_start(dst, src).then_inc(ld_w, 16)

                load_x(Step(0, 0))
                for ct, (o, m) in enumerate(ZT):
                    load_w(wn[0:m, ct, :], w_qkv[o:o + m, :])
                load_w(lnw_bb[:, :], ln_w.rearrange("(a c) -> a c", a=1).to_broadcast([128, C]))
                load_w(lnb_bb[:, :], ln_b.rearrange("(a c) -> a c", a=1).to_broadcast([128, C]))
                dw_rows = w_dw.rearrange("o a y x -> o (a y x)")
                load_w(wdw[:, :, :], dw_rows[0:QK * 128, :].rearrange("(t p) k -> p t k", p=128))
                load_w(wdw_v[:, :, :], dw_rows[2 * C:3 * C, :].rearrange("(t p) k -> p t k", p=G2))
                load_w(s_rows[:, :], s_view)
                load_w(wpr[:, 0, :], w_proj[0:CA, :])
                load_w(wpr[0:CB, 1, :], w_proj[CA:C, :])
                load_w(gate_raw[:, 0, :], gate_w[0:CA, :])
                load_w(gate_raw[0:CB, 1, :], gate_w[CA:C, :])
                load_w(gate_raw[CB:128, 1, :], gate_w[CA:C, :])
                load_w(gate_bb[:, :], gate_b.rearrange("(a c) -> a c", a=1).to_broadcast([128, E]))
                for h in range(HEADS):
                    load_w(temp[HD * (h % 4):HD * (h % 4) + HD, h // 4:h // 4 + 1],
                           temperature[h:h + 1, :, 0].to_broadcast([HD, 1]))
                load_w(b2_row[:, :], b2)
                with nc.allow_non_contiguous_dma(reason="24 columns of biases, once"):
                    load_w(b1_col[:, :], b1.rearrange("e (m p) -> p (e m)", p=128))
                assert n_w[0] == N_LD_W, n_w
                load_x(Step(0, 1))
                sp.wait_ge(const, 8)
                sp.dma_start(v_view[:, :, 0, :], zero[:, 0, :, :]).then_inc(ld_zero, 16)
                sp.dma_start(v_view[:, :, H + 1, :], zero[:, 1, :, :]).then_inc(ld_zero, 16)
                w1_rows = w1.rearrange("e c h -> c e h")
                w2_rows = w2.rearrange("e (m p) d -> p (e m) d", p=128)

                def stage_piece(n):
                    wait(sp, e_lo, n)
                    if n == 0:
                        dst = stage[:, :].rearrange("p (e h) -> p e h", e=E)
                        sp.dma_start(dst, w1_rows[0:CA]).then_inc(ld_e, 32)
                    elif n == 1:
                        for o in (0, CB):
                            dst = stage[o:o + CB, :].rearrange("p (e h) -> p e h", e=E)
                            sp.dma_start(dst, w1_rows[CA:C]).then_inc(ld_e, 16)
                    else:
                        k = NCH // 2
                        dst = stage[:, 0:k * C].rearrange("p (m d) -> p m d", d=C)
                        sp.dma_start(dst, w2_rows[:, (n - 2) * k:(n - 1) * k, :]).then_inc(ld_e, 32)

                def step(i):
                    load_x(i + 4)
                    b = i + 2
                    if b.within(0, NB - 1):
                        sp.wait_ge(xt_a, 2 * b.val + 2)
                        sp.dma_start(xtok_dram[bass.ds(b.val * ROWS, ROWS), :, :].rearrange("r p c -> p r c"),
                                     xtok[:, b.par, :, :]).then_inc(st_xt[b.par], 16)
                    n = i + 1
                    if n.within(0, NB):
                        wait(sp, qs_ok, QK * (n.val - 1))
                        lo, hi = slots(n)
                        rows = s_view[bass.ds(n.val * ROWS - 1 + lo, hi - lo), :].rearrange("r w -> (r w)")
                        sp.dma_start(s_bc[:, n.par, lo:hi, :].rearrange("p r w -> p (r w)"),
                                     rows.rearrange("(a n) -> a n", a=1).to_broadcast([128, (hi - lo) * W]))\
                          .then_inc(ld_s[n.par], 16)
                    if i.within(0, NB - 1):
                        sp.wait_ge(z_a, 5 * i.val + 5)
                        sp.dma_start(v_view[:, :, bass.ds(i.val * ROWS + 1, ROWS), :].rearrange("p g r w -> p g (r w)"),
                                     zv[:, :, :]).then_inc(st_v, 16)
                    if i.static and i.val == 0:
                        stage_piece(0)

                steps(sp, step, FIRST, LAST, LO, HI)
                for n in range(1, 4):
                    stage_piece(n)
                sp.wait_ge(ld_zero, 32)
                for p in (0, 1):
                    sp.wait_ge(st_xt[p], 16 * NB // 2)
                sp.wait_ge(st_v, 16 * NB)

            @blk.gpsimd
            def _(pool):
                nc.gpsimd.memset(gate_r[:, :, :].bitcast(FP32), 0.0).then_inc(const, 1)
                nc.gpsimd.memset(ident[:, :], 0.0).then_inc(const, 1)
                nc.gpsimd.memset(zero[:, :, :, :], 0.0).then_inc(const, 1)
                nc.gpsimd.memset(zwin[0][:, :, :, :], 0.0).then_inc(const, 1)
                nc.gpsimd.memset(zwin[1][:, :, :, :], 0.0).then_inc(const, 1)
                nc.gpsimd.memset(pw[:, 0, :], -0.5).then_inc(const, 1)
                nc.gpsimd.memset(pw[:, 1, :], EPS_C).then_inc(const, 1)
                nc.gpsimd.memset(pw[:, 2, :], EPS_LN).then_inc(const, 1)
                pool.wait_ge(const, 8)
                nc.gpsimd.affine_select(out=ident[:, :], in_=ident[:, :], compare_op=ALU.not_equal, fill=1.0,
                                        base=0, pattern=[[-1, 128]], channel_multiplier=1).then_inc(const, 1)
                nc.gpsimd.memset(sel[:, :, :], 0.0).then_inc(const, 1)
                nc.gpsimd.memset(mask[:, :, :, :], 0.0).then_inc(const, 1)
                pool.wait_ge(const, 11)
                nc.gpsimd.affine_select(out=sel[:, :, :], in_=sel[:, :, :], compare_op=ALU.not_equal, fill=1.0,
                                        base=0, pattern=[[-1, QK], [0, G2]], channel_multiplier=1).then_inc(const, 1)
                nc.gpsimd.affine_select(out=mask[:, :, :, :], in_=mask[:, :, :, :], compare_op=ALU.is_ge, fill=NEG,
                                        base=0, pattern=[[0, 2], [-HD, E], [0, HD]], channel_multiplier=1).then_inc(const, 1)
                pool.wait_ge(const, 13)
                nc.gpsimd.affine_select(out=mask[:, :, :, :], in_=mask[:, :, :, :], compare_op=ALU.is_ge, fill=NEG,
                                        base=HD - 1, pattern=[[0, 2], [HD, E], [0, HD]], channel_multiplier=-1).then_inc(const, 1)

                links = 5

                def step(i):
                    n = i - 1
                    if n.within(0, NB):
                        lo, hi = slots(n)
                        wait(pool, ld_s[n.par], 16 * n.half + 16)
                        wait(pool, q_t, ROWS * (n.val - 1) - 1)
                        wait(pool, sq_ok, QK * (n.val - 1))
                        for ct in range(QK):
                            pool.wait_ge(dw_l[ct], n_dve * (n.val + 1))
                            nc.gpsimd.tensor_tensor(qs[:, n.par, ct, lo:hi, :], acc[:, ct, lo:hi, :],
                                                    s_bc[:, n.par, lo:hi, :], ALU.mult).then_inc(qs_ok, 1)
                    b = i + 2
                    if b.within(0, NB - 1):
                        var = mv[:, b.par, :, 1]
                        t = [small[:, k, :] for k in range(4)]
                        pool.wait_ge(stats, b.val + 1)
                        base = links * b.val

                        def link(k, ins):
                            ins.then_inc(r_link, 1)
                            pool.wait_ge(r_link, base + k)

                        link(1, nc.gpsimd.tensor_tensor(t[0], var, pw[:, 1, :], ALU.add))
                        link(2, nc.gpsimd.tensor_tensor(t[1], t[0], pw[:, 0, :], ALU.pow))
                        link(3, nc.gpsimd.tensor_tensor(t[2], t[1], t[1], ALU.mult))
                        link(4, nc.gpsimd.tensor_tensor(t[3], t[2], var, ALU.mult))
                        link(5, nc.gpsimd.tensor_tensor(t[0], t[3], pw[:, 2, :], ALU.add))
                        nc.gpsimd.tensor_tensor(t[2], t[0], pw[:, 0, :], ALU.pow).then_inc(r_ok, 1)
                        pool.wait_ge(r_ok, 2 * b.val + 1)
                        if not (b.static and b.val < 2):
                            pool.wait_ge(tn_ok, b.val - 1)
                        nc.gpsimd.tensor_tensor(rstd[:, b.par, :], t[2], t[1], ALU.mult).then_inc(r_ok, 1)
                        pool.wait_ge(r_ok, 2 * b.val + 2)
                    if i.static and i.val == NB:
                        for ct in range(QK):
                            pool.wait_ge(dw_l[ct], n_dve * (NB - 1))
                        pool.wait_ge(dw_t, QK * (NB - 1))
                        nc.gpsimd.memset(zwin[NB % 2][:, :, 2, 1:W + 1], 0.0).then_inc(row_z, 1)

                steps(pool, step, FIRST, LAST, LO, HI)
                pool.wait_ge(at_v, 1)
                nc.gpsimd.tensor_scalar(n2[:, 1, :], pw[:, 0, 0:QK], -1.0, 0.0, ALU.mult, ALU.add).then_inc(at_p, 1)
                pool.wait_ge(at_p, 1)
                nc.gpsimd.tensor_tensor(n2[:, 2, :], n2[:, 0, :], n2[:, 1, :], ALU.pow).then_inc(at_p, 1)

            @blk.scalar
            def _(act):
                act.wait_ge(ld_w, 16 * N_LD_W)
                act.wait_ge(const, 1)
                nc.scalar.activation(gate_r[:, 0, 0:E], gate_raw[:, 0, :], ACT.Copy).then_inc(su_a, 1)
                nc.scalar.activation(gate_r[:, 2, 0:E], gate_raw[:, 1, :], ACT.Copy).then_inc(su_a, 1)
                for ct, (o, m) in enumerate(ZT):
                    act.wait_ge(su_t, 2 * ct + 2)
                    nc.scalar.activation(wq_ah[:, o:o + m], zb[ct % 2][:, 0:m], ACT.Copy).then_inc(su_a, 1)
                    nc.scalar.activation(wq_ch[:, o:o + m], zb[ct % 2][:, 128:128 + m], ACT.Copy).then_inc(su_a, 1)
                act.wait_ge(su_t, 11)
                nc.scalar.activation(s_tok[:, :], db[0][:, 0:128], ACT.Copy).then_inc(su_a, 1)
                act.wait_ge(su_t, 12)
                nc.scalar.activation(wpt[:, :, :], db[1][0:G2, 0:2 * C].rearrange("p (g o) -> p g o", g=2), ACT.Copy)\
                    .then_inc(su_a, 1)
                act.wait_ge(const, 8)

                def copy_q(n, t):
                    lo, hi = slots(n)
                    if lo <= t < hi:
                        c = ROWS * n.val - 1 + t
                        act.wait_ge(q_t, c + 1)
                        wait(act, gr_t, c - 1)
                        nc.scalar.activation(qk_tok[:, t % 2, :], qb[:, 0:2 * C], ACT.Copy).then_inc(q_a, 1)

                def copy_z(i, ct):
                    c = 5 * i.val + ct
                    m = ZT[ct][1]
                    act.wait_ge(z_t, c + 1)
                    if ct < QK:
                        wait(act, dw_l[ct], n_dve * (i.val - 1))
                        wait(act, dw_t, QK * (i.val - 2) + ct + 1)
                        nc.scalar.activation(zwin[i.par][:, ct, 2:6, 1:W + 1],
                                             zb[(i.par + ct) % 2][:, :].rearrange("p (r w) -> p r w", w=W),
                                             ACT.Identity, bias=bz[:, ct:ct + 1]).then_inc(z_a, 1)
                    else:
                        if ct == QK:
                            wait(act, st_v, 16 * i.val)
                        nc.scalar.activation(zv[:, ct - QK, :], zb[(i.par + ct) % 2][0:m, :], ACT.Identity,
                                             bias=bz[0:m, ct:ct + 1]).then_inc(z_a, 1)

                def step(i):
                    if i.within(0, NB - 1):
                        act.wait_ge(ac_t, 2 * i.val + 1)
                        wait(act, z_t, 5 * i.val)
                        nc.scalar.activation(xh_a[:, 0, :], tp[0][:, :], ACT.Copy).then_inc(hi_ok, 1)
                        act.wait_ge(ac_t, 2 * i.val + 2)
                        nc.scalar.activation(x_c[:, 0, :], tp[1][:, :], ACT.Copy).then_inc(hi_ok, 1)
                    if i.within(1, NB):
                        act.wait_ge(z_a, 5 * i.val)
                        for ct in range(QK):
                            wait(act, dw_l[ct], n_dve * (i.val - 1))
                        wait(act, dw_t, QK * (i.val - 1))
                        nc.scalar.activation(zwin[i.par][:, :, 0:2, 1:W + 1], zwin[1 - i.par][:, :, 4:6, 1:W + 1],
                                             ACT.Copy).then_inc(carry, 1)
                    n = i - 2
                    if n.within(0, NB):
                        lo, hi = slots(n)
                        for ct in range(QK):
                            act.wait_ge(qs_ok, QK * n.val + ct + 1)
                            wait(act, sq_ok, QK * n.val + ct)
                            nc.scalar.activation(junk[:, lo * W:hi * W], qs[:, n.par, ct, lo:hi, :].rearrange("p r w -> p (r w)"),
                                                 ACT.Square, accum_out=nrm[:, ct, bass.ds(n.val, 1)]).then_inc(sq_ok, 1)
                        copy_q(n, 0)
                        copy_q(n, 1)
                    b = i + 2
                    if b.within(0, NB - 1):
                        for k in (0, 1):
                            act.wait_ge(xt_t, b.val + 1)
                            if k == 0:
                                wait(act, st_xt[b.par], 16 * b.half)
                                wait(act, tn_ok, b.val - 1)
                            nc.scalar.activation(xtok[:, b.par, 2 * k:2 * k + 2, :],
                                                 tp[k][:, 0:2 * C].rearrange("p (r c) -> p r c", c=C),
                                                 ACT.Copy).then_inc(xt_a, 1)
                    if n.within(0, NB):
                        copy_q(n, 2)
                        copy_q(n, 3)
                    if i.within(0, NB - 1):
                        for ct in range(2):
                            copy_z(i, ct)
                    if (i + 1).within(0, NB - 1):
                        act.wait_ge(tn_ok, (i + 1).val + 1)
                        nc.scalar.activation(tn[:, :, C:256], tn[:, :, CA:C], ACT.Copy).then_inc(tn_dup, 1)
                    if i.within(0, NB - 1):
                        for ct in range(2, 5):
                            copy_z(i, ct)

                steps(act, step, FIRST, LAST, LO, HI)
                k = NCH // 2
                for n in range(4):
                    act.wait_ge(ld_e, 32 * n + 32)
                    if n < 2:
                        src, dst = stage[:, :], (w1_ah, w1_ch)[n][:, :]
                    else:
                        src = stage[:, 0:k * C].rearrange("p (m d) -> p m d", d=C)
                        dst = w2_hl[:, (n - 2) * k:(n - 1) * k, 0:C]
                    nc.scalar.activation(dst, src, ACT.Copy).then_inc(e_hi, 1)
                act.wait_ge(at_t, 1)
                nc.scalar.activation(rn_row[:, :], db[0][0:QK, 0:128], ACT.Copy).then_inc(at_a, 1)
                act.wait_ge(at_t, 2)
                nc.scalar.activation(rb[:, :], db[1][0:G2, 0:2 * C], ACT.Copy).then_inc(at_a, 1)
                act.wait_ge(at_v, 12)
                for g in (0, 1):
                    nc.scalar.activation(attn[:, 2, g, :], attn[:, 1, g, :], ACT.Exp, bias=acol[:, 2, g:g + 1],
                                         accum_out=acol[:, 3, g:g + 1]).then_inc(at_a, 1)
                act.wait_ge(at_t, 3)
                nc.scalar.activation(mt[:, :, :], db[0][0:G2, 0:2 * C].rearrange("p (g o) -> p g o", g=2), ACT.Copy)\
                    .then_inc(at_a, 1)

            @blk.vector
            def _(dve):
                dve.wait_ge(ld_w, 16 * N_LD_W)
                n_v = [0]

                def link(ins):
                    n_v[0] += 1
                    ins.then_inc(su_v, 1)
                    dve.wait_ge(su_v, n_v[0])

                for ct, (o, m) in enumerate(ZT):
                    nc.vector.tensor_tensor(wp[0:m, ct, 0:C], wn[0:m, ct, :], lnw_bb[0:m, :], ALU.mult)
                    nc.vector.tensor_tensor(wp[0:m, ct, C:256], wn[0:m, ct, CA:C], lnw_bb[0:m, CA:C], ALU.mult)
                    link(nc.vector.tensor_tensor(wtmp[0:m, :], wn[0:m, ct, :], lnb_bb[0:m, :], ALU.mult))
                    link(nc.vector.reduce_sum(bz[0:m, ct:ct + 1], wtmp[0:m, :], AX))
                dve.wait_ge(su_a, 2)
                link(nc.vector.tensor_tensor(gate_r[:, 1, 0:E], gate_raw[:, 0, :], gate_r[:, 0, 0:E].bitcast(FP32), ALU.subtract))
                link(nc.vector.tensor_tensor(gate_r[:, 3, 0:E], gate_raw[:, 1, :], gate_r[:, 2, 0:E].bitcast(FP32), ALU.subtract))
                dve.wait_ge(const, 9)
                for ct in range(QK):
                    for k, tap in enumerate(PE_TAPS):
                        link(nc.vector.tensor_scalar(diag[:, ct, k, :], ident[:, :], wdw[:, ct, tap:tap + 1], None, ALU.mult))
                for ct, (o, m) in enumerate(ZT):
                    dve.wait_ge(su_a, 2 * ct + 4)
                    link(nc.vector.tensor_tensor(wq_al[:, o:o + m], zb[ct % 2][:, 0:m], wq_ah[:, o:o + m].bitcast(FP32), ALU.subtract))
                    link(nc.vector.tensor_tensor(wq_cl[:, o:o + m], zb[ct % 2][:, 128:128 + m], wq_ch[:, o:o + m].bitcast(FP32), ALU.subtract))

                def window_ready(n):
                    if n.within(0, NB - 1):
                        dve.wait_ge(z_a, 5 * n.val + QK)
                    wait(dve, carry, n.val)
                    if n.static and n.val == NB:
                        dve.wait_ge(row_z, 1)

                def tap(n, ct, k):
                    lo, hi = slots(n)
                    ky, kx = divmod(DVE_TAPS[k], KX)
                    a = acc[:, ct, lo:hi, :]
                    if k == 0:
                        wait(dve, qs_ok, QK * (n.val - 1) + ct + 1)
                        dve.wait_ge(dw_t, QK * n.val + ct + 1)
                        before = db[(n.par + ct) % 2][:, lo * W:hi * W].rearrange("p (r w) -> p r w", w=W)
                    else:
                        dve.wait_ge(dw_l[ct], n_dve * n.val + k)
                        before = a
                    nc.vector.scalar_tensor_tensor(
                        out=a, in0=zwin[n.par][:, ct, ky + lo:ky + hi, kx:kx + W],
                        scalar=wdw[:, ct, DVE_TAPS[k]:DVE_TAPS[k] + 1], in1=before, op0=ALU.mult, op1=ALU.add).then_inc(dw_l[ct], 1)

                def step(i):
                    if i.within(0, NB - 1):
                        dve.wait_ge(hi_ok, 2 * i.val + 1)
                        nc.vector.tensor_tensor(xl_a[:, 0, :], tp[0][:, :], xh_a[:, 0, :].bitcast(FP32), ALU.subtract).then_inc(lo_ok, 1)
                        dve.wait_ge(hi_ok, 2 * i.val + 2)
                        nc.vector.tensor_tensor(x_c[CB:128, 0, :], tp[1][CB:128, :], x_c[CB:128, 0, :].bitcast(FP32), ALU.subtract)\
                            .then_inc(lo_ok, 1)
                    n = i - 1
                    if n.within(0, NB):
                        window_ready(n)
                        tap(n, 0, 0)
                        for k in range(n_dve):
                            if k + 1 < n_dve:
                                tap(n, 0, k + 1)
                            tap(n, 1, k)
                    b = i + 1
                    if b.within(0, NB - 1):
                        wait(dve, ac_t, 2 * b.val)
                        dve.wait_ge(r_ok, 2 * b.val + 2)
                        for t in range(ROWS):
                            last = nc.vector.tensor_scalar(tn[:, t, 0:C], xtok[:, b.par, t, :], mv[:, b.par, t, 0:1],
                                                           rstd[:, b.par, t:t + 1], ALU.subtract, ALU.mult)
                        last.then_inc(tn_ok, 1)
                    b = i + 2
                    if n.within(0, NB):
                        tap(n, 2, 0)
                    if b.within(0, NB - 1):
                        dve.wait_ge(xt_a, 2 * b.val + 2)
                        wait(dve, r_ok, 2 * b.val - 2)
                    for t in range(ROWS):
                        if b.within(0, NB - 1):
                            last = nc.vector.bn_stats(stat[:, b.par, t, :], xtok[:, b.par, t, :])
                            if t == ROWS - 1:
                                last.then_inc(su_v, 1)
                        if n.within(0, NB):
                            tap(n, 2, t + 1)
                    if b.within(0, NB - 1):
                        dve.wait_ge(su_v, n_v[0] + b.val + 1)
                        nc.vector.memset(pause[:, 0:1], 0.0)
                        for t in range(ROWS):
                            last = nc.vector.bn_aggr(mv[:, b.par, t, :], stat[:, b.par, t, :])
                        last.then_inc(stats, 1)
                    if n.within(0, NB):
                        for k in range(ROWS + 1, n_dve):
                            tap(n, 2, k)

                steps(dve, step, FIRST, LAST, LO, HI)
                k = NCH // 2
                for n in range(4):
                    dve.wait_ge(e_hi, n + 1)
                    if n < 2:
                        src, hi, dst = stage[:, :], (w1_ah, w1_ch)[n][:, :], (w1_al, w1_cl)[n][:, :]
                    else:
                        src = stage[:, 0:k * C].rearrange("p (m d) -> p m d", d=C)
                        hi, dst = (w2_hl[:, (n - 2) * k:(n - 1) * k, o:o + C] for o in (0, C))
                    nc.vector.tensor_tensor(dst, src, hi.bitcast(FP32), ALU.subtract).then_inc(e_lo, 1)
                dve.wait_ge(sq_ok, QK * (NB + 1))
                nc.vector.reduce_sum(n2[:, 0, :], nrm[:, :, :], AX).then_inc(at_v, 1)
                dve.wait_ge(at_p, 2)
                nc.vector.tensor_scalar(n2[:, 3, :], n2[:, 2, :], EPS_NORM, None, ALU.max).then_inc(at_v, 1)
                dve.wait_ge(at_v, 2)
                nc.vector.reciprocal(n2[:, 1, :], n2[:, 3, :]).then_inc(at_v, 1)
                dve.wait_ge(at_a, 2)
                for g in (0, 1):
                    nc.vector.tensor_tensor(attn[:, 0, g, :], rb[:, G2 * g:G2 * g + G2], ident[0:G2, 0:G2], ALU.mult).then_inc(at_v, 1)
                dve.wait_ge(at_v, 5)
                nc.vector.reduce_sum(acol[:, 0, :], attn[:, 0, :, :], AX).then_inc(at_v, 1)
                dve.wait_ge(at_v, 6)
                nc.vector.tensor_tensor(acol[:, 1, :], acol[:, 0, :], temp[:, :], ALU.mult).then_inc(at_v, 1)
                dve.wait_ge(at_v, 7)
                dve.wait_ge(gr_t, H)
                dve.wait_ge(const, 14)
                for g in (0, 1):
                    nc.vector.scalar_tensor_tensor(out=attn[:, 0, g, :], in0=gb[0:G2, G2 * g:G2 * g + G2], scalar=acol[:, 1, g:g + 1],
                                                   in1=rb[:, C + G2 * g:C + G2 * g + G2], op0=ALU.mult, op1=ALU.mult).then_inc(at_v, 1)
                dve.wait_ge(at_v, 9)
                nc.vector.tensor_tensor(attn[:, 1, :, :].rearrange("p g c -> p (g c)"), attn[:, 0, :, :].rearrange("p g c -> p (g c)"),
                                        mask[:, :, :, :].rearrange("p g h c -> p (g h c)"), ALU.add).then_inc(at_v, 1)
                dve.wait_ge(at_v, 10)
                nc.vector.tensor_reduce(out=acol[:, 4, :], in_=attn[:, 1, :, :], axis=AX, op=ALU.max).then_inc(at_v, 1)
                dve.wait_ge(at_v, 11)
                nc.vector.tensor_scalar(acol[:, 2, :], acol[:, 4, :], -1.0, None, ALU.mult).then_inc(at_v, 1)
                dve.wait_ge(at_a, 4)
                nc.vector.reciprocal(acol[:, 5, :], acol[:, 3, :]).then_inc(at_v, 1)
                dve.wait_ge(at_v, 13)
                for g in (0, 1):
                    nc.vector.tensor_scalar(attn[:, 3, g, :], attn[:, 2, g, :], acol[:, 5, g:g + 1], None, ALU.mult).then_inc(at_v, 1)

            @blk.tensor
            def _(pe):
                pe.wait_ge(const, 9)
                for ct, (o, m) in enumerate(ZT):
                    pe.wait_ge(su_v, 2 * ct + 2)
                    if ct >= 2:
                        pe.wait_ge(su_v, 10 + 2 + QK * len(PE_TAPS) + 2 * (ct - 1))
                    nc.tensor.transpose(zb[ct % 2][:, 0:m], wp[0:m, ct, 0:CA], ident[0:m, 0:m]).then_inc(su_t, 1)
                    nc.tensor.transpose(zb[ct % 2][:, 128:128 + m], wp[0:m, ct, CA:256], ident[0:m, 0:m]).then_inc(su_t, 1)
                nc.tensor.transpose(db[0][:, 0:128], s_rows[:, :], ident[:, :]).then_inc(su_t, 1)
                for g in (0, 1):
                    nc.tensor.transpose(db[1][0:G2, g * C:g * C + CA], wpr[:, 0, G2 * g:G2 * g + G2], ident[:, :])
                    last = nc.tensor.transpose(db[1][0:G2, g * C + CA:g * C + C], wpr[0:CB, 1, G2 * g:G2 * g + G2], ident[0:CB, 0:CB])
                last.then_inc(su_t, 1)
                n_su_v = 10 + 2 + QK * len(PE_TAPS) + 10
                pe.wait_ge(su_v, n_su_v)
                pe.wait_ge(su_a, 14)

                def dw(n, ct):
                    lo, hi = slots(n)
                    if ct == 0:
                        if n.within(0, NB - 1):
                            pe.wait_ge(z_a, 5 * n.val + QK)
                        wait(pe, carry, n.val)
                        if n.static and n.val == NB:
                            pe.wait_ge(row_z, 1)
                    if ct == 2 or not (n.static and n.val == 0):
                        last_n, last_ct = (n, 0) if ct == 2 else (n - 1, ct + 1)
                        pe.wait_ge(dw_l[last_ct], n_dve * last_n.val + 1)
                    for k, tap in enumerate(PE_TAPS):
                        ky, kx = divmod(tap, KX)
                        last = nc.tensor.matmul(db[(n.par + ct) % 2][:, lo * W:hi * W].rearrange("p (r w) -> p r w", w=W),
                                                diag[:, ct, k, :], zwin[n.par][:, ct, ky + lo:ky + hi, kx:kx + W],
                                                start=(k == 0), stop=(k == len(PE_TAPS) - 1))
                    last.then_inc(dw_t, 1)

                def tile_no(n, t):
                    return ROWS * n.val - 1 + t

                def q_tr(n, t):
                    lo, hi = slots(n)
                    if lo <= t < hi:
                        c = tile_no(n, t)
                        if t == lo:
                            pe.wait_ge(qs_ok, QK * n.val + QK)
                        wait(pe, q_a, c)
                        for ct in range(QK):
                            last = nc.tensor.transpose(qb[:, ct * 128:ct * 128 + 128], qs[:, n.par, ct, t, :], ident[:, :])
                        last.then_inc(q_t, 1)

                def gram(n, t):
                    lo, hi = slots(n)
                    if lo <= t < hi:
                        c = tile_no(n, t)
                        pe.wait_ge(q_a, c + 1)
                        first = n.static and n.val == 0 and t == lo
                        final = n.static and n.val == NB
                        for g in (0, 1):
                            last = nc.tensor.matmul(gb[0:G2, g * G2:g * G2 + G2], qk_tok[:, t % 2, G2 * g:G2 * g + G2],
                                                    qk_tok[:, t % 2, C + G2 * g:C + G2 * g + G2],
                                                    start=(first and g == 0), stop=final, skip_group_check=True)
                        last.then_inc(gr_t, 1)

                def z(i, ct):
                    o, m = ZT[ct]
                    c = 5 * i.val + ct
                    if ct == 0:
                        pe.wait_ge(lo_ok, 2 * i.val + 2)
                    wait(pe, z_a, c - 1)
                    dst = zb[(i.par + ct) % 2][0:m, :]
                    ops = [(wq_ah, xh_a), (wq_al, xh_a), (wq_ah, xl_a), (wq_ch, x_c), (wq_cl, x_c)]
                    for k, (w, v) in enumerate(ops):
                        last = nc.tensor.matmul(dst, w[:, o:o + m], v[:, 0, :], start=(k == 0), stop=(k == 4))
                    last.then_inc(z_t, 1)

                def step(i):
                    if i.within(0, NB - 1):
                        pe.wait_ge(tn_dup, i.val + 1)
                        wait(pe, xt_a, 2 * min(i.val + 2, NB) if i.static else 2 * i.val + 4)
                        for h in (0, 1):
                            for t in range(ROWS):
                                last = nc.tensor.transpose(tp[h][:, t * 128:t * 128 + 128], tn[:, t, h * 128:h * 128 + 128], ident[:, :])
                            last.then_inc(ac_t, 1)
                    n, m = i - 1, i - 2
                    has_n, has_m = n.within(0, NB), m.within(0, NB)
                    if has_n:
                        dw(n, 0)
                    if has_m:
                        q_tr(m, 0)
                    if has_n:
                        dw(n, 1)
                    if has_m:
                        q_tr(m, 1)
                        gram(m, 0)
                    b = i + 2
                    if b.within(0, NB - 1):
                        pe.wait_ge(ld_x[b.par], 32 * b.half + 32)
                        if i.static:
                            wait(pe, lo_ok, 2 * i.val + 2)
                            wait(pe, xt_a, 2 * b.val)
                        else:
                            pe.wait_ge(lo_ok, 2 * i.val + 2)
                        for t in range(ROWS):
                            cols = slice(t * 128, t * 128 + 128)
                            o = t % 2 * C
                            nc.tensor.transpose(tp[t // 2][:, o:o + CA], xc_a[:, b.par, cols], ident[:, :])
                            last = nc.tensor.transpose(tp[t // 2][:, o + CA:o + C], xc_b[:, b.par, cols], ident[0:CB, 0:CB])
                        last.then_inc(xt_t, 1)
                    if has_m:
                        q_tr(m, 2)
                        gram(m, 1)
                    if has_n:
                        dw(n, 2)
                    if has_m:
                        q_tr(m, 3)
                        gram(m, 2)
                    if i.within(0, NB - 1):
                        z(i, 0)
                    if has_m:
                        gram(m, 3)
                    if i.within(0, NB - 1):
                        for ct in range(1, 5):
                            z(i, ct)

                steps(pe, step, FIRST, LAST, LO, HI)
                pe.wait_ge(at_v, 3)
                nc.tensor.transpose(db[0][0:QK, 0:128], n2[:, 1, :], ident[:, :]).then_inc(at_t, 1)
                pe.wait_ge(at_a, 1)
                pe.wait_ge(const, 13)
                for ct in range(QK):
                    last = nc.tensor.matmul(db[1][0:G2, ct * 128:ct * 128 + 128], sel[:, ct, :], rn_row[:, :], start=True, stop=True)
                last.then_inc(at_t, 1)
                pe.wait_ge(at_v, 15)
                for g in (0, 1):
                    last = nc.tensor.matmul(db[0][0:G2, g * C:g * C + C], attn[:, 3, g, :], wpt[:, g, :], start=True, stop=True)
                last.then_inc(at_t, 1)

        p2 = ExitStack()
        with p2:
            vwin = sb(p2, "vwin", [G2, 2, 2, 6, W + 2])
            vd = sb(p2, "vd", [G2, 2, ROWS, W])
            y_acc = sb(p2, "y_acc", [128, 2, ROWS, 2 * C])
            hf = sb(p2, "hf", [128, 3, TOK])
            hh = sb(p2, "hh", [128, 3, TOK], F32R)
            hl = sb(p2, "hl", [128, 3, TOK], F32R)
            fin = sb(p2, "fin", [128, ROWS, C])
            fin_a = sb(p2, "fin_a", [CA, TOK])
            fin_b = sb(p2, "fin_b", [CB, TOK])
            sc = sb(p2, "sc", [128, 8, ROWS, E])
            cmp_ = sb(p2, "cmp", [128, 4, ROWS, E, E])
            col = sb(p2, "col", [128, 6, ROWS])
            tri = sb(p2, "tri", [128, ROWS, E, E])
            e_base = sb(p2, "e_base", [128, ROWS, E])
            gm = sb(p2, "gm", [128, 2, ROWS, E])
            gmt = sb(p2, "gmt", [E, TOK])
            sc_row = sb(p2, "sc_row", [E, TOK])

            lb = banks[0:2]
            yb = banks[2:6]
            mb = banks[6:8]

            c2 = sem("c2")
            ld_xt = [sem("ld_xt0"), sem("ld_xt1")]
            ld_v = [sem("ld_v0"), sem("ld_v1")]
            st_out = sem("st_out")
            vd_l, vd_ok = sem("vd_l"), sem("vd_ok")
            co_t = sem("co_t")
            x1_ok, bn_l, mv2, r2_l, r2_ok, tn2, tn2_dup, ac2 = (sem(s) for s in ("x1_ok", "bn_l", "mv2", "r2_l", "r2_ok", "tn2", "tn2_dup", "ac2"))
            hi2, lo2, g_t, g_a, g_v, g_p, g_l, gm_ok = (sem(s) for s in ("hi2", "lo2", "g_t", "g_a", "g_v", "g_p", "g_l", "gm_ok"))
            gt_t, gt_a, b2_t, b2_a = (sem(s) for s in ("gt_t", "gt_a", "b2_t", "b2_a"))
            l1, gelu, hh_ok, hl_ok, y_t, y_v = (sem(s) for s in ("l1", "gelu", "hh_ok", "hl_ok", "y_t", "y_v"))
            fin_ok, ot_t, ot_a = sem("fin_ok"), sem("ot_t"), sem("ot_a")

            FIRST2, LAST2, LO2, HI2 = -1, NB, 1, NB - 4
            GATE_AT = {2: 4, 3: 5}
            TAPS_AT = {0: 1, 3: 1, 4: 2, 5: 2, 6: 1, 8: 1, 9: 2, 10: 2, 11: 2, 12: 1, 14: 2, 15: 1}
            assert sum(TAPS_AT.values()) == 18
            PROJ_AT, X1_AT, TN_AT, AC_AT, HI_AT, LO_AT, SCORE_AT, SCORE_TR_AT, GATE1_AT = 16, 16, 18, 19, 19, 20, 21, 22, 23
            GT_AT, B2_AT, B2C_AT, OUT_AT, OUTC_AT = 4, 5, 6, 8, 9
            GATE_V, GATE_L = 3, 10

            def second_done(s, k, t=None):
                e, m = divmod(k, CH)
                done = (E * s.val + e) * (CH - 1 + ROWS) + m + 1
                return done + (ROWS - 1 if t is None else t) if m == CH - 1 else done

            def buffer_free(eng, i, k):
                old = (i, k - 3) if k >= 3 else (i - 1, k - 3 + NCH)
                if old[0].within(0, NB - 1):
                    eng.wait_ge(y_t, second_done(*old))

            blk = p2.enter_context(nc.Block())

            @blk.sync
            def _(sp):
                def load(b):
                    if not b.within(0, NB - 1):
                        return
                    wait(sp, x1_ok, ROWS * (b.val - 1))
                    sp.dma_start(xtok[:, b.par, :, :], xtok_dram[bass.ds(b.val * ROWS, ROWS), :, :].rearrange("r p c -> p r c"))\
                        .then_inc(ld_xt[b.par], 16)
                    for g in (0, 1):
                        sp.dma_start(vwin[:, b.par, g, :, 1:W + 1], v_view[:, g, bass.ds(b.val * ROWS, 6), :]).then_inc(ld_v[b.par], 16)

                def step(i):
                    load(i + 2)
                    b = i - 1
                    if b.within(0, NB - 1):
                        cols = bass.ds(b.val * TOK, TOK)
                        sp.wait_ge(ot_a, 2 * b.val + 1)
                        sp.dma_start(out_view[0:CA, cols], fin_a[:, :]).then_inc(st_out, 16)
                        sp.wait_ge(ot_a, 2 * b.val + 2)
                        sp.dma_start(out_view[CA:C, cols], fin_b[:, :]).then_inc(st_out, 16)

                sp.wait_ge(c2, 1)
                load(Step(0, 0))
                steps(sp, step, FIRST2, LAST2, LO2, HI2)
                sp.wait_ge(st_out, 32 * NB)

            @blk.gpsimd
            def _(pool):
                nc.gpsimd.memset(vwin[:, :, :, :, :], 0.0).then_inc(c2, 1)
                nc.gpsimd.memset(tri[:, :, :, :], 1.0).then_inc(c2, 1)
                nc.gpsimd.memset(e_base[:, :, :], E_BASE).then_inc(c2, 1)
                pool.wait_ge(c2, 3)
                nc.gpsimd.affine_select(out=tri[:, :, :, :], in_=tri[:, :, :, :], compare_op=ALU.is_gt, fill=0.0,
                                        base=0, pattern=[[0, ROWS], [1, E], [-1, E]], channel_multiplier=0).then_inc(c2, 1)

                def step(i):
                    b = i - 1
                    if b.within(0, NB - 1):
                        pool.wait_ge(y_v, 4 * E * b.val + 4 * E)
                        wait(pool, ot_t, 2 * b.val)
                        nc.gpsimd.tensor_tensor(fin[:, :, :], y_acc[:, b.par, :, 0:C], y_acc[:, b.par, :, C:2 * C], ALU.add)\
                            .then_inc(fin_ok, 1)
                    b = i + 1
                    if b.within(0, NB - 1):
                        pool.wait_ge(mv2, b.val + 1)
                        nc.gpsimd.tensor_tensor(small[:, 4, :], mv[:, 0, :, 1], pw[:, 2, :], ALU.add).then_inc(r2_l, 1)
                        pool.wait_ge(r2_l, b.val + 1)
                        nc.gpsimd.tensor_tensor(rstd[:, 0, :], small[:, 4, :], pw[:, 0, :], ALU.pow).then_inc(r2_ok, 1)
                        pool.wait_ge(g_v, GATE_V * b.val + 3)
                        nc.gpsimd.tensor_tensor(sc[:, 2, :, :], e_base[:, :, :], sc[:, 1, :, :], ALU.pow).then_inc(g_p, 1)

                steps(pool, step, FIRST2, LAST2, LO2, HI2)

            @blk.scalar
            def _(act):
                def chunk(i, k):
                    c = NCH * i.val + k
                    act.wait_ge(l1, c + 1)
                    wait(act, hl_ok, c - 2)
                    nc.scalar.activation(hf[:, k % 3, :], lb[k % 2][:, :], ACT.Gelu, bias=b1_col[:, k:k + 1]).then_inc(gelu, 1)
                    act.wait_ge(gelu, c + 1)
                    buffer_free(act, i, k)
                    nc.scalar.activation(hh[:, k % 3, :], hf[:, k % 3, :], ACT.Copy).then_inc(hh_ok, 1)

                def step(i):
                    cur, nxt, old = i.within(0, NB - 1), (i + 1).within(0, NB - 1), (i - 1).within(0, NB - 1)
                    for k in range(NCH):
                        if cur:
                            chunk(i, k)
                        if k == GT_AT and cur:
                            act.wait_ge(gt_t, i.val + 1)
                            wait(act, b2_t, 2 * i.val)
                            nc.scalar.activation(gmt[:, :], mb[0][0:E, :], ACT.Copy).then_inc(gt_a, 1)
                        if k == B2C_AT and cur:
                            for h in (0, 1):
                                act.wait_ge(b2_t, 2 * i.val + h + 1)
                                wait(act, fin_ok, i.val - 1)
                                nc.scalar.activation(y_acc[:, i.par, 2 * h:2 * h + 2, C:2 * C],
                                                     mb[h][:, 0:2 * C].rearrange("p (t c) -> p t c", c=C), ACT.Copy).then_inc(b2_a, 1)
                        if k == OUTC_AT and old:
                            b = i - 1
                            act.wait_ge(ot_t, 2 * b.val + 1)
                            wait(act, st_out, 32 * b.val)
                            nc.scalar.activation(fin_a[:, :], mb[0][:, :], ACT.Copy).then_inc(ot_a, 1)
                            act.wait_ge(ot_t, 2 * b.val + 2)
                            nc.scalar.activation(fin_b[:, :], mb[1][0:CB, :], ACT.Copy).then_inc(ot_a, 1)
                        if k == TN_AT and nxt:
                            act.wait_ge(tn2, i.val + 2)
                            nc.scalar.activation(tn[:, :, C:256], tn[:, :, CA:C], ACT.Copy).then_inc(tn2_dup, 1)
                        if k == SCORE_AT and nxt:
                            act.wait_ge(g_t, 2 * (i + 1).val + 1)
                            nc.scalar.activation(sc_row[:, :], mb[0][0:E, :], ACT.Copy).then_inc(g_a, 1)
                        if k == HI_AT and nxt:
                            b = i + 1
                            act.wait_ge(ac2, 2 * b.val + 1)
                            wait(act, l1, NCH * (b.val - 1))
                            nc.scalar.activation(xh_a[:, b.par, :], mb[0][:, :], ACT.Copy).then_inc(hi2, 1)
                            act.wait_ge(ac2, 2 * b.val + 2)
                            nc.scalar.activation(x_c[:, b.par, :], mb[1][:, :], ACT.Copy).then_inc(hi2, 1)

                steps(act, step, FIRST2, LAST2, LO2, HI2)

            @blk.vector
            def _(dve):
                def tap(b, n):
                    g, k = divmod(n, 9)
                    ky, kx = divmod(k, KX)
                    src = vwin[:, b.par, g, ky:ky + ROWS, kx:kx + W]
                    if n == 0:
                        dve.wait_ge(ld_v[b.par], 32 * b.half + 32)
                        wait(dve, co_t, 2 * b.val)
                    if k == 0:
                        ins = nc.vector.tensor_scalar(vd[:, g, :, :], src, wdw_v[:, g, 0:1], None, ALU.mult)
                    else:
                        dve.wait_ge(vd_l, 18 * b.val + n)
                        ins = nc.vector.scalar_tensor_tensor(out=vd[:, g, :, :], in0=src, scalar=wdw_v[:, g, k:k + 1],
                                                             in1=vd[:, g, :, :], op0=ALU.mult, op1=ALU.add)
                    ins.then_inc(vd_l, 1)

                def expert_sum(s, e):
                    ex = E * s.val + e
                    if e == 0:
                        dve.wait_ge(gm_ok, s.val + 1)
                        dve.wait_ge(b2_a, 2 * s.val + 2)
                        dve.wait_ge(x1_ok, ROWS * s.val + ROWS)
                    else:
                        dve.wait_ge(y_v, 4 * ex)
                    for t in range(ROWS):
                        dve.wait_ge(y_t, second_done(s, CH * e + CH - 1, t))
                        nc.vector.scalar_tensor_tensor(out=y_acc[:, s.par, t, :], in0=yb[t][:, 0:2 * C], scalar=gm[:, s.par, t, e:e + 1],
                                                       in1=y_acc[:, s.par, t, :], op0=ALU.mult, op1=ALU.add).then_inc(y_v, 1)

                def gate_1(b):
                    base = GATE_V * b.val
                    dve.wait_ge(g_t, 2 * b.val + 2)
                    nc.vector.tensor_tensor(sc[:, 0, :, :], mb[1][:, 0:ROWS * E].rearrange("p (t e) -> p t e", e=E),
                                            gate_bb[:, None, :].to_broadcast([128, ROWS, E]), ALU.add).then_inc(g_v, 1)
                    dve.wait_ge(g_v, base + 1)
                    nc.vector.tensor_reduce(out=col[:, 0, :], in_=sc[:, 0, :, :], axis=AX, op=ALU.max).then_inc(g_v, 1)
                    dve.wait_ge(g_v, base + 2)
                    wait(dve, gm_ok, b.val)
                    nc.vector.tensor_tensor(sc[:, 1, :, :], sc[:, 0, :, :], col[:, 0, :, None].to_broadcast([128, ROWS, E]),
                                            ALU.subtract).then_inc(g_v, 1)

                def gate_2(b):
                    p = sc[:, 2, :, :]
                    other = p[:, :, None, :].to_broadcast([128, ROWS, E, E])
                    own = p[:, :, :, None].to_broadcast([128, ROWS, E, E])
                    dve.wait_ge(g_p, b.val + 1)
                    nc.vector.tensor_tensor(cmp_[:, 0], other, own, ALU.is_gt).then_inc(g_l, 1)
                    nc.vector.tensor_tensor(cmp_[:, 1], other, own, ALU.is_equal).then_inc(g_l, 1)
                    nc.vector.reduce_sum(col[:, 1, :], p, AX).then_inc(g_l, 1)
                    yield
                    dve.wait_ge(g_l, GATE_L * b.val + 2)
                    nc.vector.tensor_tensor(cmp_[:, 2], cmp_[:, 1], tri[:, :, :, :], ALU.mult).then_inc(g_l, 1)
                    yield
                    dve.wait_ge(g_l, GATE_L * b.val + 4)
                    nc.vector.tensor_tensor(cmp_[:, 3], cmp_[:, 2], cmp_[:, 0], ALU.add).then_inc(g_l, 1)
                    yield
                    dve.wait_ge(g_l, GATE_L * b.val + 5)
                    nc.vector.reduce_sum(sc[:, 3, :, :], cmp_[:, 3], AX).then_inc(g_l, 1)
                    yield
                    dve.wait_ge(g_l, GATE_L * b.val + 6)
                    nc.vector.scalar_tensor_tensor(out=sc[:, 4, :, :], in0=sc[:, 3, :, :], scalar=1.5, in1=p,
                                                   op0=ALU.is_lt, op1=ALU.mult).then_inc(g_l, 1)
                    yield
                    dve.wait_ge(g_l, GATE_L * b.val + 7)
                    nc.vector.reduce_sum(col[:, 2, :], sc[:, 4, :, :], AX).then_inc(g_l, 1)
                    yield
                    dve.wait_ge(g_l, GATE_L * b.val + 8)
                    nc.vector.scalar_tensor_tensor(out=col[:, 3, :], in0=col[:, 1, :], scalar=EPS_GATE, in1=col[:, 2, :],
                                                   op0=ALU.mult, op1=ALU.add).then_inc(g_l, 1)
                    yield
                    dve.wait_ge(g_l, GATE_L * b.val + 9)
                    nc.vector.reciprocal(col[:, 4, :], col[:, 3, :]).then_inc(g_l, 1)
                    yield
                    dve.wait_ge(g_l, GATE_L * b.val + 10)
                    wait(dve, y_v, 4 * E * (b.val - 1))
                    nc.vector.tensor_tensor(gm[:, b.par, :, :], sc[:, 4, :, :], col[:, 4, :, None].to_broadcast([128, ROWS, E]),
                                            ALU.mult).then_inc(gm_ok, 1)
                    yield

                def step(i):
                    cur, nxt, old = i.within(0, NB - 1), (i + 1).within(0, NB - 1), (i - 1).within(0, NB - 1)
                    taps = 0
                    gate = gate_2(i)
                    for k in range(NCH):
                        e, m = divmod(k + 1 - LAG, CH)
                        if m == 0 and e > 0 and cur:
                            expert_sum(i, e - 1)
                        if k == LAG - 1 and old:
                            expert_sum(i - 1, E - 1)
                        if cur:
                            c = NCH * i.val + k
                            dve.wait_ge(hh_ok, c + 1)
                            buffer_free(dve, i, k)
                            nc.vector.tensor_tensor(hl[:, k % 3, :], hf[:, k % 3, :], hh[:, k % 3, :].bitcast(FP32), ALU.subtract)\
                                .then_inc(hl_ok, 1)
                        for _ in range(GATE_AT.get(k, 0) if cur else 0):
                            next(gate)
                        b = i + 1
                        if nxt:
                            for _ in range(TAPS_AT.get(k, 0)):
                                tap(b, taps)
                                taps += 1
                            if k == X1_AT:
                                dve.wait_ge(ld_xt[b.par], 16 * b.half + 16)
                                wait(dve, fin_ok, b.val - 1)
                                for t in range(ROWS):
                                    dve.wait_ge(co_t, 2 * b.val + t // 2 + 1)
                                    nc.vector.scalar_tensor_tensor(
                                        out=y_acc[:, b.par, t, 0:C], in0=mb[t // 2][:, t % 2 * C:t % 2 * C + C],
                                        scalar=s_tok[:, bass.ds(b.val * ROWS + t, 1)], in1=xtok[:, b.par, t, :],
                                        op0=ALU.mult, op1=ALU.add).then_inc(x1_ok, 1)
                                dve.wait_ge(x1_ok, ROWS * b.val + ROWS)
                                for t in range(ROWS):
                                    last = nc.vector.bn_stats(stat[:, 0, t, :], y_acc[:, b.par, t, 0:C])
                                last.then_inc(bn_l, 1)
                                dve.wait_ge(bn_l, b.val + 1)
                                nc.vector.memset(pause[:, 1:2], 0.0)
                                for t in range(ROWS):
                                    last = nc.vector.bn_aggr(mv[:, 0, t, :], stat[:, 0, t, :])
                                last.then_inc(mv2, 1)
                            if k == TN_AT:
                                dve.wait_ge(r2_ok, b.val + 1)
                                wait(dve, ac2, 2 * b.val)
                                for t in range(ROWS):
                                    last = nc.vector.tensor_scalar(tn[:, t, 0:C], y_acc[:, b.par, t, 0:C], mv[:, 0, t, 0:1],
                                                                   rstd[:, 0, t:t + 1], ALU.subtract, ALU.mult)
                                last.then_inc(tn2, 1)
                            if k == LO_AT:
                                dve.wait_ge(hi2, 2 * b.val + 2)
                                nc.vector.tensor_tensor(xl_a[:, b.par, :], mb[0][:, :], xh_a[:, b.par, :].bitcast(FP32), ALU.subtract).then_inc(lo2, 1)
                                nc.vector.tensor_tensor(x_c[CB:128, b.par, :], mb[1][CB:128, :], x_c[CB:128, b.par, :].bitcast(FP32), ALU.subtract)\
                                    .then_inc(lo2, 1)
                            if k == GATE1_AT:
                                gate_1(b)

                dve.wait_ge(c2, 4)
                steps(dve, step, FIRST2, LAST2, LO2, HI2)

            @blk.tensor
            def _(pe):
                def first(i, k):
                    c = NCH * i.val + k
                    if k == 0:
                        pe.wait_ge(lo2, 2 * i.val + 2)
                    wait(pe, gelu, c - 1)
                    ops = [(w1_ah, xh_a), (w1_al, xh_a), (w1_ah, xl_a), (w1_ch, x_c), (w1_cl, x_c)]
                    for n, (w, v) in enumerate(ops):
                        last = nc.tensor.matmul(lb[k % 2][:, :], w[:, k * 128:k * 128 + 128], v[:, i.par, :], start=(n == 0), stop=(n == 4))
                    last.then_inc(l1, 1)

                def second(s, k):
                    c = NCH * s.val + k
                    e, m = divmod(k, CH)
                    ex = E * s.val + e
                    pe.wait_ge(hl_ok, c + 1)
                    for t in range(ROWS):
                        if m == 0:
                            wait(pe, y_v, 4 * (ex - 1) + t + 1)
                        cols = slice(t * 128, t * 128 + 128)
                        nc.tensor.matmul(yb[t][:, 0:2 * C], hh[:, k % 3, cols], w2_hl[:, k, :], start=(m == 0), stop=False, skip_group_check=True)
                        last = nc.tensor.matmul(yb[t][:, 0:C], hl[:, k % 3, cols], w2_hl[:, k, 0:C], start=False, stop=(m == CH - 1), skip_group_check=True)
                        if t == ROWS - 1 or m == CH - 1:
                            last.then_inc(y_t, 1)

                def step(i):
                    cur, nxt, old = i.within(0, NB - 1), (i + 1).within(0, NB - 1), (i - 1).within(0, NB - 1)
                    for k in range(NCH):
                        if cur:
                            first(i, k)
                        if k < LAG:
                            if old:
                                second(i - 1, NCH - LAG + k)
                        elif cur:
                            second(i, k - LAG)
                        if cur and k == GT_AT:
                            pe.wait_ge(gm_ok, i.val + 1)
                            for t in range(ROWS):
                                last = nc.tensor.transpose(mb[0][0:E, t * 128:t * 128 + 128], gm[:, i.par, t, :], ident[:, :])
                            last.then_inc(gt_t, 1)
                        if cur and k == B2_AT:
                            pe.wait_ge(gt_a, i.val + 1)
                            for t in range(ROWS):
                                last = nc.tensor.matmul(mb[t // 2][:, t % 2 * C:t % 2 * C + C], gmt[:, t * 128:t * 128 + 128], b2_row[:, :],
                                                        start=True, stop=True)
                                if t % 2:
                                    last.then_inc(b2_t, 1)
                        if old and k == OUT_AT:
                            b = i - 1
                            pe.wait_ge(fin_ok, b.val + 1)
                            if cur:
                                pe.wait_ge(b2_a, 2 * i.val + 2)
                            for t in range(ROWS):
                                last = nc.tensor.transpose(mb[0][:, t * 128:t * 128 + 128], fin[:, t, 0:CA], ident[:, :])
                            last.then_inc(ot_t, 1)
                            for t in range(ROWS):
                                last = nc.tensor.transpose(mb[1][0:CB, t * 128:t * 128 + 128], fin[:, t, CA:C], ident[:, :])
                            last.then_inc(ot_t, 1)
                        if nxt and k == PROJ_AT:
                            b = i + 1
                            pe.wait_ge(vd_l, 18 * b.val + 18)
                            if old:
                                pe.wait_ge(ot_a, 2 * (i - 1).val + 2)
                            elif cur:
                                pe.wait_ge(b2_a, 2 * i.val + 2)
                            for t in range(ROWS):
                                for g in (0, 1):
                                    last = nc.tensor.matmul(mb[t // 2][:, t % 2 * C:t % 2 * C + C], vd[:, g, t, :], mt[:, g, :],
                                                            start=(g == 0), stop=(g == 1))
                                if t % 2:
                                    last.then_inc(co_t, 1)
                        if nxt and k == AC_AT:
                            b = i + 1
                            for h in (0, 1):
                                pe.wait_ge((tn2, tn2_dup)[h], b.val + 1)
                                for t in range(ROWS):
                                    last = nc.tensor.transpose(mb[h][:, t * 128:t * 128 + 128], tn[:, t, h * 128:h * 128 + 128], ident[:, :])
                                last.then_inc(ac2, 1)
                        if nxt and k == SCORE_AT:
                            b = i + 1
                            pe.wait_ge(lo2, 2 * b.val + 2)
                            ops = [(xh_a, 0), (xh_a, 1), (xl_a, 0), (x_c, 2), (x_c, 3)]
                            for n, (v, w) in enumerate(ops):
                                last = nc.tensor.matmul(mb[0][:, :], gate_r[:, w, :], v[:, b.par, :], start=(n == 0), stop=(n == 4))
                            last.then_inc(g_t, 1)
                        if nxt and k == SCORE_TR_AT:
                            b = i + 1
                            pe.wait_ge(g_a, b.val + 1)
                            for t in range(ROWS):
                                last = nc.tensor.matmul(mb[1][:, t * E:t * E + E], sc_row[:, t * 128:t * 128 + 128], ident[0:E, 0:E],
                                                        start=True, stop=True)
                            last.then_inc(g_t, 1)

                steps(pe, step, FIRST2, LAST2, LO2, HI2)
    return nc


_INS = ["x", "L0_conv_spatial_interaction", "L0_conv_ln_w", "L0_conv_ln_b", "L0_conv_w_qkv", "L0_conv_w_dw",
        "L0_conv_w_proj", "L0_conv_temperature", "L0_ffn_gate_w", "L0_ffn_gate_b", "L0_ffn_w1", "L0_ffn_b1",
        "L0_ffn_w2", "L0_ffn_b2"]


def kernel(**inputs):
    import numpy as _np
    import concourse.bacc as _bacc
    from concourse import mybir as _mybir
    from concourse.bass_utils import run_bass_kernel_spmd as _run

    nc = _bacc.Bacc("TRN2", target_bir_lowering=False, num_devices=1)
    arrays, args = {}, []
    for name in _INS:
        a = _np.ascontiguousarray(inputs[name])
        arrays[f"in_{name}_dram"] = a
        args.append(nc.dram_tensor(f"in_{name}_dram", a.shape, _mybir.dt.from_np(a.dtype), kind="ExternalInput").ap())
    out = nc.dram_tensor("out_0_dram", (1, C, H, W), _mybir.dt.float32, kind="ExternalOutput").ap()
    build(nc, *args, out)
    r = _run(nc, [arrays], core_ids=[0])
    return r.results[0]["out_0_dram"]
```

```python
import concourse.bass as bass
from concourse import mybir
from contextlib import ExitStack

FP32 = mybir.dt.float32
F32R = mybir.dt.float32r
ALU = mybir.AluOpType
ACT = mybir.ActivationFunctionType
AX = mybir.AxisListType.X

C = 192
H = W = 128
ROWS = 4
TOK = ROWS * W
NB = H // ROWS
CA = 128
CB = C - CA
G2 = C // 2
HEADS = 8
HD = C // HEADS
E = 4
HID = 4 * C
CH = HID // 128
NCH = E * CH
LAG = 2
ZT = [(0, 128), (128, 128), (256, 128), (384, G2), (480, G2)]
QK = 3
KX = 3
PE_TAPS = [[0, 1, 2], [0, 1], [0, 1]]
DVE_TAPS = [[3, 4, 5, 6, 7], [2, 3, 4, 5, 6, 7], [2, 3, 4, 5, 6, 7]]
POOL_TAP = 8
HEAD_START = 2
EPS_C, EPS_LN, EPS_NORM, EPS_GATE = 1e-6, 1e-5, 1e-12, 1e-9
NEG = -1e30
E_BASE = 2.718281828459045


class Step:

    def __init__(self, j, c):
        self.j, self.c = j, c

    def __add__(self, n):
        return Step(self.j, self.c + n)

    def __sub__(self, n):
        return Step(self.j, self.c - n)

    @property
    def static(self):
        return isinstance(self.j, int)

    @property
    def val(self):
        return 2 * self.j + self.c

    @property
    def half(self):
        return self.j + self.c // 2

    @property
    def par(self):
        return self.c % 2

    def within(self, lo, hi):
        return not self.static or lo <= self.val <= hi


def wait(eng, sem, value):
    if isinstance(value, int) and value <= 0:
        return
    eng.wait_ge(sem, value)


def steps(eng, emit, first, last, lo, hi, setup=None):
    assert (hi - lo) % 2 == 1
    for n in range(first, lo):
        emit(Step(0, n))
        if setup and n == first:
            setup()
    with eng.Fori(0, (hi - lo + 1) // 2) as j:
        for u in (0, 1):
            emit(Step(j, lo + u))
    for n in range(hi + 1, last + 1):
        emit(Step(0, n))


def build(nc, x, spat, ln_w, ln_b, w_qkv, w_dw, w_proj, temperature, gate_w, gate_b, w1, b1, w2, b2, out):
    top = ExitStack()
    with top:
        def sb(stack, name, shape, dt=FP32):
            return stack.enter_context(nc.sbuf_tensor(name, shape, dt))

        def sem(name):
            return top.enter_context(nc.semaphore(name))

        xtok_dram = nc.dram_tensor("xtok_scratch", (H, W, C), FP32, kind="Internal").ap()
        v_dram = nc.dram_tensor("v_scratch", (C, H + 2, W), FP32, kind="Internal").ap()
        v_view = v_dram.rearrange("(g p) r w -> p g r w", g=2)
        x_view = x.rearrange("a c h w -> (a c) (h w)")
        out_view = out.rearrange("a c h w -> (a c) (h w)")
        s_view = spat.rearrange("a b h w -> (a b h) w")

        ident = sb(top, "ident", [128, 128])
        w1_ah = sb(top, "w1_ah", [CA, NCH * 128], F32R)
        w1_al = sb(top, "w1_al", [CA, NCH * 128], F32R)
        w1_ch = sb(top, "w1_ch", [128, NCH * 128], F32R)
        w1_cl = sb(top, "w1_cl", [128, NCH * 128], F32R)
        w2_hl = sb(top, "w2_hl", [128, NCH, 2 * C], F32R)
        b1_col = sb(top, "b1_col", [128, NCH])
        gate_bb = sb(top, "gate_bb", [128, E])
        wdw_v = sb(top, "wdw_v", [G2, 2, 9])
        s_tok = sb(top, "s_tok", [128, H])
        mt = sb(top, "mt", [G2, 2, C])
        xh_a = sb(top, "xh_a", [CA, 2, TOK], F32R)
        xl_a = sb(top, "xl_a", [CA, 2, TOK], F32R)
        x_c = sb(top, "x_c", [128, 2, TOK], F32R)
        tn = sb(top, "tn", [128, ROWS, 2 * 128])
        xtok = sb(top, "xtok", [128, 2, ROWS, C])
        stat = sb(top, "stat", [128, 2, ROWS, 6])
        mv = sb(top, "mv", [128, 2, ROWS, 2])
        rstd = sb(top, "rstd", [128, 2, ROWS])
        pw = sb(top, "pw", [128, 3, ROWS])
        pause = sb(top, "pause", [128, 2])
        small = sb(top, "small", [128, 6, ROWS])

        banks = [top.enter_context(nc.psum_tensor(f"bank{n}", [128, 512], FP32)) for n in range(8)]

        p1 = ExitStack()
        with p1:
            stage = sb(p1, "stage", [128, NCH * 128])
            wn = stage[:, 0:5 * C].rearrange("p (t c) -> p t c", t=5)
            wp = stage[:, 5 * C:5 * C + 5 * 256].rearrange("p (t c) -> p t c", t=5)
            wtmp = stage[:, 5 * (C + 256):5 * (C + 256) + C]
            lnw_bb = sb(p1, "lnw_bb", [128, C])
            lnb_bb = sb(p1, "lnb_bb", [128, C])
            bz = sb(p1, "bz", [128, 5])
            wq_ah = sb(p1, "wq_ah", [CA, 3 * C], F32R)
            wq_al = sb(p1, "wq_al", [CA, 3 * C], F32R)
            wq_ch = sb(p1, "wq_ch", [128, 3 * C], F32R)
            wq_cl = sb(p1, "wq_cl", [128, 3 * C], F32R)
            wdw = sb(p1, "wdw", [128, QK, 9])
            diag = sb(p1, "diag", [128, QK, max(map(len, PE_TAPS)), 128])
            last_tap = sb(p1, "last_tap", [128, QK, ROWS, W])
            wpr = sb(p1, "wpr", [128, 2, C])
            wpt = sb(p1, "wpt", [G2, 2, C])
            s_rows = sb(p1, "s_rows", [128, W])
            zero = sb(p1, "zero", [G2, 2, 2, W])
            xc_a = sb(p1, "xc_a", [CA, 2, TOK])
            xc_b = sb(p1, "xc_b", [CB, 2, TOK])
            zwin = [sb(p1, f"zwin{p}", [128, QK, 6, W + 2]) for p in (0, 1)]
            zv = sb(p1, "zv", [G2, 2, TOK])
            s_bc = sb(p1, "s_bc", [128, 2, ROWS, W])
            acc = sb(p1, "acc", [128, QK, ROWS, W])
            qs = sb(p1, "qs", [128, 2, QK, ROWS, W])
            junk = xl_a[:, 1, :]
            qk_tok = sb(p1, "qk_tok", [128, 2, 2 * C])
            nrm = sb(p1, "nrm", [128, QK, NB + 1])
            n2 = sb(p1, "n2", [128, 4, QK])
            rn_row = sb(p1, "rn_row", [QK, 128])
            sel = sb(p1, "sel", [QK, QK, G2])
            rb = sb(p1, "rb", [G2, 2 * C])
            temp = sb(p1, "temp", [G2, 2])
            mask = sb(p1, "mask", [G2, 2, E, HD])
            attn = xc_a[0:G2, :, :].rearrange("p a n -> p (a n)")[:, 0:4 * C].rearrange("p (k g c) -> p k g c", k=4, g=2)
            acol = sb(p1, "acol", [G2, 6, 2])

            tp = banks[0:2]
            zb = banks[2:4]
            db = banks[4:6]
            qb = banks[6]
            gb = banks[7]

            ld_q, ld_w = sem("ld_q"), sem("ld_w")
            ld_zero = sem("ld_zero")
            ld_x = [sem("ld_x0"), sem("ld_x1")]
            ld_s = [sem("ld_s0"), sem("ld_s1")]
            st_xt = [sem("st_xt0"), sem("st_xt1")]
            st_v = sem("st_v")
            ld_e = sem("ld_e")
            e_hi, e_lo = sem("e_hi"), sem("e_lo")
            const = sem("const")
            su_v, su_t, su_a = sem("su_v"), sem("su_t"), sem("su_a")
            xt_t, xt_a = sem("xt_t"), sem("xt_a")
            bn_ok = sem("bn_ok")
            stats = sem("stats")
            r_link, r_ok = sem("r_link"), sem("r_ok")
            tn_ok, tn_dup = sem("tn_ok"), sem("tn_dup")
            ac_t = sem("ac_t")
            hi_ok, lo_ok = sem("hi_ok"), sem("lo_ok")
            z_t, z_a = sem("z_t"), sem("z_a")
            carry = sem("carry")
            dw_t, dw_l = sem("dw_t"), [sem(f"dw_l{ct}") for ct in range(QK)]
            lt_a, lt_p = sem("lt_a"), sem("lt_p")
            qs_ok, sq_ok = sem("qs_ok"), sem("sq_ok")
            q_t, q_a, gr_t = sem("q_t"), sem("q_a"), sem("gr_t")
            row_z = sem("row_z")
            at_v, at_t, at_a, at_p = sem("at_v"), sem("at_t"), sem("at_a"), sem("at_p")

            FIRST, LAST, LO, HI = -2, NB + 2, 3, NB - 6

            def slots(n):
                if n.static and n.val == 0:
                    return 1, ROWS
                if n.static and n.val == NB:
                    return 0, 1
                return 0, ROWS

            half = NCH // 2
            stage_w2 = stage[:, 0:half * C].rearrange("p (m d) -> p m d", d=C)
            pieces = [(hi[:, o:o + 512], lo[:, o:o + 512], stage[:, o:o + 512])
                      for hi, lo in ((w1_ah, w1_al), (w1_ch, w1_cl)) for o in range(0, NCH * 128, 512)]
            pieces += [(w2_hl[:, o:o + 3, 0:C], w2_hl[:, o:o + 3, C:2 * C], stage_w2[:, o % half:o % half + 3, :]) for o in range(0, NCH, 3)]
            PIECES_AT = {1: (0, 3), 2: (3, 6), NB - 5: (6, 9), NB - 4: (9, 12), NB - 2: (12, 16), NB: (16, 20)}
            LOAD_AT = {0: 0, 2: 1, NB - 4: 2, NB - 2: 3}
            FIRST_PIECE = (0, 6, 12, 16)

            def pieces_of(i):
                if not i.static or i.val not in PIECES_AT:
                    return []
                return [(n, max(g for g in range(4) if FIRST_PIECE[g] <= n)) for n in range(*PIECES_AT[i.val])]

            n_dve = [len(taps) for taps in DVE_TAPS]
            n_diag = sum(map(len, PE_TAPS))
            blk = p1.enter_context(nc.Block())
            N_LD_Q, N_LD_W = 7, 15

            @blk.sync
            def _(sp):
                def load_x(b):
                    if b.within(0, NB - 1):
                        wait(sp, xt_t, b.val - 1)
                        cols = bass.ds(b.val * TOK, TOK)
                        sp.dma_start(xc_a[:, b.par, :], x_view[0:CA, cols]).then_inc(ld_x[b.par], 16)
                        sp.dma_start(xc_b[:, b.par, :], x_view[CA:C, cols]).then_inc(ld_x[b.par], 16)

                n_w = [0]

                def load_w(dst, src):
                    n_w[0] += 1
                    sp.dma_start(dst, src).then_inc(ld_w, 16)

                def load_q(dst, src):
                    sp.dma_start(dst, src).then_inc(ld_q, 16)

                load_x(Step(0, 0))
                for ct, (o, m) in enumerate(ZT):
                    load_q(wn[0:m, ct, :], w_qkv[o:o + m, :])
                load_q(lnw_bb[:, :], ln_w.rearrange("(a c) -> a c", a=1).to_broadcast([128, C]))
                load_q(lnb_bb[:, :], ln_b.rearrange("(a c) -> a c", a=1).to_broadcast([128, C]))
                load_x(Step(0, 1))
                dw_rows = w_dw.rearrange("o a y x -> o (a y x)")
                load_w(wdw[:, :, :], dw_rows[0:QK * 128, :].rearrange("(t p) k -> p t k", p=128))
                load_w(wdw_v[:, :, :], dw_rows[2 * C:3 * C, :].rearrange("(t p) k -> p t k", p=G2))
                load_w(s_rows[:, :], s_view)
                load_w(wpr[:, 0, :], w_proj[0:CA, :])
                load_w(wpr[0:CB, 1, :], w_proj[CA:C, :])
                load_w(gate_bb[:, :], gate_b.rearrange("(a c) -> a c", a=1).to_broadcast([128, E]))
                for h in range(HEADS):
                    load_w(temp[HD * (h % 4):HD * (h % 4) + HD, h // 4:h // 4 + 1],
                           temperature[h:h + 1, :, 0].to_broadcast([HD, 1]))
                with nc.allow_non_contiguous_dma(reason="24 columns of biases, once"):
                    load_w(b1_col[:, :], b1.rearrange("e (m p) -> p (e m)", p=128))
                assert n_w[0] == N_LD_W, n_w
                sp.wait_ge(const, 7)
                sp.dma_start(v_view[:, :, 0, :], zero[:, 0, :, :]).then_inc(ld_zero, 16)
                sp.dma_start(v_view[:, :, H + 1, :], zero[:, 1, :, :]).then_inc(ld_zero, 16)
                w1_rows = w1.rearrange("e c h -> c e h")
                w2_rows = w2.rearrange("e (m p) d -> p (e m) d", p=128)

                def load_experts(n):
                    wait(sp, e_lo, FIRST_PIECE[n])
                    if n == 0:
                        sp.dma_start(stage[:, :].rearrange("p (e h) -> p e h", e=E), w1_rows[0:CA]).then_inc(ld_e, 32)
                    elif n == 1:
                        for o in (0, CB):
                            sp.dma_start(stage[o:o + CB, :].rearrange("p (e h) -> p e h", e=E), w1_rows[CA:C]).then_inc(ld_e, 16)
                    else:
                        sp.dma_start(stage_w2, w2_rows[:, (n - 2) * half:(n - 1) * half, :]).then_inc(ld_e, 32)

                def step(i):
                    load_x(i + 4)
                    b = i + 2
                    if b.within(0, NB - 1):
                        sp.wait_ge(xt_a, 2 * b.val + 2)
                        sp.dma_start(xtok_dram[bass.ds(b.val * ROWS, ROWS), :, :].rearrange("r p c -> p r c"),
                                     xtok[:, b.par, :, :]).then_inc(st_xt[b.par], 16)
                    n = i + 1
                    if n.within(0, NB):
                        wait(sp, qs_ok, QK * (n.val - 1))
                        lo, hi = slots(n)
                        rows = s_view[bass.ds(n.val * ROWS - 1 + lo, hi - lo), :].rearrange("r w -> (r w)")
                        sp.dma_start(s_bc[:, n.par, lo:hi, :].rearrange("p r w -> p (r w)"),
                                     rows.rearrange("(a n) -> a n", a=1).to_broadcast([128, (hi - lo) * W]))\
                          .then_inc(ld_s[n.par], 16)
                    if i.within(0, NB - 1):
                        sp.wait_ge(z_a, 5 * i.val + 5)
                        sp.dma_start(v_view[:, :, bass.ds(i.val * ROWS + 1, ROWS), :].rearrange("p g r w -> p g (r w)"),
                                     zv[:, :, :]).then_inc(st_v, 16)
                    if i.static and i.val in LOAD_AT:
                        load_experts(LOAD_AT[i.val])

                steps(sp, step, FIRST, LAST, LO, HI)
                sp.wait_ge(ld_zero, 32)
                for p in (0, 1):
                    sp.wait_ge(st_xt[p], 16 * NB // 2)
                sp.wait_ge(st_v, 16 * NB)

            @blk.gpsimd
            def _(pool):
                nc.gpsimd.memset(ident[:, :], 0.0).then_inc(const, 1)
                nc.gpsimd.memset(zero[:, :, :, :], 0.0).then_inc(const, 1)
                nc.gpsimd.memset(zwin[0][:, :, :, :], 0.0).then_inc(const, 1)
                nc.gpsimd.memset(zwin[1][:, :, :, :], 0.0).then_inc(const, 1)
                nc.gpsimd.memset(pw[:, 0, :], -0.5).then_inc(const, 1)
                nc.gpsimd.memset(pw[:, 1, :], EPS_C).then_inc(const, 1)
                nc.gpsimd.memset(pw[:, 2, :], EPS_LN).then_inc(const, 1)
                pool.wait_ge(const, 7)
                nc.gpsimd.affine_select(out=ident[:, :], in_=ident[:, :], compare_op=ALU.not_equal, fill=1.0,
                                        base=0, pattern=[[-1, 128]], channel_multiplier=1).then_inc(const, 1)
                nc.gpsimd.memset(sel[:, :, :], 0.0).then_inc(const, 1)
                nc.gpsimd.memset(mask[:, :, :, :], 0.0).then_inc(const, 1)
                pool.wait_ge(const, 10)
                nc.gpsimd.affine_select(out=sel[:, :, :], in_=sel[:, :, :], compare_op=ALU.not_equal, fill=1.0,
                                        base=0, pattern=[[-1, QK], [0, G2]], channel_multiplier=1).then_inc(const, 1)
                nc.gpsimd.affine_select(out=mask[:, :, :, :], in_=mask[:, :, :, :], compare_op=ALU.is_ge, fill=NEG,
                                        base=0, pattern=[[0, 2], [-HD, E], [0, HD]], channel_multiplier=1).then_inc(const, 1)
                pool.wait_ge(const, 12)
                nc.gpsimd.affine_select(out=mask[:, :, :, :], in_=mask[:, :, :, :], compare_op=ALU.is_ge, fill=NEG,
                                        base=HD - 1, pattern=[[0, 2], [HD, E], [0, HD]], channel_multiplier=-1).then_inc(const, 1)

                links = 5

                def step(i):
                    n = i - 1
                    if n.within(0, NB):
                        lo, hi = slots(n)
                        wait(pool, ld_s[n.par], 16 * n.half + 16)
                        wait(pool, q_t, ROWS * (n.val - 1) - 1)
                        wait(pool, sq_ok, QK * (n.val - 1))
                        for ct in range(QK):
                            pool.wait_ge(dw_l[ct], n_dve[ct] * (n.val + 1))
                            pool.wait_ge(lt_a, QK * n.val + ct + 1)
                            nc.gpsimd.tensor_tensor(last_tap[:, ct, lo:hi, :], acc[:, ct, lo:hi, :], last_tap[:, ct, lo:hi, :],
                                                    ALU.add).then_inc(lt_p, 1)
                            pool.wait_ge(lt_p, QK * n.val + ct + 1)
                            nc.gpsimd.tensor_tensor(qs[:, n.par, ct, lo:hi, :], last_tap[:, ct, lo:hi, :],
                                                    s_bc[:, n.par, lo:hi, :], ALU.mult).then_inc(qs_ok, 1)
                    b = i + 2
                    if b.within(0, NB - 1):
                        var = mv[:, b.par, :, 1]
                        t = [small[:, k, :] for k in range(4)]
                        pool.wait_ge(stats, b.val + 1)
                        base = links * b.val

                        def link(k, ins):
                            ins.then_inc(r_link, 1)
                            pool.wait_ge(r_link, base + k)

                        link(1, nc.gpsimd.tensor_tensor(t[0], var, pw[:, 1, :], ALU.add))
                        link(2, nc.gpsimd.tensor_tensor(t[1], t[0], pw[:, 0, :], ALU.pow))
                        link(3, nc.gpsimd.tensor_tensor(t[2], t[1], t[1], ALU.mult))
                        link(4, nc.gpsimd.tensor_tensor(t[3], t[2], var, ALU.mult))
                        link(5, nc.gpsimd.tensor_tensor(t[0], t[3], pw[:, 2, :], ALU.add))
                        nc.gpsimd.tensor_tensor(t[2], t[0], pw[:, 0, :], ALU.pow).then_inc(r_ok, 1)
                        pool.wait_ge(r_ok, 2 * b.val + 1)
                        if not (b.static and b.val < 2):
                            pool.wait_ge(tn_ok, b.val - 1)
                        nc.gpsimd.tensor_tensor(rstd[:, b.par, :], t[2], t[1], ALU.mult).then_inc(r_ok, 1)
                        pool.wait_ge(r_ok, 2 * b.val + 2)
                    if i.static and i.val == NB:
                        for ct in range(QK):
                            pool.wait_ge(dw_l[ct], n_dve[ct] * (NB - 1))
                        pool.wait_ge(dw_t, QK * (NB - 1))
                        pool.wait_ge(lt_a, QK * (NB - 1))
                        nc.gpsimd.memset(zwin[NB % 2][:, :, 2, 1:W + 1], 0.0).then_inc(row_z, 1)
                    for n, g in pieces_of(i):
                        pool.wait_ge(e_hi, n + 1)
                        hi, lo, raw = pieces[n]
                        nc.gpsimd.tensor_tensor(lo, raw, hi.bitcast(FP32), ALU.subtract).then_inc(e_lo, 1)

                steps(pool, step, FIRST, LAST, LO, HI)
                pool.wait_ge(at_v, 1)
                nc.gpsimd.tensor_scalar(n2[:, 1, :], pw[:, 0, 0:QK], -1.0, 0.0, ALU.mult, ALU.add).then_inc(at_p, 1)
                pool.wait_ge(at_p, 1)
                nc.gpsimd.tensor_tensor(n2[:, 2, :], n2[:, 0, :], n2[:, 1, :], ALU.pow).then_inc(at_p, 1)

            @blk.scalar
            def _(act):
                def copy_q(n, t):
                    lo, hi = slots(n)
                    if lo <= t < hi:
                        c = ROWS * n.val - 1 + t
                        act.wait_ge(q_t, c + 1)
                        wait(act, gr_t, c - 1)
                        nc.scalar.activation(qk_tok[:, t % 2, :], qb[:, 0:2 * C], ACT.Copy).then_inc(q_a, 1)

                def copy_z(i, ct):
                    c = 5 * i.val + ct
                    m = ZT[ct][1]
                    act.wait_ge(z_t, c + 1)
                    if ct < QK:
                        wait(act, dw_l[ct], n_dve[ct] * (i.val - 1))
                        wait(act, dw_t, QK * (i.val - 2) + ct + 1)
                        nc.scalar.activation(zwin[i.par][:, ct, 2:6, 1:W + 1],
                                             zb[(i.par + ct) % 2][:, :].rearrange("p (r w) -> p r w", w=W),
                                             ACT.Identity, bias=bz[:, ct:ct + 1]).then_inc(z_a, 1)
                    else:
                        if ct == QK:
                            wait(act, st_v, 16 * i.val)
                        nc.scalar.activation(zv[:, ct - QK, :], zb[(i.par + ct) % 2][0:m, :], ACT.Identity,
                                             bias=bz[0:m, ct:ct + 1]).then_inc(z_a, 1)

                def act_tap(n, ct):
                    lo, hi = slots(n)
                    ky, kx = divmod(POOL_TAP, KX)
                    if n.static and n.val == NB:
                        act.wait_ge(row_z, 1)
                    wait(act, qs_ok, QK * (n.val - 1) + ct + 1)
                    nc.scalar.activation(last_tap[:, ct, lo:hi, :], zwin[n.par][:, ct, ky + lo:ky + hi, kx:kx + W], ACT.Identity,
                                         scale=wdw[:, ct, POOL_TAP:POOL_TAP + 1]).then_inc(lt_a, 1)

                def step(i):
                    if i.within(0, NB - 1):
                        act.wait_ge(ac_t, 2 * i.val + 1)
                        wait(act, z_t, 5 * i.val)
                        nc.scalar.activation(xh_a[:, 0, :], tp[0][:, :], ACT.Copy).then_inc(hi_ok, 1)
                        act.wait_ge(ac_t, 2 * i.val + 2)
                        nc.scalar.activation(x_c[:, 0, :], tp[1][:, :], ACT.Copy).then_inc(hi_ok, 1)
                    if i.within(1, NB):
                        act.wait_ge(z_a, 5 * i.val)
                        for ct in range(QK):
                            wait(act, dw_l[ct], n_dve[ct] * (i.val - 1))
                        wait(act, dw_t, QK * (i.val - 1))
                        nc.scalar.activation(zwin[i.par][:, :, 0:2, 1:W + 1], zwin[1 - i.par][:, :, 4:6, 1:W + 1],
                                             ACT.Copy).then_inc(carry, 1)
                    n = i - 2
                    if n.within(0, NB):
                        lo, hi = slots(n)
                        for ct in range(QK):
                            act.wait_ge(qs_ok, QK * n.val + ct + 1)
                            wait(act, sq_ok, QK * n.val + ct)
                            nc.scalar.activation(junk[:, lo * W:hi * W], qs[:, n.par, ct, lo:hi, :].rearrange("p r w -> p (r w)"),
                                                 ACT.Square, accum_out=nrm[:, ct, bass.ds(n.val, 1)]).then_inc(sq_ok, 1)
                        copy_q(n, 0)
                    if (i - 1).within(0, NB):
                        act.wait_ge(z_a, 5 * min(i.val, NB) if i.static else 5 * i.val)
                        act_tap(i - 1, 0)
                    if n.within(0, NB):
                        copy_q(n, 1)
                    if (i - 1).within(0, NB):
                        act_tap(i - 1, 1)
                    b = i + 2
                    if b.within(0, NB - 1):
                        for k in (0, 1):
                            act.wait_ge(xt_t, b.val + 1)
                            if k == 0:
                                wait(act, st_xt[b.par], 16 * b.half)
                                wait(act, tn_ok, b.val - 1)
                            nc.scalar.activation(xtok[:, b.par, 2 * k:2 * k + 2, :],
                                                 tp[k][:, 0:2 * C].rearrange("p (r c) -> p r c", c=C),
                                                 ACT.Copy).then_inc(xt_a, 1)
                    if n.within(0, NB):
                        copy_q(n, 2)
                        copy_q(n, 3)
                    if (i - 1).within(0, NB):
                        act_tap(i - 1, 2)
                    if i.within(0, NB - 1):
                        for ct in range(2):
                            copy_z(i, ct)
                    if (i + 1).within(0, NB - 1):
                        act.wait_ge(tn_ok, (i + 1).val + 1)
                        nc.scalar.activation(tn[:, :, C:256], tn[:, :, CA:C], ACT.Copy).then_inc(tn_dup, 1)
                    if i.within(0, NB - 1):
                        for ct in range(2, 5):
                            copy_z(i, ct)
                    for n, g in pieces_of(i):
                        act.wait_ge(ld_e, 32 * (g + 1))
                        hi, lo, raw = pieces[n]
                        nc.scalar.activation(hi, raw, ACT.Copy).then_inc(e_hi, 1)

                def setup():
                    for ct, (o, m) in enumerate(ZT):
                        act.wait_ge(su_t, 2 * ct + 2)
                        nc.scalar.activation(wq_ah[:, o:o + m], zb[ct % 2][:, 0:m], ACT.Copy).then_inc(su_a, 1)
                        nc.scalar.activation(wq_ch[:, o:o + m], zb[ct % 2][:, 128:128 + m], ACT.Copy).then_inc(su_a, 1)
                    act.wait_ge(su_t, 11)
                    nc.scalar.activation(s_tok[:, :], db[0][:, 0:128], ACT.Copy).then_inc(su_a, 1)
                    act.wait_ge(su_t, 12)
                    nc.scalar.activation(wpt[:, :, :], db[1][0:G2, 0:2 * C].rearrange("p (g o) -> p g o", g=2), ACT.Copy)\
                        .then_inc(su_a, 1)
                    act.wait_ge(const, 7)
                    act.wait_ge(ld_w, 16 * N_LD_W)

                steps(act, step, FIRST, LAST, LO, HI, setup)
                act.wait_ge(at_t, 1)
                nc.scalar.activation(rn_row[:, :], db[0][0:QK, 0:128], ACT.Copy).then_inc(at_a, 1)
                act.wait_ge(at_t, 2)
                nc.scalar.activation(rb[:, :], db[1][0:G2, 0:2 * C], ACT.Copy).then_inc(at_a, 1)
                act.wait_ge(at_v, 12)
                for g in (0, 1):
                    nc.scalar.activation(attn[:, 2, g, :], attn[:, 1, g, :], ACT.Exp, bias=acol[:, 2, g:g + 1],
                                         accum_out=acol[:, 3, g:g + 1]).then_inc(at_a, 1)
                act.wait_ge(at_t, 3)
                nc.scalar.activation(mt[:, :, :], db[0][0:G2, 0:2 * C].rearrange("p (g o) -> p g o", g=2), ACT.Copy)\
                    .then_inc(at_a, 1)

            @blk.vector
            def _(dve):
                def window_ready(n):
                    if n.within(0, NB - 1):
                        dve.wait_ge(z_a, 5 * n.val + QK)
                    wait(dve, carry, n.val)
                    if n.static and n.val == NB:
                        dve.wait_ge(row_z, 1)

                def tap(n, ct, k):
                    lo, hi = slots(n)
                    ky, kx = divmod(DVE_TAPS[ct][k], KX)
                    a = acc[:, ct, lo:hi, :]
                    if k == 0:
                        wait(dve, qs_ok, QK * (n.val - 1) + ct + 1)
                        dve.wait_ge(dw_t, QK * n.val + ct + 1)
                        before = db[(n.par + ct) % 2][:, lo * W:hi * W].rearrange("p (r w) -> p r w", w=W)
                    else:
                        dve.wait_ge(dw_l[ct], n_dve[ct] * n.val + k)
                        before = a
                    nc.vector.scalar_tensor_tensor(
                        out=a, in0=zwin[n.par][:, ct, ky + lo:ky + hi, kx:kx + W],
                        scalar=wdw[:, ct, DVE_TAPS[ct][k]:DVE_TAPS[ct][k] + 1], in1=before, op0=ALU.mult, op1=ALU.add).then_inc(dw_l[ct], 1)

                def step(i):
                    if i.within(0, NB - 1):
                        dve.wait_ge(hi_ok, 2 * i.val + 1)
                        nc.vector.tensor_tensor(xl_a[:, 0, :], tp[0][:, :], xh_a[:, 0, :].bitcast(FP32), ALU.subtract).then_inc(lo_ok, 1)
                        dve.wait_ge(hi_ok, 2 * i.val + 2)
                        nc.vector.tensor_tensor(x_c[CB:128, 0, :], tp[1][CB:128, :], x_c[CB:128, 0, :].bitcast(FP32), ALU.subtract)\
                            .then_inc(lo_ok, 1)
                    n = i - 1
                    if n.within(0, NB):
                        window_ready(n)
                        for k in range(HEAD_START):
                            tap(n, 0, k)
                        for k in range(n_dve[1]):
                            if k + HEAD_START < n_dve[0]:
                                tap(n, 0, k + HEAD_START)
                            tap(n, 1, k)
                    b = i + 1
                    if b.within(0, NB - 1):
                        wait(dve, ac_t, 2 * b.val)
                        dve.wait_ge(r_ok, 2 * b.val + 2)
                        for t in range(ROWS):
                            last = nc.vector.tensor_scalar(tn[:, t, 0:C], xtok[:, b.par, t, :], mv[:, b.par, t, 0:1],
                                                           rstd[:, b.par, t:t + 1], ALU.subtract, ALU.mult)
                        last.then_inc(tn_ok, 1)
                    b = i + 2
                    if n.within(0, NB):
                        tap(n, 2, 0)
                    if b.within(0, NB - 1):
                        dve.wait_ge(xt_a, 2 * b.val + 2)
                        wait(dve, r_ok, 2 * b.val - 2)
                    for t in range(ROWS):
                        if b.within(0, NB - 1):
                            last = nc.vector.bn_stats(stat[:, b.par, t, :], xtok[:, b.par, t, :])
                            if t == ROWS - 1:
                                last.then_inc(bn_ok, 1)
                        if n.within(0, NB):
                            tap(n, 2, t + 1)
                    if b.within(0, NB - 1):
                        dve.wait_ge(bn_ok, b.val + 1)
                        nc.vector.memset(pause[:, 0:1], 0.0)
                        for t in range(ROWS):
                            last = nc.vector.bn_aggr(mv[:, b.par, t, :], stat[:, b.par, t, :])
                        last.then_inc(stats, 1)
                    if n.within(0, NB):
                        for k in range(ROWS + 1, n_dve[2]):
                            tap(n, 2, k)

                def setup():
                    dve.wait_ge(ld_q, 16 * N_LD_Q)
                    n_v = [0]

                    def link(ins):
                        n_v[0] += 1
                        ins.then_inc(su_v, 1)
                        dve.wait_ge(su_v, n_v[0])

                    for ct, (o, m) in enumerate(ZT):
                        nc.vector.tensor_tensor(wp[0:m, ct, 0:C], wn[0:m, ct, :], lnw_bb[0:m, :], ALU.mult)
                        nc.vector.tensor_tensor(wp[0:m, ct, C:256], wn[0:m, ct, CA:C], lnw_bb[0:m, CA:C], ALU.mult)
                        link(nc.vector.tensor_tensor(wtmp[0:m, :], wn[0:m, ct, :], lnb_bb[0:m, :], ALU.mult))
                        link(nc.vector.reduce_sum(bz[0:m, ct:ct + 1], wtmp[0:m, :], AX))
                    for ct, (o, m) in enumerate(ZT):
                        dve.wait_ge(su_a, 2 * ct + 2)
                        link(nc.vector.tensor_tensor(wq_al[:, o:o + m], zb[ct % 2][:, 0:m], wq_ah[:, o:o + m].bitcast(FP32), ALU.subtract))
                        link(nc.vector.tensor_tensor(wq_cl[:, o:o + m], zb[ct % 2][:, 128:128 + m], wq_ch[:, o:o + m].bitcast(FP32), ALU.subtract))
                    dve.wait_ge(const, 8)
                    dve.wait_ge(ld_w, 16 * N_LD_W)
                    for ct in range(QK):
                        for k, tap in enumerate(PE_TAPS[ct]):
                            link(nc.vector.tensor_scalar(diag[:, ct, k, :], ident[:, :], wdw[:, ct, tap:tap + 1], None, ALU.mult))

                steps(dve, step, FIRST, LAST, LO, HI, setup)
                dve.wait_ge(sq_ok, QK * (NB + 1))
                nc.vector.reduce_sum(n2[:, 0, :], nrm[:, :, :], AX).then_inc(at_v, 1)
                dve.wait_ge(at_p, 2)
                nc.vector.tensor_scalar(n2[:, 3, :], n2[:, 2, :], EPS_NORM, None, ALU.max).then_inc(at_v, 1)
                dve.wait_ge(at_v, 2)
                nc.vector.reciprocal(n2[:, 1, :], n2[:, 3, :]).then_inc(at_v, 1)
                dve.wait_ge(at_a, 2)
                for g in (0, 1):
                    nc.vector.tensor_tensor(attn[:, 0, g, :], rb[:, G2 * g:G2 * g + G2], ident[0:G2, 0:G2], ALU.mult).then_inc(at_v, 1)
                dve.wait_ge(at_v, 5)
                nc.vector.reduce_sum(acol[:, 0, :], attn[:, 0, :, :], AX).then_inc(at_v, 1)
                dve.wait_ge(at_v, 6)
                nc.vector.tensor_tensor(acol[:, 1, :], acol[:, 0, :], temp[:, :], ALU.mult).then_inc(at_v, 1)
                dve.wait_ge(at_v, 7)
                dve.wait_ge(gr_t, H)
                dve.wait_ge(const, 13)
                for g in (0, 1):
                    nc.vector.scalar_tensor_tensor(out=attn[:, 0, g, :], in0=gb[0:G2, G2 * g:G2 * g + G2], scalar=acol[:, 1, g:g + 1],
                                                   in1=rb[:, C + G2 * g:C + G2 * g + G2], op0=ALU.mult, op1=ALU.mult).then_inc(at_v, 1)
                dve.wait_ge(at_v, 9)
                nc.vector.tensor_tensor(attn[:, 1, :, :].rearrange("p g c -> p (g c)"), attn[:, 0, :, :].rearrange("p g c -> p (g c)"),
                                        mask[:, :, :, :].rearrange("p g h c -> p (g h c)"), ALU.add).then_inc(at_v, 1)
                dve.wait_ge(at_v, 10)
                nc.vector.tensor_reduce(out=acol[:, 4, :], in_=attn[:, 1, :, :], axis=AX, op=ALU.max).then_inc(at_v, 1)
                dve.wait_ge(at_v, 11)
                nc.vector.tensor_scalar(acol[:, 2, :], acol[:, 4, :], -1.0, None, ALU.mult).then_inc(at_v, 1)
                dve.wait_ge(at_a, 4)
                nc.vector.reciprocal(acol[:, 5, :], acol[:, 3, :]).then_inc(at_v, 1)
                dve.wait_ge(at_v, 13)
                for g in (0, 1):
                    nc.vector.tensor_scalar(attn[:, 3, g, :], attn[:, 2, g, :], acol[:, 5, g:g + 1], None, ALU.mult).then_inc(at_v, 1)

            @blk.tensor
            def _(pe):
                pe.wait_ge(const, 8)

                def dw(n, ct):
                    lo, hi = slots(n)
                    if ct == 0:
                        if n.within(0, NB - 1):
                            pe.wait_ge(z_a, 5 * n.val + QK)
                        wait(pe, carry, n.val)
                        if n.static and n.val == NB:
                            pe.wait_ge(row_z, 1)
                    if ct == 2 or not (n.static and n.val == 0):
                        last_n, last_ct = (n, 0) if ct == 2 else (n - 1, ct + 1)
                        pe.wait_ge(dw_l[last_ct], n_dve[last_ct] * last_n.val + 1)
                    for k, tap in enumerate(PE_TAPS[ct]):
                        ky, kx = divmod(tap, KX)
                        last = nc.tensor.matmul(db[(n.par + ct) % 2][:, lo * W:hi * W].rearrange("p (r w) -> p r w", w=W),
                                                diag[:, ct, k, :], zwin[n.par][:, ct, ky + lo:ky + hi, kx:kx + W],
                                                start=(k == 0), stop=(k == len(PE_TAPS[ct]) - 1))
                    last.then_inc(dw_t, 1)

                def tile_no(n, t):
                    return ROWS * n.val - 1 + t

                def q_tr(n, t):
                    lo, hi = slots(n)
                    if lo <= t < hi:
                        c = tile_no(n, t)
                        if t == lo:
                            pe.wait_ge(qs_ok, QK * n.val + QK)
                        wait(pe, q_a, c)
                        for ct in range(QK):
                            last = nc.tensor.transpose(qb[:, ct * 128:ct * 128 + 128], qs[:, n.par, ct, t, :], ident[:, :])
                        last.then_inc(q_t, 1)

                def gram(n, t):
                    lo, hi = slots(n)
                    if lo <= t < hi:
                        c = tile_no(n, t)
                        pe.wait_ge(q_a, c + 1)
                        first = n.static and n.val == 0 and t == lo
                        final = n.static and n.val == NB
                        for g in (0, 1):
                            last = nc.tensor.matmul(gb[0:G2, g * G2:g * G2 + G2], qk_tok[:, t % 2, G2 * g:G2 * g + G2],
                                                    qk_tok[:, t % 2, C + G2 * g:C + G2 * g + G2],
                                                    start=(first and g == 0), stop=final, skip_group_check=True)
                        last.then_inc(gr_t, 1)

                def z(i, ct):
                    o, m = ZT[ct]
                    c = 5 * i.val + ct
                    if ct == 0:
                        pe.wait_ge(lo_ok, 2 * i.val + 2)
                    wait(pe, z_a, c - 1)
                    dst = zb[(i.par + ct) % 2][0:m, :]
                    ops = [(wq_ah, xh_a), (wq_al, xh_a), (wq_ah, xl_a), (wq_ch, x_c), (wq_cl, x_c)]
                    for k, (w, v) in enumerate(ops):
                        last = nc.tensor.matmul(dst, w[:, o:o + m], v[:, 0, :], start=(k == 0), stop=(k == 4))
                    last.then_inc(z_t, 1)

                def step(i):
                    if i.within(0, NB - 1):
                        pe.wait_ge(tn_dup, i.val + 1)
                        wait(pe, xt_a, 2 * min(i.val + 2, NB) if i.static else 2 * i.val + 4)
                        for h in (0, 1):
                            for t in range(ROWS):
                                last = nc.tensor.transpose(tp[h][:, t * 128:t * 128 + 128], tn[:, t, h * 128:h * 128 + 128], ident[:, :])
                            last.then_inc(ac_t, 1)
                    n, m = i - 1, i - 2
                    has_i, has_n, has_m = i.within(0, NB - 1), n.within(0, NB), m.within(0, NB)
                    if has_n:
                        dw(n, 0)
                        dw(n, 1)
                    if has_m:
                        q_tr(m, 0)
                    b = i + 2
                    if b.within(0, NB - 1):
                        pe.wait_ge(ld_x[b.par], 32 * b.half + 32)
                        if i.static:
                            wait(pe, lo_ok, 2 * i.val + 2)
                            wait(pe, xt_a, 2 * b.val)
                        else:
                            pe.wait_ge(lo_ok, 2 * i.val + 2)
                        for t in range(ROWS):
                            cols = slice(t * 128, t * 128 + 128)
                            o = t % 2 * C
                            nc.tensor.transpose(tp[t // 2][:, o:o + CA], xc_a[:, b.par, cols], ident[:, :])
                            last = nc.tensor.transpose(tp[t // 2][:, o + CA:o + C], xc_b[:, b.par, cols], ident[0:CB, 0:CB])
                        last.then_inc(xt_t, 1)
                    if has_m:
                        q_tr(m, 1)
                        gram(m, 0)
                    if has_i:
                        z(i, 0)
                    if has_m:
                        q_tr(m, 2)
                        gram(m, 1)
                    if has_i:
                        z(i, 1)
                    if has_m:
                        q_tr(m, 3)
                        gram(m, 2)
                    if has_n:
                        dw(n, 2)
                    if has_m:
                        gram(m, 3)
                    if has_i:
                        z(i, 2)
                        z(i, 3)
                        z(i, 4)

                def setup():
                    for ct, (o, m) in enumerate(ZT):
                        pe.wait_ge(su_v, 2 * ct + 2)
                        if ct >= 2:
                            pe.wait_ge(su_v, 10 + 2 * (ct - 1))
                        nc.tensor.transpose(zb[ct % 2][:, 0:m], wp[0:m, ct, 0:CA], ident[0:m, 0:m]).then_inc(su_t, 1)
                        nc.tensor.transpose(zb[ct % 2][:, 128:128 + m], wp[0:m, ct, CA:256], ident[0:m, 0:m]).then_inc(su_t, 1)
                    pe.wait_ge(ld_w, 16 * N_LD_W)
                    nc.tensor.transpose(db[0][:, 0:128], s_rows[:, :], ident[:, :]).then_inc(su_t, 1)
                    for g in (0, 1):
                        nc.tensor.transpose(db[1][0:G2, g * C:g * C + CA], wpr[:, 0, G2 * g:G2 * g + G2], ident[:, :])
                        last = nc.tensor.transpose(db[1][0:G2, g * C + CA:g * C + C], wpr[0:CB, 1, G2 * g:G2 * g + G2], ident[0:CB, 0:CB])
                    last.then_inc(su_t, 1)
                    n_su_v = 10 + n_diag + 10
                    pe.wait_ge(su_v, n_su_v)
                    pe.wait_ge(su_a, 12)

                steps(pe, step, FIRST, LAST, LO, HI, setup)
                pe.wait_ge(at_v, 3)
                nc.tensor.transpose(db[0][0:QK, 0:128], n2[:, 1, :], ident[:, :]).then_inc(at_t, 1)
                pe.wait_ge(at_a, 1)
                pe.wait_ge(const, 12)
                for ct in range(QK):
                    last = nc.tensor.matmul(db[1][0:G2, ct * 128:ct * 128 + 128], sel[:, ct, :], rn_row[:, :], start=True, stop=True)
                last.then_inc(at_t, 1)
                pe.wait_ge(at_v, 15)
                for g in (0, 1):
                    last = nc.tensor.matmul(db[0][0:G2, g * C:g * C + C], attn[:, 3, g, :], wpt[:, g, :], start=True, stop=True)
                last.then_inc(at_t, 1)

        p2 = ExitStack()
        with p2:
            vwin = sb(p2, "vwin", [G2, 2, 2, 6, W + 2])
            vd = sb(p2, "vd", [G2, 2, ROWS, W])
            y_acc = sb(p2, "y_acc", [128, 2, ROWS, 2 * C])
            hf = sb(p2, "hf", [128, 3, TOK])
            hh = sb(p2, "hh", [128, 3, TOK], F32R)
            hl = sb(p2, "hl", [128, 3, TOK], F32R)
            fin = sb(p2, "fin", [128, ROWS, C])
            fin_a = sb(p2, "fin_a", [CA, TOK])
            fin_b = sb(p2, "fin_b", [CB, TOK])
            sc = sb(p2, "sc", [128, 8, ROWS, E])
            cmp_ = sb(p2, "cmp", [128, 4, ROWS, E, E])
            col = sb(p2, "col", [128, 6, ROWS])
            tri = sb(p2, "tri", [128, ROWS, E, E])
            e_base = sb(p2, "e_base", [128, ROWS, E])
            gm = sb(p2, "gm", [128, 2, ROWS, E])
            gate_bc = sb(p2, "gate_bc", [128, C, E])
            b2_bc = sb(p2, "b2_bc", [128, E, C])
            score = sb(p2, "score", [128, ROWS, E])
            prods = sb(p2, "prods", [128, 4, C])
            b2_p = sb(p2, "b2_p", [128, E, C])
            b2_q = sb(p2, "b2_q", [128, 2, C])
            zcol = sb(p2, "zcol", [128, 1])
            b2_s = sb(p2, "b2_s", [128, ROWS, C])

            lb = banks[0:2]
            yb = banks[2:6]
            mb = banks[6:8]

            c2 = sem("c2")
            ld_xt = [sem("ld_xt0"), sem("ld_xt1")]
            ld_v = [sem("ld_v0"), sem("ld_v1")]
            st_out = sem("st_out")
            vd_l = sem("vd_l")
            co_t = sem("co_t")
            x1_ok, bn_l, mv2, r2_l, r2_ok, tn2, tn2_dup, ac2 = (sem(s) for s in ("x1_ok", "bn_l", "mv2", "r2_l", "r2_ok", "tn2", "tn2_dup", "ac2"))
            hi2, lo2, sc_l, g_v, g_p, g_l, gm_ok = (sem(s) for s in ("hi2", "lo2", "sc_l", "g_v", "g_p", "g_l", "gm_ok"))
            ld_g, b2_l, ylo_ok, fin_l = (sem(s) for s in ("ld_g", "b2_l", "ylo_ok", "fin_l"))
            l1, gelu, hh_ok, hl_ok, y_t, y_v = (sem(s) for s in ("l1", "gelu", "hh_ok", "hl_ok", "y_t", "y_v"))
            fin_ok, ot_t, ot_a = sem("fin_ok"), sem("ot_t"), sem("ot_a")

            FIRST2, LAST2, LO2, HI2 = -1, NB + 1, 3, NB - 4
            GATE_AT = {3: 4, 4: 5}
            TAPS_AT = {0: 2, 2: 2, 3: 1, 4: 1, 5: 2, 6: 2, 8: 2, 9: 2, 10: 2, 11: 2}
            assert sum(TAPS_AT.values()) == 18
            PROJ_AT, X1_AT, TN_AT, TN_DUP_AT, AC_AT, HI_AT, LO_AT, GATE1_AT = 14, 15, 17, 18, 20, 20, 21, 22
            SCORE_AT = {18: 4, 19: 4, 20: 4, 21: 4}
            OUT_AT, OUTC_AT, PROJ0_AT = 2, 2, 8
            GATE_V, GATE_L = 3, 10

            def second_done(s, k, t=None):
                e, m = divmod(k, CH)
                done = (E * s.val + e) * (CH - 1 + ROWS) + m + 1
                return done + (ROWS - 1 if t is None else t) if m == CH - 1 else done

            def buffer_free(eng, i, k):
                old = (i, k - 3) if k >= 3 else (i - 1, k - 3 + NCH)
                if old[0].within(0, NB - 1):
                    eng.wait_ge(y_t, second_done(*old))

            blk = p2.enter_context(nc.Block())

            @blk.sync
            def _(sp):
                def load(b):
                    if not b.within(0, NB - 1):
                        return
                    wait(sp, x1_ok, ROWS * (b.val - 1))
                    sp.dma_start(xtok[:, b.par, :, :], xtok_dram[bass.ds(b.val * ROWS, ROWS), :, :].rearrange("r p c -> p r c"))\
                        .then_inc(ld_xt[b.par], 16)
                    for g in (0, 1):
                        sp.dma_start(vwin[:, b.par, g, :, 1:W + 1], v_view[:, g, bass.ds(b.val * ROWS, 6), :]).then_inc(ld_v[b.par], 16)

                def step(i):
                    b = i - 2
                    if b.within(0, NB - 1):
                        cols = bass.ds(b.val * TOK, TOK)
                        sp.wait_ge(ot_a, 2 * b.val + 1)
                        sp.dma_start(out_view[0:CA, cols], fin_a[:, :]).then_inc(st_out, 16)
                        sp.wait_ge(ot_a, 2 * b.val + 2)
                        sp.dma_start(out_view[CA:C, cols], fin_b[:, :]).then_inc(st_out, 16)
                    load(i + 2)

                sp.wait_ge(c2, 1)
                load(Step(0, 0))
                sp.dma_start(gate_bc[:, :, :].rearrange("p c e -> p (c e)"),
                             gate_w.rearrange("c e -> (c e)").rearrange("(a n) -> a n", a=1).to_broadcast([128, C * E])).then_inc(ld_g, 16)
                sp.dma_start(b2_bc[:, :, :].rearrange("p e c -> p (e c)"),
                             b2.rearrange("e c -> (e c)").rearrange("(a n) -> a n", a=1).to_broadcast([128, E * C])).then_inc(ld_g, 16)
                steps(sp, step, FIRST2, LAST2, LO2, HI2)
                sp.wait_ge(st_out, 32 * NB)

            @blk.gpsimd
            def _(pool):
                sides = vwin[:, :, :, :, :].rearrange("p a g r w -> p (a g r) w")
                nc.gpsimd.memset(sides[:, :, 0:W + 2:W + 1], 0.0).then_inc(c2, 1)
                nc.gpsimd.memset(tri[:, :, :, :], 1.0).then_inc(c2, 1)
                nc.gpsimd.memset(e_base[:, :, :], E_BASE).then_inc(c2, 1)
                nc.gpsimd.memset(zcol[:, :], 0.0).then_inc(c2, 1)
                pool.wait_ge(c2, 4)
                nc.gpsimd.affine_select(out=tri[:, :, :, :], in_=tri[:, :, :, :], compare_op=ALU.is_gt, fill=0.0,
                                        base=0, pattern=[[0, ROWS], [1, E], [-1, E]], channel_multiplier=0).then_inc(c2, 1)

                pool.wait_ge(ld_g, 32)

                def step(i):
                    b = i - 1
                    if b.within(0, NB - 1):
                        pool.wait_ge(y_v, 4 * E * b.val + 4 * E)
                        wait(pool, ot_t, 2 * b.val)
                        nc.gpsimd.tensor_tensor(fin[:, :, :], y_acc[:, b.par, :, 0:C], y_acc[:, b.par, :, C:2 * C], ALU.add)\
                            .then_inc(fin_l, 1)
                        pool.wait_ge(fin_l, b.val + 1)
                        nc.gpsimd.tensor_tensor(fin[:, :, :], fin[:, :, :], b2_s[:, :, :], ALU.add).then_inc(fin_ok, 1)
                        pool.wait_ge(fin_ok, b.val + 1)
                    b = i + 1
                    if b.within(0, NB - 1):
                        zeros = zcol[:, :, None].to_broadcast([128, ROWS, C])
                        nc.gpsimd.tensor_tensor(y_acc[:, b.par, :, C:2 * C], zeros, zeros, ALU.add).then_inc(ylo_ok, 1)
                    if i.within(0, NB - 1):
                        pool.wait_ge(gm_ok, i.val + 1)
                        for t in range(ROWS):
                            base = 3 * (ROWS * i.val + t)
                            nc.gpsimd.tensor_tensor(b2_p[:, :, :], b2_bc[:, :, :], gm[:, i.par, t, :, None].to_broadcast([128, E, C]),
                                                    ALU.mult).then_inc(b2_l, 1)
                            pool.wait_ge(b2_l, base + 1)
                            nc.gpsimd.tensor_tensor(b2_q[:, :, :], b2_p[:, 0:2, :], b2_p[:, 2:4, :], ALU.add).then_inc(b2_l, 1)
                            pool.wait_ge(b2_l, base + 2)
                            nc.gpsimd.tensor_tensor(b2_s[:, t, :], b2_q[:, 0, :], b2_q[:, 1, :], ALU.add).then_inc(b2_l, 1)
                            pool.wait_ge(b2_l, base + 3)
                    if b.within(0, NB - 1):
                        pool.wait_ge(mv2, b.val + 1)
                        nc.gpsimd.tensor_tensor(small[:, 4, :], mv[:, 0, :, 1], pw[:, 2, :], ALU.add).then_inc(r2_l, 1)
                        pool.wait_ge(r2_l, b.val + 1)
                        nc.gpsimd.tensor_tensor(rstd[:, 0, :], small[:, 4, :], pw[:, 0, :], ALU.pow).then_inc(r2_ok, 1)
                        pool.wait_ge(g_v, GATE_V * b.val + 3)
                        nc.gpsimd.tensor_tensor(sc[:, 2, :, :], e_base[:, :, :], sc[:, 1, :, :], ALU.pow).then_inc(g_p, 1)

                steps(pool, step, FIRST2, LAST2, LO2, HI2)

            @blk.scalar
            def _(act):
                def chunk(i, k):
                    c = NCH * i.val + k
                    act.wait_ge(l1, c + 1)
                    wait(act, hl_ok, c - 2)
                    nc.scalar.activation(hf[:, k % 3, :], lb[k % 2][:, :], ACT.Gelu, bias=b1_col[:, k:k + 1]).then_inc(gelu, 1)
                    act.wait_ge(gelu, c + 1)
                    buffer_free(act, i, k)
                    nc.scalar.activation(hh[:, k % 3, :], hf[:, k % 3, :], ACT.Copy).then_inc(hh_ok, 1)

                def step(i):
                    cur, nxt, old = i.within(0, NB - 1), (i + 1).within(0, NB - 1), (i - 1).within(0, NB - 1)
                    for k in range(NCH):
                        if cur:
                            chunk(i, k)
                        b = i - 2
                        if k == OUTC_AT and b.within(0, NB - 1):
                            act.wait_ge(ot_t, 2 * b.val + 1)
                            wait(act, st_out, 32 * b.val)
                            nc.scalar.activation(fin_a[:, :], mb[0][:, :], ACT.Copy).then_inc(ot_a, 1)
                            act.wait_ge(ot_t, 2 * b.val + 2)
                            nc.scalar.activation(fin_b[:, :], mb[1][0:CB, :], ACT.Copy).then_inc(ot_a, 1)
                        if k == TN_DUP_AT and nxt:
                            act.wait_ge(tn2, i.val + 2)
                            nc.scalar.activation(tn[:, :, C:256], tn[:, :, CA:C], ACT.Copy).then_inc(tn2_dup, 1)
                        if k == HI_AT and nxt:
                            b = i + 1
                            act.wait_ge(ac2, 2 * b.val + 1)
                            wait(act, l1, NCH * (b.val - 1))
                            nc.scalar.activation(xh_a[:, b.par, :], mb[0][:, :], ACT.Copy).then_inc(hi2, 1)
                            act.wait_ge(ac2, 2 * b.val + 2)
                            nc.scalar.activation(x_c[:, b.par, :], mb[1][:, :], ACT.Copy).then_inc(hi2, 1)

                steps(act, step, FIRST2, LAST2, LO2, HI2)

            @blk.vector
            def _(dve):
                def tap(b, n):
                    g, k = divmod(n, 9)
                    ky, kx = divmod(k, KX)
                    src = vwin[:, b.par, g, ky:ky + ROWS, kx:kx + W]
                    if n == 0:
                        dve.wait_ge(ld_v[b.par], 32 * b.half + 32)
                        wait(dve, co_t, 2 * b.val)
                    if k == 0:
                        ins = nc.vector.tensor_scalar(vd[:, g, :, :], src, wdw_v[:, g, 0:1], None, ALU.mult)
                    else:
                        dve.wait_ge(vd_l, 18 * b.val + n)
                        ins = nc.vector.scalar_tensor_tensor(out=vd[:, g, :, :], in0=src, scalar=wdw_v[:, g, k:k + 1],
                                                             in1=vd[:, g, :, :], op0=ALU.mult, op1=ALU.add)
                    ins.then_inc(vd_l, 1)

                def expert_sum(s, e):
                    ex = E * s.val + e
                    if e == 0:
                        dve.wait_ge(gm_ok, s.val + 1)
                        dve.wait_ge(ylo_ok, s.val + 1)
                        dve.wait_ge(x1_ok, ROWS * s.val + ROWS)
                    else:
                        dve.wait_ge(y_v, 4 * ex)
                    for t in range(ROWS):
                        dve.wait_ge(y_t, second_done(s, CH * e + CH - 1, t))
                        nc.vector.scalar_tensor_tensor(out=y_acc[:, s.par, t, :], in0=yb[t][:, 0:2 * C], scalar=gm[:, s.par, t, e:e + 1],
                                                       in1=y_acc[:, s.par, t, :], op0=ALU.mult, op1=ALU.add).then_inc(y_v, 1)

                def score_part(b, n):
                    t, e = divmod(n, E)
                    if n == 0:
                        dve.wait_ge(tn2, b.val + 1)
                    wait(dve, sc_l, ROWS * E * b.val + n - 3)
                    nc.vector.scalar_tensor_tensor(out=prods[:, n % 4, :], in0=tn[:, t, 0:C], scalar=1.0, in1=gate_bc[:, :, e],
                                                   op0=ALU.mult, op1=ALU.mult, accum_out=score[:, t, e:e + 1]).then_inc(sc_l, 1)

                def gate_1(b):
                    base = GATE_V * b.val
                    dve.wait_ge(sc_l, ROWS * E * (b.val + 1))
                    nc.vector.tensor_tensor(sc[:, 0, :, :], score[:, :, :],
                                            gate_bb[:, None, :].to_broadcast([128, ROWS, E]), ALU.add).then_inc(g_v, 1)
                    dve.wait_ge(g_v, base + 1)
                    nc.vector.tensor_reduce(out=col[:, 0, :], in_=sc[:, 0, :, :], axis=AX, op=ALU.max).then_inc(g_v, 1)
                    dve.wait_ge(g_v, base + 2)
                    wait(dve, gm_ok, b.val)
                    nc.vector.tensor_tensor(sc[:, 1, :, :], sc[:, 0, :, :], col[:, 0, :, None].to_broadcast([128, ROWS, E]),
                                            ALU.subtract).then_inc(g_v, 1)

                def gate_2(b):
                    p = sc[:, 2, :, :]
                    other = p[:, :, None, :].to_broadcast([128, ROWS, E, E])
                    own = p[:, :, :, None].to_broadcast([128, ROWS, E, E])
                    dve.wait_ge(g_p, b.val + 1)
                    nc.vector.tensor_tensor(cmp_[:, 0], other, own, ALU.is_gt).then_inc(g_l, 1)
                    nc.vector.tensor_tensor(cmp_[:, 1], other, own, ALU.is_equal).then_inc(g_l, 1)
                    nc.vector.reduce_sum(col[:, 1, :], p, AX).then_inc(g_l, 1)
                    yield
                    dve.wait_ge(g_l, GATE_L * b.val + 2)
                    nc.vector.tensor_tensor(cmp_[:, 2], cmp_[:, 1], tri[:, :, :, :], ALU.mult).then_inc(g_l, 1)
                    yield
                    dve.wait_ge(g_l, GATE_L * b.val + 4)
                    nc.vector.tensor_tensor(cmp_[:, 3], cmp_[:, 2], cmp_[:, 0], ALU.add).then_inc(g_l, 1)
                    yield
                    dve.wait_ge(g_l, GATE_L * b.val + 5)
                    nc.vector.reduce_sum(sc[:, 3, :, :], cmp_[:, 3], AX).then_inc(g_l, 1)
                    yield
                    dve.wait_ge(g_l, GATE_L * b.val + 6)
                    nc.vector.scalar_tensor_tensor(out=sc[:, 4, :, :], in0=sc[:, 3, :, :], scalar=1.5, in1=p,
                                                   op0=ALU.is_lt, op1=ALU.mult).then_inc(g_l, 1)
                    yield
                    dve.wait_ge(g_l, GATE_L * b.val + 7)
                    nc.vector.reduce_sum(col[:, 2, :], sc[:, 4, :, :], AX).then_inc(g_l, 1)
                    yield
                    dve.wait_ge(g_l, GATE_L * b.val + 8)
                    nc.vector.scalar_tensor_tensor(out=col[:, 3, :], in0=col[:, 1, :], scalar=EPS_GATE, in1=col[:, 2, :],
                                                   op0=ALU.mult, op1=ALU.add).then_inc(g_l, 1)
                    yield
                    dve.wait_ge(g_l, GATE_L * b.val + 9)
                    nc.vector.reciprocal(col[:, 4, :], col[:, 3, :]).then_inc(g_l, 1)
                    yield
                    dve.wait_ge(g_l, GATE_L * b.val + 10)
                    wait(dve, y_v, 4 * E * (b.val - 1))
                    wait(dve, fin_ok, b.val - 1)
                    nc.vector.tensor_tensor(gm[:, b.par, :, :], sc[:, 4, :, :], col[:, 4, :, None].to_broadcast([128, ROWS, E]),
                                            ALU.mult).then_inc(gm_ok, 1)
                    yield

                def step(i):
                    cur, nxt, old = i.within(0, NB - 1), (i + 1).within(0, NB - 1), (i - 1).within(0, NB - 1)
                    taps = scored = 0
                    gate = gate_2(i)
                    for k in range(NCH):
                        e, m = divmod(k + 1 - LAG, CH)
                        if m == 0 and e > 0 and cur:
                            expert_sum(i, e - 1)
                        if k == LAG - 1 and old:
                            expert_sum(i - 1, E - 1)
                        if cur:
                            c = NCH * i.val + k
                            dve.wait_ge(hh_ok, c + 1)
                            buffer_free(dve, i, k)
                            nc.vector.tensor_tensor(hl[:, k % 3, :], hf[:, k % 3, :], hh[:, k % 3, :].bitcast(FP32), ALU.subtract)\
                                .then_inc(hl_ok, 1)
                        for _ in range(GATE_AT.get(k, 0) if cur else 0):
                            next(gate)
                        b = i + 1
                        if nxt:
                            for _ in range(TAPS_AT.get(k, 0)):
                                tap(b, taps)
                                taps += 1
                            if k == X1_AT:
                                dve.wait_ge(ld_xt[b.par], 16 * b.half + 16)
                                wait(dve, fin_ok, b.val - 1)
                                for t in range(ROWS):
                                    dve.wait_ge(co_t, 2 * b.val + t // 2 + 1)
                                    nc.vector.scalar_tensor_tensor(
                                        out=y_acc[:, b.par, t, 0:C], in0=mb[t // 2][:, t % 2 * C:t % 2 * C + C],
                                        scalar=s_tok[:, bass.ds(b.val * ROWS + t, 1)], in1=xtok[:, b.par, t, :],
                                        op0=ALU.mult, op1=ALU.add).then_inc(x1_ok, 1)
                                dve.wait_ge(x1_ok, ROWS * b.val + ROWS)
                                for t in range(ROWS):
                                    last = nc.vector.bn_stats(stat[:, 0, t, :], y_acc[:, b.par, t, 0:C])
                                last.then_inc(bn_l, 1)
                                dve.wait_ge(bn_l, b.val + 1)
                                nc.vector.memset(pause[:, 1:2], 0.0)
                                for t in range(ROWS):
                                    last = nc.vector.bn_aggr(mv[:, 0, t, :], stat[:, 0, t, :])
                                last.then_inc(mv2, 1)
                            if k == TN_AT:
                                dve.wait_ge(r2_ok, b.val + 1)
                                wait(dve, ac2, 2 * b.val)
                                for t in range(ROWS):
                                    last = nc.vector.tensor_scalar(tn[:, t, 0:C], y_acc[:, b.par, t, 0:C], mv[:, 0, t, 0:1],
                                                                   rstd[:, 0, t:t + 1], ALU.subtract, ALU.mult)
                                last.then_inc(tn2, 1)
                            n_scores = SCORE_AT.get(k, 0) if cur else ROWS * E if k == LO_AT else 0
                            if k == LO_AT:
                                dve.wait_ge(hi2, 2 * b.val + 2)
                                nc.vector.tensor_tensor(xl_a[:, b.par, :], mb[0][:, :], xh_a[:, b.par, :].bitcast(FP32), ALU.subtract).then_inc(lo2, 1)
                                nc.vector.tensor_tensor(x_c[CB:128, b.par, :], mb[1][CB:128, :], x_c[CB:128, b.par, :].bitcast(FP32), ALU.subtract)\
                                    .then_inc(lo2, 1)
                            for _ in range(n_scores):
                                score_part(b, scored)
                                scored += 1
                            if k == GATE1_AT:
                                gate_1(b)

                dve.wait_ge(c2, 5)
                dve.wait_ge(ld_g, 32)
                steps(dve, step, FIRST2, LAST2, LO2, HI2)

            @blk.tensor
            def _(pe):
                def first(i, k):
                    c = NCH * i.val + k
                    if k == 0:
                        pe.wait_ge(lo2, 2 * i.val + 2)
                    wait(pe, gelu, c - 1)
                    ops = [(w1_ah, xh_a), (w1_al, xh_a), (w1_ah, xl_a), (w1_ch, x_c), (w1_cl, x_c)]
                    for n, (w, v) in enumerate(ops):
                        last = nc.tensor.matmul(lb[k % 2][:, :], w[:, k * 128:k * 128 + 128], v[:, i.par, :], start=(n == 0), stop=(n == 4))
                    last.then_inc(l1, 1)

                def second(s, k):
                    c = NCH * s.val + k
                    e, m = divmod(k, CH)
                    ex = E * s.val + e
                    pe.wait_ge(hl_ok, c + 1)
                    for t in range(ROWS):
                        if m == 0:
                            wait(pe, y_v, 4 * (ex - 1) + t + 1)
                        cols = slice(t * 128, t * 128 + 128)
                        nc.tensor.matmul(yb[t][:, 0:2 * C], hh[:, k % 3, cols], w2_hl[:, k, :], start=(m == 0), stop=False, skip_group_check=True)
                        last = nc.tensor.matmul(yb[t][:, 0:C], hl[:, k % 3, cols], w2_hl[:, k, 0:C], start=False, stop=(m == CH - 1), skip_group_check=True)
                        if t == ROWS - 1 or m == CH - 1:
                            last.then_inc(y_t, 1)

                def step(i):
                    cur, nxt, old = i.within(0, NB - 1), (i + 1).within(0, NB - 1), (i - 1).within(0, NB - 1)
                    for k in range(NCH):
                        if cur:
                            first(i, k)
                        b = i - 2
                        if k == OUT_AT and b.within(0, NB - 1):
                            pe.wait_ge(fin_ok, b.val + 1)
                            wait(pe, ot_a, 2 * b.val)
                            for t in range(ROWS):
                                last = nc.tensor.transpose(mb[0][:, t * 128:t * 128 + 128], fin[:, t, 0:CA], ident[:, :])
                            last.then_inc(ot_t, 1)
                            for t in range(ROWS):
                                last = nc.tensor.transpose(mb[1][0:CB, t * 128:t * 128 + 128], fin[:, t, CA:C], ident[:, :])
                            last.then_inc(ot_t, 1)
                        if nxt and k in (PROJ0_AT, PROJ_AT):
                            b, g = i + 1, int(k == PROJ_AT)
                            pe.wait_ge(vd_l, 18 * b.val + 9 * g + 9)
                            if (i - 2).within(0, NB - 1):
                                pe.wait_ge(ot_a, 2 * (i - 2).val + 2)
                            for t in range(ROWS):
                                last = nc.tensor.matmul(mb[t // 2][:, t % 2 * C:t % 2 * C + C], vd[:, g, t, :], mt[:, g, :],
                                                        start=(g == 0 and t % 2 == 0), stop=(g == 1), skip_group_check=True)
                                if g == 1 and t % 2:
                                    last.then_inc(co_t, 1)
                        if nxt and k == AC_AT:
                            b = i + 1
                            for h in (0, 1):
                                pe.wait_ge((tn2, tn2_dup)[h], b.val + 1)
                                for t in range(ROWS):
                                    last = nc.tensor.transpose(mb[h][:, t * 128:t * 128 + 128], tn[:, t, h * 128:h * 128 + 128], ident[:, :])
                                last.then_inc(ac2, 1)
                        if k < LAG:
                            if old:
                                second(i - 1, NCH - LAG + k)
                        elif cur:
                            second(i, k - LAG)

                steps(pe, step, FIRST2, LAST2, LO2, HI2)
    return nc


_INS = ["x", "L0_conv_spatial_interaction", "L0_conv_ln_w", "L0_conv_ln_b", "L0_conv_w_qkv", "L0_conv_w_dw",
        "L0_conv_w_proj", "L0_conv_temperature", "L0_ffn_gate_w", "L0_ffn_gate_b", "L0_ffn_w1", "L0_ffn_b1",
        "L0_ffn_w2", "L0_ffn_b2"]


def kernel(**inputs):
    import numpy as _np
    import concourse.bacc as _bacc
    from concourse import mybir as _mybir
    from concourse.bass_utils import run_bass_kernel_spmd as _run

    nc = _bacc.Bacc("TRN2", target_bir_lowering=False, num_devices=1)
    arrays, args = {}, []
    for name in _INS:
        a = _np.ascontiguousarray(inputs[name])
        arrays[f"in_{name}_dram"] = a
        args.append(nc.dram_tensor(f"in_{name}_dram", a.shape, _mybir.dt.from_np(a.dtype), kind="ExternalInput").ap())
    out = nc.dram_tensor("out_0_dram", (1, C, H, W), _mybir.dt.float32, kind="ExternalOutput").ap()
    build(nc, *args, out)
    r = _run(nc, [arrays], core_ids=[0])
    return r.results[0]["out_0_dram"]
```
